# Optimizing a Trainium2 kernel written in Bass

```python
import numpy as np
import jax
import jax.numpy as jnp

def _softmax(x, axis=-1):
    return jax.nn.softmax(x, axis=axis)

def _gelu(x):
    return jax.nn.gelu(x, approximate=True)

def _silu(x):
    return jax.nn.silu(x)

def _sigmoid(x):
    return jax.nn.sigmoid(x)

def _layernorm(x, axis=-1, eps=1e-05):
    m = jnp.mean(x, axis=axis, keepdims=True)
    v = jnp.var(x, axis=axis, keepdims=True)
    return (x - m) / jnp.sqrt(v + eps)

def _scatter_add(tgt, idx, src, axis=0):
    return tgt.at[idx].add(src)

def _segment_sum(src, seg, n):
    return jax.ops.segment_sum(src, seg, n)
kernel_name = 'mk_conv_attn_hybrid_d2_conv_nhwc512_r4_eaf68a'

def setup_inputs(seed: int=0):
    np.random.seed(seed)
    _w = jnp.asarray

    def _rec_inputs():
        import jax
        import jax.numpy as jnp
        _gk = jax.random.key(seed)
        x = -0.000125 + 0.9999 * jax.random.normal(jax.random.fold_in(_gk, 1), (16, 16, 16, 128), jnp.float32)
        return x
    x = _rec_inputs()

    def _L0_conv_setup():
        import jax, jax.numpy as jnp
        import numpy as np
        WS = 8
        HEADS = 16
        HEAD_DIM = 32
        DIM = 128
        NEG_INF = float('-inf')

        def _create_mask(ws, disp, upper_lower, left_right):
            size = ws * ws
            m = np.zeros((size, size), dtype=np.float32)
            d = disp
            if upper_lower:
                m[-d * ws:, :-d * ws] = NEG_INF
                m[:-d * ws, -d * ws:] = NEG_INF
            if left_right:
                m = m.reshape(ws, ws, ws, ws)
                m[:, -d:, :, :-d] = NEG_INF
                m[:, :-d, :, -d:] = NEG_INF
                m = m.reshape(size, size)
            return m

        def _relative_indices(ws):
            coords = np.array([[x, y] for x in range(ws) for y in range(ws)])
            dist = coords[None, :, :] - coords[:, None, :]
            dist += ws - 1
            return dist.astype(np.int64)
        _REL_IDX = _relative_indices(WS)
        _UL_MASK = jnp.asarray(_create_mask(WS, WS // 2, True, False))
        _LR_MASK = jnp.asarray(_create_mask(WS, WS // 2, False, True))
        key = jax.random.key(seed)
        ks = jax.random.split(key, 5)
        b, n = (16, 16)
        return {'x': jax.random.normal(ks[0], (b, n, n, DIM), dtype=jnp.float32), 'w_qkv': jax.random.normal(ks[1], (3 * HEADS * HEAD_DIM, DIM), dtype=jnp.float32) * 0.02, 'pos_embedding': jax.random.normal(ks[2], (2 * WS - 1, 2 * WS - 1), dtype=jnp.float32), 'w_out': jax.random.normal(ks[3], (DIM, HEADS * HEAD_DIM), dtype=jnp.float32) * 0.02, 'b_out': jax.random.normal(ks[4], (DIM,), dtype=jnp.float32) * 0.02}
    _L0_conv_all = _L0_conv_setup()
    _L0_conv_in = {k: v for k, v in _L0_conv_all.items() if k in ('w_qkv', 'pos_embedding', 'w_out', 'b_out')}
    del _L0_conv_all

    def _L1_attn_setup():
        import jax, jax.numpy as jnp
        import numpy as np
        B, N, C, H = (2, 1024, 128, 8)
        DH = C // H
        key = jax.random.key(seed)
        k1, k2, k3 = jax.random.split(key, 3)
        s = 0.02
        return {'x': jax.random.normal(k1, (B, N, C), dtype=jnp.float32), 'w_qkv': jax.random.normal(k2, (C, 3 * C), dtype=jnp.float32) * s, 'b_qkv': jnp.zeros((3 * C,), dtype=jnp.float32), 'w_out': jax.random.normal(k3, (C, C), dtype=jnp.float32) * s, 'b_out': jnp.zeros((C,), dtype=jnp.float32)}
    _L1_attn_all = _L1_attn_setup()
    _L1_attn_in = {k: v for k, v in _L1_attn_all.items() if k in ('w_qkv', 'b_qkv', 'w_out', 'b_out')}
    del _L1_attn_all

    def _L1_ffn_setup():
        import jax, jax.numpy as jnp
        import numpy as np
        TOP_K = 2
        key = jax.random.key(seed)
        ks = jax.random.split(key, 4)
        b, t, d, e, h = (2, 512, 128, 8, 256)
        scale = 0.02
        return {'x': jax.random.normal(ks[0], (b, t, d), dtype=jnp.float32), 'router_w': jax.random.normal(ks[1], (e, d), dtype=jnp.float32) * scale, 'router_b': jnp.zeros((e,), dtype=jnp.float32), 'fc1_w': jax.random.normal(ks[2], (e, 2 * h, d), dtype=jnp.float32) * scale, 'fc1_b': jnp.zeros((e, 2 * h), dtype=jnp.float32), 'fc2_w': jax.random.normal(ks[3], (e, d, h), dtype=jnp.float32) * scale, 'fc2_b': jnp.zeros((e, d), dtype=jnp.float32)}
    _L1_ffn_all = _L1_ffn_setup()
    _L1_ffn_in = {k: v for k, v in _L1_ffn_all.items() if k in ('router_w', 'router_b', 'fc1_w', 'fc1_b', 'fc2_w', 'fc2_b')}
    del _L1_ffn_all
    return {'x': x, 'L0_conv_w_qkv': _L0_conv_in['w_qkv'], 'L0_conv_pos_embedding': _L0_conv_in['pos_embedding'], 'L0_conv_w_out': _L0_conv_in['w_out'], 'L0_conv_b_out': _L0_conv_in['b_out'], 'L1_attn_w_qkv': _L1_attn_in['w_qkv'], 'L1_attn_b_qkv': _L1_attn_in['b_qkv'], 'L1_attn_w_out': _L1_attn_in['w_out'], 'L1_attn_b_out': _L1_attn_in['b_out'], 'L1_ffn_router_w': _L1_ffn_in['router_w'], 'L1_ffn_router_b': _L1_ffn_in['router_b'], 'L1_ffn_fc1_w': _L1_ffn_in['fc1_w'], 'L1_ffn_fc1_b': _L1_ffn_in['fc1_b'], 'L1_ffn_fc2_w': _L1_ffn_in['fc2_w'], 'L1_ffn_fc2_b': _L1_ffn_in['fc2_b']}

def reference(x, L0_conv_w_qkv, L0_conv_pos_embedding, L0_conv_w_out, L0_conv_b_out, L1_attn_w_qkv, L1_attn_b_qkv, L1_attn_w_out, L1_attn_b_out, L1_ffn_router_w, L1_ffn_router_b, L1_ffn_fc1_w, L1_ffn_fc1_b, L1_ffn_fc2_w, L1_ffn_fc2_b):
    import jax
    import jax.numpy as jnp

    def _L0_conv_ref(x, w_qkv, pos_embedding, w_out, b_out):
        import jax, jax.numpy as jnp
        import numpy as np
        WS = 8
        HEADS = 16
        HEAD_DIM = 32
        DIM = 128
        NEG_INF = float('-inf')

        def _create_mask(ws, disp, upper_lower, left_right):
            size = ws * ws
            m = np.zeros((size, size), dtype=np.float32)
            d = disp
            if upper_lower:
                m[-d * ws:, :-d * ws] = NEG_INF
                m[:-d * ws, -d * ws:] = NEG_INF
            if left_right:
                m = m.reshape(ws, ws, ws, ws)
                m[:, -d:, :, :-d] = NEG_INF
                m[:, :-d, :, -d:] = NEG_INF
                m = m.reshape(size, size)
            return m

        def _relative_indices(ws):
            coords = np.array([[x, y] for x in range(ws) for y in range(ws)])
            dist = coords[None, :, :] - coords[:, None, :]
            dist += ws - 1
            return dist.astype(np.int64)
        _REL_IDX = _relative_indices(WS)
        _UL_MASK = jnp.asarray(_create_mask(WS, WS // 2, True, False))
        _LR_MASK = jnp.asarray(_create_mask(WS, WS // 2, False, True))
        disp = WS // 2
        scale = HEAD_DIM ** (-0.5)
        b, n_h, n_w, _ = x.shape
        nw_h, nw_w = (n_h // WS, n_w // WS)
        x = jnp.roll(x, shift=(-disp, -disp), axis=(1, 2))
        qkv = x @ w_qkv.T
        qkv = qkv.reshape(b, nw_h, WS, nw_w, WS, 3, HEADS, HEAD_DIM)
        qkv = qkv.transpose(5, 0, 6, 1, 3, 2, 4, 7).reshape(3, b, HEADS, nw_h * nw_w, WS * WS, HEAD_DIM)
        q, k, v = (qkv[0], qkv[1], qkv[2])
        dots = jnp.einsum('bhwid,bhwjd->bhwij', q, k) * scale
        dots = dots + pos_embedding[_REL_IDX[:, :, 0], _REL_IDX[:, :, 1]]
        dots = dots.at[:, :, -nw_w:].add(_UL_MASK)
        dots = dots.at[:, :, nw_w - 1::nw_w].add(_LR_MASK)
        attn = jax.nn.softmax(dots, axis=-1)
        out = jnp.einsum('bhwij,bhwjd->bhwid', attn, v)
        out = out.reshape(b, HEADS, nw_h, nw_w, WS, WS, HEAD_DIM)
        out = out.transpose(0, 2, 4, 3, 5, 1, 6).reshape(b, n_h, n_w, HEADS * HEAD_DIM)
        out = out @ w_out.T + b_out
        out = jnp.roll(out, shift=(disp, disp), axis=(1, 2))
        return out

    def _L1_attn_ref(x, w_qkv, b_qkv, w_out, b_out):
        import jax, jax.numpy as jnp
        import numpy as np
        B, N, C, H = (2, 1024, 128, 8)
        DH = C // H
        b, n, c = x.shape
        scale = c ** (-0.5)
        qkv = x @ w_qkv + b_qkv
        qkv = qkv.reshape(b, n, 3, H, DH)
        q, k, v = [jnp.transpose(qkv[:, :, i], (0, 2, 1, 3)) for i in range(3)]
        attn = jnp.einsum('bhqd,bhkd->bhqk', q, k) * scale
        attn = jax.nn.softmax(attn, axis=-1)
        out = jnp.einsum('bhqk,bhkd->bhqd', attn, v)
        out = jnp.transpose(out, (0, 2, 1, 3)).reshape(b, n, c)
        return out @ w_out + b_out

    def _L1_ffn_ref(x, router_w, router_b, fc1_w, fc1_b, fc2_w, fc2_b):
        import jax, jax.numpy as jnp
        import numpy as np
        TOP_K = 2
        n_experts = router_w.shape[0]
        temp = 1.0
        logits = (jnp.einsum('btd,ed->bte', x, router_w) + router_b) / temp
        topk_val, topk_idx = jax.lax.top_k(logits, TOP_K)
        weights = jax.nn.softmax(topk_val, axis=-1)
        onehot = jax.nn.one_hot(topk_idx, n_experts, dtype=x.dtype)
        cw = jnp.einsum('btk,btke->bte', weights, onehot)
        h = jnp.einsum('btd,efd->btef', x, fc1_w) + fc1_b
        h1, h2 = jnp.split(h, 2, axis=-1)
        a = jax.nn.silu(h1) * h2
        y = jnp.einsum('bteh,edh->bted', a, fc2_w) + fc2_b
        out = jnp.einsum('bted,bte->btd', y, cw)
        return out

    def _gn(v, G=32, eps=1e-05):
        B_, H_, W_, C_ = v.shape
        g = v.reshape(B_, H_, W_, G, C_ // G)
        m = jnp.mean(g, axis=(1, 2, 4), keepdims=True)
        s = jnp.var(g, axis=(1, 2, 4), keepdims=True)
        return ((g - m) / jnp.sqrt(s + eps)).reshape(v.shape)

    def _ln_c(v, eps=1e-06):
        m = jnp.mean(v, axis=-1, keepdims=True)
        s = jnp.var(v, axis=-1, keepdims=True)
        return (v - m) / jnp.sqrt(s + eps)

    def _ln_t(v, eps=1e-05):
        m = jnp.mean(v, axis=-1, keepdims=True)
        s = jnp.var(v, axis=-1, keepdims=True)
        return (v - m) / jnp.sqrt(s + eps)

    def _to_tokens(v):
        B_, H_, W_, C_ = v.shape
        return v.reshape(B_, H_ * W_, C_)

    def _from_tokens(t, like):
        return t.reshape(like.shape)
    x = x + _L0_conv_ref(_gn(x), L0_conv_w_qkv, L0_conv_pos_embedding, L0_conv_w_out, L0_conv_b_out)
    t = _to_tokens(x)
    t = t + _L1_attn_ref(_ln_t(t), L1_attn_w_qkv, L1_attn_b_qkv, L1_attn_w_out, L1_attn_b_out)
    t = t + _L1_ffn_ref(_ln_t(t), L1_ffn_router_w, L1_ffn_router_b, L1_ffn_fc1_w, L1_ffn_fc1_b, L1_ffn_fc2_w, L1_ffn_fc2_b)
    x = _from_tokens(t, x)
    return x

_drawn_inputs = setup_inputs


def setup_inputs(seed=0):
    import zlib

    import numpy as np

    out = dict(_drawn_inputs(seed))
    spreads = {'L1_attn_b_qkv': (0.0, 0.308),
     'L1_attn_b_out': (0.0, 0.1),
     'L1_ffn_router_b': (0.0, 0.1),
     'L1_ffn_fc1_b': (0.0, 0.8),
     'L1_ffn_fc2_b': (0.0, 0.524)}
    factors = {'L1_attn_w_qkv': 8.0, 'L1_ffn_fc1_w': 8.0, 'L1_ffn_fc2_w': 8.0}
    for name, (base, spread) in spreads.items():
        noise = np.random.default_rng([zlib.crc32(name.encode()), seed]).standard_normal(out[name].shape)
        drawn = base * np.exp(spread * noise) if base else spread * noise
        out[name] = jnp.asarray(drawn.astype(out[name].dtype))
    for name, factor in factors.items():
        out[name] = (out[name] * factor).astype(out[name].dtype)
    return out
```

```python
import numpy as np
import concourse.bass as bass
from concourse import mybir
from contextlib import ExitStack

B, C = 16, 128
TOK = 256
NTOK = B * TOK
H0, D0 = 16, 32
NCH = H0 * D0 // 128
WIN = 64
NWIN = TOK // WIN
H1, D1 = 8, 16
PAD1 = 32
E, HID, TOPK = 8, 256, 2
NFC = E * HID // 128
GRP = 512
NGRP = NTOK // GRP
AU, BU = 4, 8
GU = 12
SCALE0 = D0 ** -0.5
SCALE1 = C ** -0.5
EPS = 1e-5
LOOP_FROM, LOOP_TO = 4, 14
C0_DMAS, C1_DMAS, F_DMAS = 7 * 16, 8 * 16, 7 * 16


class Image:

    def __init__(self, j, half, par):
        self.j, self.half, self.par = j, half, par

    def cols(self, width):
        return bass.ds(self.j * width, width)


def wait(eng, sem, value):
    if isinstance(value, int) and value <= 0:
        return
    eng.wait_ge(sem, value)


def chunk_use(n):
    return n + n // 2


def value_use(w):
    return 3 * w + 2


def steps_back(J, prev, n, back):
    k = n - back
    if k >= 0:
        return [] if J is None else [(J, k)]
    return [] if prev is None else [(prev, k + BU)]


def turned(J, prev, n):
    if n % 2:
        return []
    u = n // 2 - 1
    return [(x, u % AU) for x in ((J if u >= 0 else prev),) if x is not None]


def applied(J, prev, n):
    return turned(J, prev, n - 1) if n % 2 else []


def collected(J, prev, n):
    if n % 2:
        return []
    return applied(J, prev, n - 1) if n else ([] if prev is None else [(prev, 2)])


def values_made(G, A, n):
    if n % 2:
        return []
    return [(x, (n // 2 - 1) % NWIN) for x in ((G if n else A),) if x is not None]


def hybrid_kernel(nc, x_tok, x_ch, w0, wo0, bo0, pos, mask, ident_d, gmat_d, sel_d, iota_d,
                  w1, bq1, bk1, bv1, wo1, bo1, rw, rb, f1, f1b, f2, f2b, out):
    f32, f32r, u32 = mybir.dt.float32, mybir.dt.float32r, mybir.dt.uint32
    ALU, ACT, AX = mybir.AluOpType, mybir.ActivationFunctionType, mybir.AxisListType

    ctx = ExitStack()
    with ctx:
        def sb(name, shape, dt=f32):
            return ctx.enter_context(nc.sbuf_tensor(name, shape, dt))

        def sem(name):
            return ctx.enter_context(nc.semaphore(name))

        def sem2(name):
            return [sem(f"{name}{p}") for p in range(2)]

        ident = sb("ident", [128, 128])
        gmat = sb("gmat", [128, 128])
        posr = sb("posr", [128, 8, 8])
        masks = sb("masks", [128, 2, 8, 8])
        bias0 = sb("bias0", [128, 2, 8, 8])
        half = sb("half", [128, B])
        wv0 = sb("wv0", [C, H0 // 2, 2, D0])
        wo0s = sb("wo0s", [128, NCH, C])
        bo0s = sb("bo0s", [128, 2, C])
        wo1s = sb("wo1s", [128, 2, C])
        bo1s = sb("bo1s", [128, 2, C])
        bq1s = sb("bq1s", [C, 1])
        bq1x = sb("bq1x", [C, 1])
        bk1s = sb("bk1s", [C, 1])
        bv1s = sb("bv1s", [128, 2])
        rws = sb("rws", [C, E])
        rbs = sb("rbs", [128, 2, E])
        xch = sb("xch", [C, NTOK])
        res2 = xch
        tnx = sb("tnx", [C, NTOK])
        logit = sb("logit", [128, 2 * B, E])
        f1s = sb("f1s", [C, 2 * NFC * 128])
        f2s = sb("f2s", [128, NFC, C])
        f1bs = sb("f1bs", [128, 2 * NFC])
        f2bs = sb("f2bs", [128, C])
        iota = sb("iota", [128, E])

        attention = ctx.enter_context(ExitStack())

        def sa_(name, shape, dt=f32):
            return attention.enter_context(nc.sbuf_tensor(name, shape, dt))

        w0h = sa_("w0h", [C, 2 * NCH * 128], f32r)
        w0l = sa_("w0l", [C, 2 * NCH * 128], f32r)
        w1s = sa_("w1s", [C, 2 * C + H1 * PAD1])
        w1h = sa_("w1h", [C, 2 * C + H1 * PAD1], f32r)
        w1l = sa_("w1l", [C, 2 * C + H1 * PAD1], f32r)
        gst = sa_("gst", [C, B, 6])
        gmv = sa_("gmv", [C, B, 2])
        gsum = sa_("gsum", [C, B, 2])
        gsq = sa_("gsq", [C, B])
        grs = sa_("grs", [C, B])
        xns = sa_("xns", [C, 2, TOK])
        xnh = sa_("xnh", [C, 2, TOK], f32r)
        xnl = sa_("xnl", [C, 2, TOK], f32r)
        kst0 = sa_("kst0", [128, NCH, TOK])
        kbd0 = [sa_(f"kbd0_{p}", [128, NCH, 4, TOK]) for p in range(2)]
        q0 = sa_("q0", [128, 2, NCH, TOK])
        v0 = [sa_(f"v0_{p}", [128, NWIN, H0 // 2, 2, D0]) for p in range(2)]
        o0 = sa_("o0", [128, NCH, TOK])
        w0s = o0[:, :, :].rearrange("p a b -> p (a b)")
        xt = sa_("xt", [128, 2, 2, C])
        t1 = sa_("t1", [128, 2, C])
        t1b = sa_("t1b", [128, 2, 2, C])
        t2 = sa_("t2", [128, 2, C])
        st1, st2 = sa_("st1", [128, 2, 6]), sa_("st2", [128, 2, 6])
        mv1, mv2 = sa_("mv1", [128, 2, 2]), sa_("mv2", [128, 2, 2])
        tn1, tn2 = sa_("tn1", [128, 2, C]), sa_("tn2", [128, 2, C])
        rs1, rs2 = sa_("rs1", [128, 2]), sa_("rs2", [128, 2])
        t1h = sa_("t1h", [C, TOK], f32r)
        t1l = sa_("t1l", [C, TOK], f32r)
        t2f = sa_("t2f", [C, TOK])
        q1 = sa_("q1", [128, 2, TOK])
        kst1 = sa_("kst1", [128, TOK])
        kbd1 = [sa_(f"kbd1_{p}", [128, H1, TOK]) for p in range(2)]
        v1 = sa_("v1", [128, 2, 2, H1 * PAD1])
        o1 = sa_("o1", [128, 2, TOK])
        pa = sa_("pa", [128, 2, 8, WIN])
        mxa = sa_("mxa", [128, 2, 8])
        sma = sa_("sma", [128, 2, 8])
        rca = sa_("rca", [128, 2, 8])
        pta = sa_("pta", [128, 2, 512])
        pb = sa_("pb", [128, 2, 2, TOK])
        mxb = sa_("mxb", [128, 2, 2])
        smb = sa_("smb", [128, 2, 2])
        rcb = sa_("rcb", [128, 2, 2])
        ptb = sa_("ptb", [128, 2, 2, TOK])

        attention.close()
        sels = sb("sels", [128, E, 128])
        sel = sb("sel", [128, E, 128], f32r)
        f1h = sb("f1h", [C, 2 * NFC * 128], f32r)
        f1l = sb("f1l", [C, 2 * NFC * 128], f32r)
        f2bst = sb("f2bst", [128, C], f32r)
        tgh = sb("tgh", [C, 2, GRP], f32r)
        tgl = sb("tgl", [C, 2, GRP], f32r)
        mx8 = sb("mx8", [128, 2 * B, 8])
        ix8 = sb("ix8", [128, 2 * B, 8], u32)
        ixf = sb("ixf", [128, 2 * B, 8])
        rdel = sb("rdel", [128, 2 * B, 1])
        rexp = sb("rexp", [128, 2 * B, 1])
        rden = sb("rden", [128, 2 * B, 1])
        wt1 = sb("wt1", [128, 2 * B, 1])
        wt2 = sb("wt2", [128, 2 * B, 1])
        cwa = sb("cwa", [128, 2 * B, E])
        cwb = sb("cwb", [128, 2 * B, E])
        cws = sb("cws", [128, 2 * B, E])
        cwt = sb("cwt", [128, NTOK], f32r)
        sil = sb("sil", [128, 2, GRP])
        gat = sb("gat", [128, 4, GRP])
        act = sb("act", [128, 4, GRP])
        yt = sb("yt", [128, GRP])
        yo = sb("yo", [128, 2, GRP])

        def bank(name):
            return ctx.enter_context(nc.psum_tensor(name, [128, 512], f32))

        pG, pM, pSA, pSB, pTA, pTB, pOA, pOB = (bank(n) for n in ("pG", "pM", "pSA", "pSB", "pTA", "pTB", "pOA", "pOB"))

        d_x = [sem(f"d_x{n}") for n in range(4)]
        d_c0 = sem("d_c0")
        d_c1 = sem("d_c1")
        d_pos = sem("d_pos")
        d_f = sem("d_f")
        d_sel = sem("d_sel")
        z_half, z_kv = sem("z_half"), sem("z_kv")
        c_w0h, c_w0l, c_w1h, c_w1l, c_bq, c_bias = (
            sem(n) for n in ("c_w0h", "c_w0l", "c_w1h", "c_w1l", "c_bq", "c_bias"))
        gn_st, gn_ag, gn_sq, gn_e2, gn_mm, gn_cp, gn_q, gn_v, gn_eps, gn_pow = (
            sem(n) for n in ("gn_st", "gn_ag", "gn_sq", "gn_e2", "gn_mm", "gn_cp", "gn_q", "gn_v", "gn_eps", "gn_pow"))
        x_s, x_h, x_l = sem("x_s"), sem("x_h"), sem("x_l")
        g_mm, g_ev = sem("g_mm"), sem("g_ev")
        k0_dma = [sem("k0_dma0"), sem("k0_dma1")]
        sa_mm, sa_add, sa_max, sa_sub, sa_exp, sa_sum, sa_rcp, sa_nrm = (
            sem(n) for n in ("sa_mm", "sa_add", "sa_max", "sa_sub", "sa_exp", "sa_sum", "sa_rcp", "sa_nrm"))
        ta_mm, ta_ev, oa_mm, oa_ev = (sem(n) for n in ("ta_mm", "ta_ev", "oa_mm", "oa_ev"))
        sb_mm, sb_max, sb_exp, sb_rcp, sb_nrm = (sem(n) for n in ("sb_mm", "sb_max", "sb_exp", "sb_rcp", "sb_nrm"))
        tb_mm, tb_ev, ob_mm, ob_ev = (sem(n) for n in ("tb_mm", "tb_ev", "ob_mm", "ob_ev"))
        xt_dma = [sem("xt_dma0"), sem("xt_dma1")]
        k1_dma = [sem("k1_dma0"), sem("k1_dma1")]
        m_xb, m_o, m_t, m_st, m_ag, m_eps, m_pow, m_tn, m_T, m_hi, m_lo, m_qk, m_qev, m_kev, m_v, m_vev, m_tb = (
            sem(n) for n in ("m_xb", "m_o", "m_t", "m_st", "m_ag", "m_eps", "m_pow", "m_tn", "m_T", "m_hi", "m_lo",
                             "m_qk", "m_qev", "m_kev", "m_v", "m_vev", "m_tb"))
        r_o, r_t, r_st, r_ag, r_eps, r_pow, r_tn, r_T, r_f, r_x, r_lg, r_lgev = (
            sem(n) for n in ("r_o", "r_t", "r_st", "r_ag", "r_eps", "r_pow", "r_tn", "r_T", "r_f", "r_x",
                             "r_lg", "r_lgev"))
        c_f1h, c_f1l, c_tgh, c_tgl, c_sel, c_b2z, c_b2h, c_b2l, c_cwz = (
            sem(n) for n in ("c_f1h", "c_f1l", "c_tgh", "c_tgl", "c_sel", "c_b2z", "c_b2h", "c_b2l", "c_cwz"))
        q_max, q_ix, q_ixf, q_d, q_exp, q_den, q_w1, q_w2, q_a, q_b, q_am, q_bm, q_cw = (
            sem(n) for n in ("q_max", "q_ix", "q_ixf", "q_d", "q_exp", "q_den", "q_w1", "q_w2", "q_a", "q_b",
                             "q_am", "q_bm", "q_cw"))
        ct_mm, ct_hi, ct_lo = sem("ct_mm"), sem("ct_hi"), sem("ct_lo")
        e_cw, e_h1, e_h2, e_sil, e_gat, e_act, e_y = (
            sem(n) for n in ("e_cw", "e_h1", "e_h2", "e_sil", "e_gat", "e_act", "e_y"))
        y_ev, y_T, y_add = sem("y_ev"), sem("y_T"), sem("y_add")
        y_dma = [sem("y_dma0"), sem("y_dma1")]

        out_v = out.rearrange("(g s p) c -> g p s c", s=GRP // 128, p=128)
        xt_v = x_tok.rearrange("(b s p) c -> p b s c", s=2, p=128)
        pos_t = pos.tensor
        w0v = w0[:, 2 * H0 * D0:3 * H0 * D0]

        LAGS = (2, 1, 0, -1, -2, -3, -4)

        def peeled(i):
            return [Image(i + lag, (i + lag) // 2, (i + lag) % 2) if 0 <= i + lag < B else None for lag in LAGS]

        def looped(it, p):
            first = LOOP_FROM + p
            return [Image(it * 2 + (first + lag), it + (first + lag) // 2, (first + lag) % 2) for lag in LAGS]

        def pipeline(eng, iteration):
            for i in range(-2, LOOP_FROM):
                iteration(*peeled(i))
            with eng.Fori(0, (LOOP_TO - LOOP_FROM) // 2) as it:
                for p in range(2):
                    iteration(*looped(it, p))
            for i in range(LOOP_TO, B + 4):
                iteration(*peeled(i))

        def ffn(eng, group):
            for g in range(3):
                group(g, g // 2, g % 2, True)
            with eng.Fori(0, (NGRP - 4) // 2) as it:
                for p in range(2):
                    group(it * 2 + (3 + p), it + (3 + p) // 2, (3 + p) % 2, True)
            group(NGRP - 1, (NGRP - 1) // 2, (NGRP - 1) % 2, True)
            group(NGRP, NGRP // 2, NGRP % 2, False)

        def pieces(c):
            e, hc = c // 2, c % 2
            return (e * 4 + hc, e * 4 + 2 + hc)

        block = ctx.enter_context(nc.Block())

        @block.sync
        def _(sp):
            sp.dma_start(xch[:, 0:NTOK // 4], x_ch[:, 0:NTOK // 4]).then_inc(d_x[0], 16)
            sp.dma_start(xch[:, NTOK // 4:NTOK // 2], x_ch[:, NTOK // 4:NTOK // 2]).then_inc(d_x[1], 16)
            sp.dma_start(xch[:, NTOK // 2:3 * NTOK // 4], x_ch[:, NTOK // 2:3 * NTOK // 4]).then_inc(d_x[2], 16)
            sp.dma_start(xch[:, 3 * NTOK // 4:NTOK], x_ch[:, 3 * NTOK // 4:NTOK]).then_inc(d_x[3], 16)
            for r in range(2):
                for qx in range(8):
                    p = r * WIN + qx * 8
                    sp.dma_start(posr[p:p + 8, :, :],
                                 bass.AP(tensor=pos_t, offset=(7 - qx) * 15, ap=[[1, 8], [15, 8], [1, 8]]))\
                      .then_inc(d_pos, 16)
            sp.dma_start(wo1s[:, :, :], wo1.rearrange("(g p) c -> p g c", p=128)).then_inc(d_c1, 16)
            sp.dma_start(bo1s[:, :, :], bo1.partition_broadcast(128)).then_inc(d_c1, 16)
            sp.dma_start(w1s[:, :], w1).then_inc(d_c1, 16)
            sp.dma_start(bq1s[:, :], bq1).then_inc(d_c1, 16)
            sp.dma_start(bk1s[:, :], bk1).then_inc(d_c1, 16)
            sp.dma_start(bv1s[:, :], bv1).then_inc(d_c1, 16)
            sp.dma_start(rws[:, :], rw).then_inc(d_c1, 16)
            sp.dma_start(rbs[:, :, :], rb.partition_broadcast(128)).then_inc(d_c1, 16)
            sp.dma_start(f1s[:, :], f1).then_inc(d_f, 16)
            sp.dma_start(f2s[:, :, :], f2.rearrange("p (j d) -> p j d", d=C)).then_inc(d_f, 16)
            sp.dma_start(f1bs[:, :], f1b).then_inc(d_f, 16)
            sp.dma_start(f2bs[0:E, :], f2b).then_inc(d_f, 16)
            sp.dma_start(f2bs[32:32 + E, :], f2b).then_inc(d_f, 16)
            sp.dma_start(f2bs[64:64 + E, :], f2b).then_inc(d_f, 16)
            sp.dma_start(iota[:, :], iota_d).then_inc(d_f, 16)

            def iteration(X, G, A, M, Bm, R, L):
                if A is not None:
                    wait(sp, m_t, A.j - 1)
                if G is not None:
                    wait(sp, g_ev, G.j * GU + (chunk_use(NCH - 1) + 1))
                    if isinstance(G.j, int) and G.j == 0:
                        sp.wait_ge(z_kv, 1)
                    for h in range(4):
                        sp.dma_start(kbd0[G.par][32 * h:32 * h + 32, :, h, :],
                                     kst0[32 * h:32 * h + 32, :, :]).then_inc(k0_dma[G.par], 16)
                if A is not None:
                    sp.dma_start(xt[:, A.par, :, :],
                                 xt_v[:, bass.ds(A.j, 1), :, :].rearrange("p b s c -> p (b s) c"))\
                      .then_inc(xt_dma[A.par], 16)
                if M is not None:
                    wait(sp, m_kev, M.j + 1)
                    for h in range(H1):
                        sp.dma_start(kbd1[M.par][D1 * h:D1 * h + D1, h, :],
                                     kst1[D1 * h:D1 * h + D1, :]).then_inc(k1_dma[M.par], 16)

            pipeline(sp, iteration)

            sp.wait_ge(r_lgev, B)
            sp.dma_start(sels[:, :, :], sel_d.rearrange("p (e c) -> p e c", e=E)).then_inc(d_sel, 16)

            for g in range(NGRP):
                sp.wait_ge(y_add, g + 1)
                sp.dma_start(out_v[g, :, :, :], yo[:, g % 2, :].rearrange("p (s c) -> p s c", c=C))\
                  .then_inc(y_dma[g % 2], 16)
            for p in range(2):
                sp.wait_ge(y_dma[p], 16 * NGRP // 2)

        @block.gpsimd
        def _(pool):
            pool.memset(half[:, :], -0.5).then_inc(z_half, 1)
            pool.memset(kbd0[0][:, :, :, :], 0.0)
            pool.memset(v0[0][:, :, :, :, :], 0.0)
            pool.memset(kbd0[1][:, :, :, :], 0.0)
            pool.memset(v0[1][:, :, :, :, :], 0.0)
            pool.memset(kbd1[0][:, :, :], 0.0)
            pool.memset(kbd1[1][:, :, :], 0.0).then_inc(z_kv, 1)
            pool.wait_ge(z_half, 1)
            pool.wait_ge(gn_eps, 1)
            pool.tensor_tensor(grs[:, :], gsq[:, :], half[:, :], ALU.pow).then_inc(gn_pow, 1)

            def iteration(X, G, A, M, Bm, R, L):
                for n in range(8):
                    if n == 0 and M is not None:
                        if isinstance(M.j, int) and M.j == 0:
                            pool.wait_ge(d_c0, C0_DMAS)
                        pool.wait_ge(xt_dma[M.par], M.half * 16 + 16)
                        pool.tensor_tensor(xt[:, M.par, :, :], xt[:, M.par, :, :], bo0s[:, :, :],
                                           ALU.add).then_inc(m_xb, 1)
                    if n == 4 and M is not None:
                        pool.wait_ge(m_eps, M.j + 1)
                        pool.tensor_tensor(rs1[:, :], rs1[:, :], half[:, 0:2], ALU.pow).then_inc(m_pow, 1)
                    if n == 5 and M is not None:
                        pool.wait_ge(m_t, M.j + 1)
                        wait(pool, r_t, M.j - 1)
                        pool.tensor_tensor(t1b[:, M.par, :, :], t1[:, :, :], bo1s[:, :, :], ALU.add).then_inc(m_tb, 1)
                    if n == 6 and R is not None:
                        pool.wait_ge(r_eps, R.j + 1)
                        pool.tensor_tensor(rs2[:, :], rs2[:, :], half[:, 0:2], ALU.pow).then_inc(r_pow, 1)
                    if Bm is not None:
                        b = n % 2
                        pool.wait_ge(sb_rcp, Bm.j * BU + (n + 1))
                        pool.tensor_tensor(pb[:, b, :, :], pb[:, b, :, :],
                                           rcb[:, b, :].unsqueeze(2).to_broadcast([128, 2, TOK]),
                                           ALU.mult).then_inc(sb_nrm, 1)
                    if A is not None and n % 2 == 1:
                        u = n // 2
                        b = u % 2
                        pool.wait_ge(sa_rcp, A.j * AU + (u + 1))
                        pool.tensor_tensor(pa[:, b, :, :], pa[:, b, :, :],
                                           rca[:, b, :].unsqueeze(2).to_broadcast([128, 8, WIN]),
                                           ALU.mult).then_inc(sa_nrm, 1)

            pipeline(pool, iteration)

        @block.scalar
        def _(a):
            a.dma_start(gmat[:, :], gmat_d).then_inc(d_c0, 16)
            a.dma_start(w0s, w0[:, 0:2 * H0 * D0]).then_inc(d_c0, 16)
            a.dma_start(ident[:, :], ident_d).then_inc(d_c0, 16)
            a.dma_start(wv0[:, :, :, :], w0v.rearrange("p (a b d) -> p a b d", b=2, d=D0)).then_inc(d_c0, 16)
            a.dma_start(masks[:, :, :, :], mask.rearrange("p (r x y) -> p r x y", r=2, x=8)).then_inc(d_c0, 16)
            a.dma_start(wo0s[:, :, :], wo0.rearrange("(j p) c -> p j c", p=128)).then_inc(d_c0, 16)
            a.dma_start(bo0s[:, :, :], bo0.partition_broadcast(128)).then_inc(d_c0, 16)
            a.wait_ge(d_c0, C0_DMAS)
            a.activation(w0h[:, :], w0s, ACT.Copy).then_inc(c_w0h, 1)
            a.wait_ge(d_c1, C1_DMAS)
            a.activation(w1h[:, :], w1s[:, :], ACT.Copy).then_inc(c_w1h, 1)
            a.activation(bq1x[:, :], bq1s[:, :], ACT.Copy, scale=SCALE1).then_inc(c_bq, 1)

            def iteration(X, G, A, M, Bm, R, L):
                def keys_or_queries(n):
                    a.wait_ge(g_mm, G.j * GU + (chunk_use(n) + 1))
                    if n < NCH:
                        if n == 0:
                            wait(a, k0_dma[(G.par + 1) % 2],
                                 (G.half + G.par) * 64 if not isinstance(G.j, int) or G.j > 0 else 0)
                        a.activation(kst0[:, n, :], pG[:, 0:TOK], ACT.Copy).then_inc(g_ev, 1)
                    else:
                        wait(a, sa_mm, (G.j - 1) * AU)
                        a.activation(q0[:, G.par, n - NCH, :], pG[:, 0:TOK], ACT.Copy,
                                     scale=SCALE0).then_inc(g_ev, 1)

                for n in range(8):
                    if G is not None and n % 2 == 1:
                        keys_or_queries(n)
                    for J, w in values_made(G, A, n):
                        a.wait_ge(g_mm, J.j * GU + (value_use(w) + 1))
                        if isinstance(J.j, int) and J.j < 2:
                            a.wait_ge(z_kv, 1)
                        wait(a, oa_mm, (J.j - 2) * AU + 2 * (w // 2) + 2)
                        for half_ in range(2):
                            rows = slice(WIN * half_, WIN * half_ + WIN)
                            last = a.activation(v0[J.par][rows, w, :, half_, :],
                                                pG[rows, 0:TOK].rearrange("p (a d) -> p a d", d=D0), ACT.Copy)
                        last.then_inc(g_ev, 1)
                    for J, u in collected(A, M, n):
                        wait(a, oa_mm, J.j * AU + (u + 1))
                        if u == 0:
                            wait(a, m_o, J.j)
                        pr, hf = u // 2, u % 2
                        for w in range(2):
                            o = pOA[:, w * TOK:(w + 1) * TOK].rearrange("p (c q) -> p c q", c=2)
                            last = a.activation(o0[:, 2 * hf:2 * hf + 2, 128 * pr + WIN * w:128 * pr + WIN * w + WIN],
                                                o[:, :, WIN * w:WIN * w + WIN], ACT.Copy)
                        last.then_inc(oa_ev, 1)
                    if M is not None and n == 5:
                        a.wait_ge(m_T, M.j + 1)
                        wait(a, m_v, M.j)
                        a.activation(t1h[:, :], pM[:, 0:TOK], ACT.Copy).then_inc(m_hi, 1)
                    if M is not None and n == 6:
                        a.wait_ge(m_qk, M.j + 1)
                        wait(a, k1_dma[(M.par + 1) % 2],
                             (M.half + M.par) * 128 if not isinstance(M.j, int) or M.j > 0 else 0)
                        a.activation(kst1[:, :], pM[:, TOK:2 * TOK], ACT.Identity, bias=bk1s[:, :]).then_inc(m_kev, 1)
                        if isinstance(M.j, int) and M.j == 0:
                            a.wait_ge(c_bq, 1)
                        wait(a, sb_mm, (M.j - 1) * BU)
                        a.activation(q1[:, M.par, :], pM[:, 0:TOK], ACT.Identity, bias=bq1x[:, :],
                                     scale=SCALE1).then_inc(m_qev, 1)
                    if A is not None and n % 2 == 1:
                        u = n // 2
                        a.wait_ge(sa_sub, A.j * AU + (u + 1))
                        a.activation(pa[:, u % 2, :, :], pa[:, u % 2, :, :], ACT.Exp).then_inc(sa_exp, 1)
                    if R is not None and n == 7:
                        a.wait_ge(r_T, R.j + 1)
                        wait(a, r_lg, R.j)
                        a.activation(t2f[:, :], pOA[:, 0:TOK], ACT.Copy).then_inc(r_f, 1)
                        a.activation(tnx[:, R.cols(TOK)], pOA[:, 0:TOK], ACT.Copy).then_inc(r_x, 1)
                    if M is not None and n == 7:
                        a.wait_ge(m_v, M.j + 1)
                        wait(a, ob_mm, (M.j - 1) * BU)
                        a.activation(v1[:, M.par, :, :], pM[:, :].rearrange("p (a b) -> p a b", a=2),
                                     ACT.Copy).then_inc(m_vev, 1)
                    if Bm is not None:
                        b = n % 2
                        wait(a, sb_max, Bm.j * BU + (n + 1))
                        wait(a, sb_rcp, Bm.j * BU + (n - 1))
                        wait(a, tb_mm, Bm.j * BU + (n - 1))
                        for qc in range(2):
                            last = a.activation(pb[:, b, qc, :], pSB[:, qc * TOK:(qc + 1) * TOK], ACT.Exp,
                                                bias=mxb[:, b, qc:qc + 1], accum_out=smb[:, b, qc:qc + 1])
                        last.then_inc(sb_exp, 1)
                    for J, k in steps_back(Bm, R, n, 1):
                        wait(a, tb_mm, J.j * BU + (k + 1))
                        wait(a, ob_mm, J.j * BU + (k - 1))
                        a.activation(ptb[:, k % 2, :, :], pTB[:, :].rearrange("p (a b) -> p a b", a=2),
                                     ACT.Copy).then_inc(tb_ev, 1)
                    if G is not None and n % 2 == 0:
                        keys_or_queries(n)
                    for J, u in turned(A, M, n):
                        wait(a, ta_mm, J.j * AU + (u + 1))
                        wait(a, oa_mm, J.j * AU + (u - 1))
                        a.activation(pta[:, u % 2, :], pTA[:, :], ACT.Copy).then_inc(ta_ev, 1)

            pipeline(a, iteration)

            a.wait_ge(r_lgev, B)
            a.wait_ge(d_f, F_DMAS)
            for q in range(4):
                w = 2 * NFC * 128 // 4
                a.activation(f1h[:, q * w:(q + 1) * w], f1s[:, q * w:(q + 1) * w], ACT.Copy).then_inc(c_f1h, 1)
                if q == 0:
                    a.activation(tgh[:, 0, :], tnx[:, 0:GRP], ACT.Copy).then_inc(c_tgh, 1)
            a.wait_ge(c_b2z, 1)
            for r in range(3):
                last = a.activation(f2bst[32 * r:32 * r + E, :], f2bs[32 * r:32 * r + E, :], ACT.Copy)
            last.then_inc(c_b2h, 1)
            a.wait_ge(q_d, 1)
            a.activation(rexp[:, :, :], rdel[:, :, :], ACT.Exp).then_inc(q_exp, 1)
            a.wait_ge(d_sel, 16)
            a.activation(sel[:, :, :], sels[:, :, :], ACT.Copy).then_inc(c_sel, 1)
            a.wait_ge(c_cwz, 1)
            for g in range(NGRP):
                a.wait_ge(ct_mm, g + 1)
                p = (pG, pM)[g % 2]
                a.activation(cwt[0:E, g * GRP:(g + 1) * GRP], p[0:E, :], ACT.Copy)
                a.activation(cwt[64:64 + E, g * GRP:(g + 1) * GRP], p[0:E, :], ACT.Copy).then_inc(ct_hi, 1)

            def group(g, gh, par, main):
                for c in range(16 if main else 5):
                    if main:
                        a.wait_ge(e_h1, g * 16 + (c + 1))
                        wait(a, e_gat, g * 16 + (c - 1))
                        i1, _ = pieces(c)
                        a.activation(sil[:, c % 2, :], (pSA, pSB)[c % 2][:, :], ACT.Silu,
                                     bias=f1bs[:, i1:i1 + 1]).then_inc(e_sil, 1)
                    if c == 2 and not (isinstance(g, int) and g == 0):
                        a.wait_ge(e_y, g * 16)
                        wait(a, y_T, g - 1)
                        a.activation(yt[:, :], (pOA, pOB)[1 - par][:, :], ACT.Copy).then_inc(y_ev, 1)
                    if c == 8 and main and not (isinstance(g, int) and g == NGRP - 1):
                        wait(a, e_h2, g * 16)
                        a.activation(tgh[:, 1 - par, :], tnx[:, bass.ds(g * GRP + GRP, GRP)],
                                     ACT.Copy).then_inc(c_tgh, 1)

            ffn(a, group)

        @block.vector
        def _(v):
            for j in range(B):
                if j % 4 == 0:
                    v.wait_ge(d_x[j // 4], 16)
                last = v.bn_stats(gst[:, j, :], xch[:, j * TOK:(j + 1) * TOK])
            last.then_inc(gn_st, 1)
            v.wait_ge(gn_st, 1)
            for j in range(B):
                last = v.bn_aggr(gmv[:, j, :], gst[:, j, :])
            last.then_inc(gn_ag, 1)
            v.wait_ge(gn_ag, 1)
            v.tensor_tensor(gsq[:, :], gmv[:, :, 0], gmv[:, :, 0], ALU.mult).then_inc(gn_sq, 1)
            v.wait_ge(gn_sq, 1)
            v.tensor_tensor(gmv[:, :, 1], gmv[:, :, 1], gsq[:, :], ALU.add).then_inc(gn_e2, 1)
            v.wait_ge(d_c0, C0_DMAS)
            v.wait_ge(d_pos, 16 * 16)
            for pr in range(2):
                for ky in range(8):
                    last = v.tensor_tensor(bias0[:, pr, :, ky], posr[:, :, 7 - ky], masks[:, pr, :, ky], ALU.add)
            last.then_inc(c_bias, 1)
            v.wait_ge(gn_mm, 1)
            v.tensor_copy(gsum[:, :, :], pG[:, 0:2 * B].rearrange("p (b t) -> p b t", t=2)).then_inc(gn_cp, 1)
            v.wait_ge(gn_cp, 1)
            v.tensor_tensor(gsq[:, :], gsum[:, :, 0], gsum[:, :, 0], ALU.mult).then_inc(gn_q, 1)
            v.wait_ge(gn_q, 1)
            v.tensor_tensor(gsq[:, :], gsum[:, :, 1], gsq[:, :], ALU.subtract).then_inc(gn_v, 1)
            v.wait_ge(gn_v, 1)
            v.tensor_scalar(gsq[:, :], gsq[:, :], EPS, None, ALU.add).then_inc(gn_eps, 1)
            v.wait_ge(c_w0h, 1)
            v.tensor_tensor(w0l[:, :], w0s, w0h[:, :].bitcast(f32), ALU.subtract).then_inc(c_w0l, 1)
            v.wait_ge(c_w1h, 1)
            v.tensor_tensor(w1l[:, :], w1s[:, :], w1h[:, :].bitcast(f32), ALU.subtract).then_inc(c_w1l, 1)
            v.wait_ge(gn_pow, 1)

            def iteration(X, G, A, M, Bm, R, L):
                def reciprocal_b(n):
                    b = n % 2
                    v.wait_ge(sb_exp, Bm.j * BU + (n + 1))
                    wait(v, sb_nrm, Bm.j * BU + (n - 1))
                    v.reciprocal(rcb[:, b, :], smb[:, b, :]).then_inc(sb_rcp, 1)

                for n in range(8):
                    if L is not None and n == 0:
                        v.wait_ge(r_lg, L.j + 1)
                        v.tensor_tensor(logit[:, bass.ds(L.j * 2, 2), :],
                                        pM[:, 0:2 * E].rearrange("p (s e) -> p s e", s=2), rbs[:, :, :],
                                        ALU.add).then_inc(r_lgev, 1)
                    if R is not None and n == 2:
                        v.wait_ge(ob_mm, R.j * BU + BU)
                        wait(v, r_o, R.j)
                        for g in range(2):
                            last = v.tensor_scalar(o1[:, g, :], pOB[:, g * TOK:(g + 1) * TOK],
                                                   bv1s[:, g:g + 1], None, ALU.add)
                        last.then_inc(ob_ev, 1)
                    if R is not None and n == 5:
                        v.wait_ge(r_o, R.j + 1)
                        v.wait_ge(m_tb, R.j + 1)
                        v.tensor_tensor(t2[:, :, :], pOA[:, 0:TOK].rearrange("p (s c) -> p s c", s=2),
                                        t1b[:, R.par, :, :], ALU.add).then_inc(r_t, 1)
                    if Bm is not None:
                        b = n % 2
                        v.wait_ge(sb_mm, Bm.j * BU + (n + 1))
                        v.tensor_reduce(mxb[:, b, :], pSB[:, :].rearrange("p (a k) -> p a k", a=2), AX.X, ALU.max,
                                        negate=True).then_inc(sb_max, 1)
                    if A is not None and n % 2 == 0:
                        u = n // 2
                        b = u % 2
                        if isinstance(A.j, int) and A.j == 0 and u == 0:
                            v.wait_ge(c_bias, 1)
                        v.wait_ge(sa_mm, A.j * AU + (u + 1))
                        wait(v, ta_mm, A.j * AU + (u - 1))
                        v.tensor_tensor(pa[:, b, :, :], pSA[:, :].rearrange("p (h k) -> p h k", h=8),
                                        bias0[:, u // 2, :, :].rearrange("p x y -> p (x y)").unsqueeze(1)
                                        .to_broadcast([128, 8, WIN]), ALU.add).then_inc(sa_add, 1)
                    if M is not None and n == 4:
                        v.wait_ge(m_pow, M.j + 1)
                        wait(v, m_T, M.j)
                        for s in range(2):
                            last = v.tensor_scalar(tn1[:, s, :], t1[:, s, :],
                                                   mv1[:, s, 0:1], rs1[:, s:s + 1], ALU.subtract, ALU.mult)
                        last.then_inc(m_tn, 1)
                    if R is not None and n == 6:
                        wait(v, r_T, R.j)
                        v.wait_ge(r_pow, R.j + 1)
                        for s in range(2):
                            last = v.tensor_scalar(tn2[:, s, :], t2[:, s, :],
                                                   mv2[:, s, 0:1], rs2[:, s:s + 1], ALU.subtract, ALU.mult)
                        last.then_inc(r_tn, 1)
                    if A is not None and n % 2 == 0:
                        v.wait_ge(sa_add, A.j * AU + (u + 1))
                        v.tensor_reduce(mxa[:, b, :], pa[:, b, :, :], AX.X, ALU.max).then_inc(sa_max, 1)
                    if Bm is not None and n % 2 == 0:
                        reciprocal_b(n)
                    if A is not None and n % 2 == 0:
                        v.wait_ge(sa_max, A.j * AU + (u + 1))
                        v.tensor_tensor(pa[:, b, :, :], pa[:, b, :, :],
                                        mxa[:, b, :].unsqueeze(2).to_broadcast([128, 8, WIN]),
                                        ALU.subtract).then_inc(sa_sub, 1)
                    if M is not None and n == 5:
                        v.wait_ge(m_hi, M.j + 1)
                        v.tensor_tensor(t1l[:, :], pM[:, 0:TOK], t1h[:, :].bitcast(f32),
                                        ALU.subtract).then_inc(m_lo, 1)
                    if A is not None and n % 2 == 1:
                        u = n // 2
                        b = u % 2
                        v.wait_ge(sa_exp, A.j * AU + (u + 1))
                        v.tensor_reduce(sma[:, b, :], pa[:, b, :, :], AX.X, ALU.add).then_inc(sa_sum, 1)
                    if Bm is not None and n % 2 == 1:
                        reciprocal_b(n)
                    if M is not None and n == 3:
                        v.wait_ge(m_o, M.j + 1)
                        v.wait_ge(m_xb, M.j + 1)
                        wait(v, m_tb, M.j)
                        v.tensor_tensor(t1[:, :, :], pM[:, 0:TOK].rearrange("p (s c) -> p s c", s=2),
                                        xt[:, M.par, :, :], ALU.add).then_inc(m_t, 1)
                        v.wait_ge(m_t, M.j + 1)
                        for s in range(2):
                            last = v.bn_stats(st1[:, s, :], t1[:, s, :])
                        last.then_inc(m_st, 1)
                        v.wait_ge(m_st, M.j + 1)
                    if A is not None and n % 2 == 1:
                        v.wait_ge(sa_sum, A.j * AU + (u + 1))
                        wait(v, sa_nrm, A.j * AU + (u - 1))
                        v.reciprocal(rca[:, b, :], sma[:, b, :]).then_inc(sa_rcp, 1)
                    if X is not None and n == 1:
                        p = X.par
                        wait(v, g_mm, (X.j - 1) * GU)
                        v.tensor_scalar(xns[:, p, :], xch[:, X.cols(TOK)], gsum[:, X.cols(1), 0],
                                        grs[:, X.cols(1)], ALU.subtract, ALU.mult).then_inc(x_s, 1)
                        v.wait_ge(x_s, X.j + 1)
                        v.tensor_copy(xnh[:, p, :], xns[:, p, :]).then_inc(x_h, 1)
                        v.wait_ge(x_h, X.j + 1)
                        v.tensor_tensor(xnl[:, p, :], xns[:, p, :], xnh[:, p, :].bitcast(f32),
                                        ALU.subtract).then_inc(x_l, 1)
                    if M is not None and n == 3:
                        for s in range(2):
                            last = v.bn_aggr(mv1[:, s, :], st1[:, s, :])
                        last.then_inc(m_ag, 1)
                        v.wait_ge(m_ag, M.j + 1)
                        v.tensor_scalar(rs1[:, :], mv1[:, :, 1], EPS, None, ALU.add).then_inc(m_eps, 1)
                    if R is not None and n == 5:
                        v.wait_ge(r_t, R.j + 1)
                        for s in range(2):
                            last = v.bn_stats(st2[:, s, :], t2[:, s, :])
                        last.then_inc(r_st, 1)
                        v.wait_ge(r_st, R.j + 1)
                        v.tensor_scalar(res2[:, R.cols(TOK)], t2[:, :, :].rearrange("p s c -> p (s c)"),
                                        1.0, None, ALU.mult)
                        for s in range(2):
                            last = v.bn_aggr(mv2[:, s, :], st2[:, s, :])
                        last.then_inc(r_ag, 1)
                        v.wait_ge(r_ag, R.j + 1)
                        v.tensor_scalar(rs2[:, :], mv2[:, :, 1], EPS, None, ALU.add).then_inc(r_eps, 1)

            pipeline(v, iteration)

            v.wait_ge(r_lgev, B)
            v.memset(f2bst[:, :].bitcast(f32), 0.0).then_inc(c_b2z, 1)
            v.memset(cwt[:, :].bitcast(f32), 0.0).then_inc(c_cwz, 1)
            v.wait_ge(c_f1h, 1)
            w = 2 * NFC * 128 // 4
            v.tensor_tensor(f1l[:, 0:w], f1s[:, 0:w], f1h[:, 0:w].bitcast(f32), ALU.subtract).then_inc(c_f1l, 1)
            v.wait_ge(c_tgh, 1)
            v.tensor_tensor(tgl[:, 0, :], tnx[:, 0:GRP], tgh[:, 0, :].bitcast(f32), ALU.subtract).then_inc(c_tgl, 1)
            for t in range(2 * B):
                last = v.max(mx8[:, t, :], logit[:, t, :])
            last.then_inc(q_max, 1)
            v.wait_ge(q_max, 1)
            v.tensor_tensor(rdel[:, :, :], mx8[:, :, 1:2], mx8[:, :, 0:1], ALU.subtract).then_inc(q_d, 1)
            for t in range(2 * B):
                last = v.max_index(ix8[:, t, :], mx8[:, t, :], logit[:, t, :])
            last.then_inc(q_ix, 1)
            v.wait_ge(q_ix, 1)
            v.tensor_copy(ixf[:, :, :], ix8[:, :, :]).then_inc(q_ixf, 1)
            v.wait_ge(q_exp, 1)
            v.tensor_scalar(rden[:, :, :], rexp[:, :, :], 1.0, None, ALU.add).then_inc(q_den, 1)
            v.wait_ge(q_den, 1)
            v.reciprocal(wt1[:, :, :], rden[:, :, :]).then_inc(q_w1, 1)
            v.wait_ge(q_w1, 1)
            v.tensor_tensor(wt2[:, :, :], rexp[:, :, :], wt1[:, :, :], ALU.mult).then_inc(q_w2, 1)
            v.wait_ge(q_ixf, 1)
            full = [128, 2 * B, E]
            v.tensor_tensor(cwa[:, :, :], iota[:, :].unsqueeze(1).to_broadcast(full),
                            ixf[:, :, 0:1].to_broadcast(full), ALU.is_equal).then_inc(q_a, 1)
            v.tensor_tensor(cwb[:, :, :], iota[:, :].unsqueeze(1).to_broadcast(full),
                            ixf[:, :, 1:2].to_broadcast(full), ALU.is_equal).then_inc(q_b, 1)
            v.wait_ge(q_a, 1)
            v.tensor_tensor(cwa[:, :, :], cwa[:, :, :], wt1[:, :, :].to_broadcast(full), ALU.mult).then_inc(q_am, 1)
            v.wait_ge(q_b, 1)
            v.wait_ge(q_w2, 1)
            v.tensor_tensor(cwb[:, :, :], cwb[:, :, :], wt2[:, :, :].to_broadcast(full), ALU.mult).then_inc(q_bm, 1)
            v.wait_ge(q_am, 1)
            v.wait_ge(q_bm, 1)
            v.tensor_tensor(cws[:, :, :], cwa[:, :, :], cwb[:, :, :], ALU.add).then_inc(q_cw, 1)
            v.wait_ge(c_b2h, 1)
            v.tensor_tensor(f2bst[64:64 + E, :], f2bs[64:64 + E, :], f2bst[64:64 + E, :].bitcast(f32),
                            ALU.subtract).then_inc(c_b2l, 1)
            for q in range(1, 4):
                v.wait_ge(c_f1h, q + 1)
                v.tensor_tensor(f1l[:, q * w:(q + 1) * w], f1s[:, q * w:(q + 1) * w],
                                f1h[:, q * w:(q + 1) * w].bitcast(f32), ALU.subtract).then_inc(c_f1l, 1)
            for g in range(NGRP):
                v.wait_ge(ct_hi, g + 1)
                p = (pG, pM)[g % 2]
                v.tensor_tensor(cwt[32:32 + E, g * GRP:(g + 1) * GRP], p[0:E, :],
                                cwt[0:E, g * GRP:(g + 1) * GRP].bitcast(f32), ALU.subtract).then_inc(ct_lo, 1)

            def group(g, gh, par, main):
                first = isinstance(g, int) and g == 0
                for c in range(16 if main else 5):
                    if main:
                        i1, i2 = pieces(c)
                        v.wait_ge(e_h2, g * 16 + (c + 1))
                        v.wait_ge(e_sil, g * 16 + (c + 1))
                        v.scalar_tensor_tensor(gat[:, c % 4, :], (pTA, pTB)[c % 2][:, :], f1bs[:, i2:i2 + 1],
                                               sil[:, c % 2, :], ALU.add, ALU.mult).then_inc(e_gat, 1)
                    if (main and c > 0) or (c == 0 and not first):
                        k = (c - 1) % 16
                        v.wait_ge(e_gat, g * 16 + c)
                        v.wait_ge(e_cw, g * 8 + (c + 1) // 2)
                        wait(v, e_y, g * 16 + (c - 4))
                        v.tensor_tensor(act[:, k % 4, :], gat[:, k % 4, :], (pG, pM)[(k // 2) % 2][:, :],
                                        ALU.mult).then_inc(e_act, 1)
                    if c == 4 and not first:
                        v.wait_ge(y_T, g)
                        if not (isinstance(g, int) and g < 3):
                            v.wait_ge(y_dma[1 - par], (gh - 1 + par) * 16)
                        v.tensor_tensor(yo[:, 1 - par, :], (pOA, pOB)[1 - par][:, :],
                                        res2[:, bass.ds(g * GRP - GRP, GRP)], ALU.add).then_inc(y_add, 1)
                    if c == 9 and main and not (isinstance(g, int) and g == NGRP - 1):
                        v.wait_ge(c_tgh, g + 2)
                        v.tensor_tensor(tgl[:, 1 - par, :], tnx[:, bass.ds(g * GRP + GRP, GRP)],
                                        tgh[:, 1 - par, :].bitcast(f32), ALU.subtract).then_inc(c_tgl, 1)

            ffn(v, group)

        @block.tensor
        def _(pe):
            def split_product(out_, wh, wl, xh, xl):
                pe.matmul(out_, wh, xh, start=True, stop=False)
                pe.matmul(out_, wl, xh, start=False, stop=False)
                return pe.matmul(out_, wh, xl, start=False, stop=True)

            pe.wait_ge(gn_e2, 1)
            pe.wait_ge(d_c0, C0_DMAS)
            pe.matmul(pG[:, 0:2 * B], gmat[:, :], gmv[:, :, :].rearrange("p b t -> p (b t)"),
                      start=True, stop=True).then_inc(gn_mm, 1)
            pe.wait_ge(gn_cp, 1)

            def iteration(X, G, A, M, Bm, R, L):
                def keys_or_queries(n):
                    if n == 0:
                        pe.wait_ge(x_l, G.j + 1)
                        if isinstance(G.j, int) and G.j == 0:
                            pe.wait_ge(c_w0l, 1)
                    wait(pe, g_ev, G.j * GU + chunk_use(n))
                    c = NCH + n if n < NCH else n - NCH
                    split_product(pG[:, 0:TOK], w0h[:, c * 128:(c + 1) * 128], w0l[:, c * 128:(c + 1) * 128],
                                  xnh[:, G.par, :], xnl[:, G.par, :]).then_inc(g_mm, 1)

                for n in range(8):
                    if G is not None and n % 2 == 1:
                        keys_or_queries(n)
                    if Bm is not None:
                        if n == 0:
                            pe.wait_ge(m_qev, Bm.j + 1)
                            pe.wait_ge(m_vev, Bm.j + 1)
                            pe.wait_ge(k1_dma[Bm.par], Bm.half * 128 + 128)
                        wait(pe, sb_exp, Bm.j * BU + n)
                        for qc in range(2):
                            mm = pe.matmul(pSB[:, qc * TOK:(qc + 1) * TOK], q1[:, Bm.par, qc * 128:(qc + 1) * 128],
                                           kbd1[Bm.par][:, n, :], start=True, stop=True)
                        mm.then_inc(sb_mm, 1)
                    if A is not None and n % 2 == 0:
                        u = n // 2
                        pr, hf = u // 2, u % 2
                        if u == 0:
                            pe.wait_ge(g_ev, A.j * GU + (chunk_use(2 * NCH - 1) + 1))
                            pe.wait_ge(k0_dma[A.par], A.half * 64 + 64)
                        wait(pe, sa_add, A.j * AU + u)
                        for cc in range(2):
                            for w in range(2):
                                t = 128 * pr + WIN * w
                                mm = pe.matmul(pSA[WIN * w:WIN * w + WIN, cc * TOK:(cc + 1) * TOK],
                                               q0[:, A.par, 2 * hf + cc, t:t + WIN],
                                               kbd0[A.par][:, 2 * hf + cc, :, t:t + WIN], start=True, stop=True)
                        mm.then_inc(sa_mm, 1)
                    for J, k in steps_back(Bm, R, n, 1):
                        wait(pe, sb_nrm, J.j * BU + (k + 1))
                        wait(pe, tb_ev, J.j * BU + k)
                        for kc in range(2):
                            for qc in range(2):
                                mm = pe.transpose(pTB[:, kc * TOK + qc * 128:kc * TOK + (qc + 1) * 128],
                                                  pb[:, k % 2, qc, kc * 128:(kc + 1) * 128], ident[:, :])
                        mm.then_inc(tb_mm, 1)
                    if G is not None and n % 2 == 0:
                        keys_or_queries(n)
                    for J, u in turned(A, M, n):
                        wait(pe, sa_nrm, J.j * AU + (u + 1))
                        wait(pe, ta_ev, J.j * AU + u)
                        for jj in range(4):
                            mm = pe.transpose(pTA[:, jj * 128:(jj + 1) * 128],
                                              pa[:, u % 2, 2 * jj:2 * jj + 2, :].rearrange("p h k -> p (h k)"),
                                              ident[:, :])
                        mm.then_inc(ta_mm, 1)
                    for J, k in steps_back(Bm, R, n, 2):
                        wait(pe, tb_ev, J.j * BU + (k + 1))
                        if k == 0:
                            wait(pe, ob_ev, J.j)
                        r, g = D1 * 2 * (k % 4), k // 4
                        for kc in range(2):
                            mm = pe.matmul(pOB[r:r + PAD1, g * TOK:(g + 1) * TOK],
                                           v1[:, J.par, kc, k * PAD1:(k + 1) * PAD1], ptb[:, k % 2, kc, :],
                                           start=(kc == 0), stop=(kc == 1))
                        mm.then_inc(ob_mm, 1)
                    for J, u in applied(A, M, n):
                        if u == 0:
                            pe.wait_ge(g_ev, J.j * GU + GU)
                        wait(pe, ta_ev, J.j * AU + (u + 1))
                        wait(pe, oa_ev, J.j * AU + u)
                        if R is not None and n == 5:
                            pe.wait_ge(r_t, R.j + 1)
                        if R is not None and n == 7:
                            pe.wait_ge(r_x, R.j + 1)
                        pr, hf = u // 2, u % 2
                        for w in range(2):
                            for jj in range(4):
                                mm = pe.matmul(pOA[WIN * (jj % 2):WIN * (jj % 2) + WIN,
                                                   (2 * w + jj // 2) * 128:(2 * w + jj // 2 + 1) * 128],
                                               v0[J.par][:, 2 * pr + w, 4 * hf + jj, :, :].rearrange("p a d -> p (a d)"),
                                               pta[:, u % 2, jj * 128:(jj + 1) * 128], start=True, stop=True)
                        mm.then_inc(oa_mm, 1)
                    if M is not None and n == 2:
                        pe.wait_ge(oa_ev, M.j * AU + AU)
                        if L is not None:
                            pe.wait_ge(r_lgev, L.j + 1)
                        else:
                            wait(pe, m_vev, M.j)
                        for s in range(2):
                            for c in range(NCH):
                                mm = pe.matmul(pM[:, s * C:(s + 1) * C], o0[:, c, s * 128:(s + 1) * 128],
                                               wo0s[:, c, :], start=(c == 0), stop=(c == NCH - 1))
                        mm.then_inc(m_o, 1)
                    if R is not None and n == 4:
                        pe.wait_ge(ob_ev, R.j + 1)
                        if A is not None:
                            pe.wait_ge(oa_ev, A.j * AU + 1)
                        else:
                            pe.wait_ge(oa_ev, B * AU)
                            pe.wait_ge(r_x, R.j)
                        for s in range(2):
                            for g in range(2):
                                mm = pe.matmul(pOA[:, s * C:(s + 1) * C], o1[:, g, s * 128:(s + 1) * 128],
                                               wo1s[:, g, :], start=(g == 0), stop=(g == 1))
                        mm.then_inc(r_o, 1)
                    if M is not None and n == 4:
                        pe.wait_ge(m_tn, M.j + 1)
                        for s in range(2):
                            mm = pe.transpose(pM[:, s * 128:(s + 1) * 128], tn1[:, s, :], ident[:, :])
                        mm.then_inc(m_T, 1)
                    if M is not None and n == 5:
                        pe.wait_ge(m_lo, M.j + 1)
                        if isinstance(M.j, int) and M.j == 0:
                            pe.wait_ge(c_w1l, 1)
                        for part in range(2):
                            mm = split_product(pM[:, part * TOK:(part + 1) * TOK], w1h[:, part * C:(part + 1) * C],
                                               w1l[:, part * C:(part + 1) * C], t1h[:, :], t1l[:, :])
                        mm.then_inc(m_qk, 1)
                    if M is not None and n == 6:
                        pe.wait_ge(m_kev, M.j + 1)
                        pe.wait_ge(m_qev, M.j + 1)
                        for s in range(2):
                            mm = split_product(pM[:, s * TOK:(s + 1) * TOK], t1h[:, s * 128:(s + 1) * 128],
                                               t1l[:, s * 128:(s + 1) * 128], w1h[:, 2 * C:], w1l[:, 2 * C:])
                        mm.then_inc(m_v, 1)
                    if R is not None and n == 6:
                        pe.wait_ge(r_tn, R.j + 1)
                        if A is not None:
                            pe.wait_ge(oa_ev, A.j * AU + 2)
                        for s in range(2):
                            mm = pe.transpose(pOA[:, s * 128:(s + 1) * 128], tn2[:, s, :], ident[:, :])
                        mm.then_inc(r_T, 1)
                    if R is not None and n == 7:
                        pe.wait_ge(r_f, R.j + 1)
                        if M is not None:
                            pe.wait_ge(m_vev, M.j + 1)
                        else:
                            pe.wait_ge(m_vev, B)
                            wait(pe, r_lgev, R.j)
                        for s in range(2):
                            mm = pe.matmul(pM[:, s * E:(s + 1) * E], t2f[:, s * 128:(s + 1) * 128], rws[:, :],
                                           start=True, stop=True)
                        mm.then_inc(r_lg, 1)
                    if G is not None and n % 2 == 1:
                        w = n // 2
                        pe.wait_ge(g_ev, G.j * GU + value_use(w))
                        for half_ in range(2):
                            mm = pe.matmul(pG[WIN * half_:WIN * half_ + WIN, 0:TOK].rearrange("p (a d) -> p a d", d=D0),
                                           xns[:, G.par, w * WIN:(w + 1) * WIN], wv0[:, :, half_, :],
                                           start=True, stop=True)
                        mm.then_inc(g_mm, 1)

            pipeline(pe, iteration)

            pe.wait_ge(r_lgev, B)
            pe.wait_ge(c_tgl, 1)
            pe.wait_ge(q_cw, 1)
            for g in range(NGRP):
                if g >= 2:
                    pe.wait_ge(ct_lo, g - 1)
                for s in range(GRP // 128):
                    mm = pe.transpose((pG, pM)[g % 2][0:E, s * 128:(s + 1) * 128], cws[:, g * 4 + s, :], ident[:, :])
                mm.then_inc(ct_mm, 1)
            pe.wait_ge(c_b2l, 1)
            pe.wait_ge(c_sel, 1)
            pe.wait_ge(ct_lo, NGRP)

            def group(g, gh, par, main):
                first = isinstance(g, int) and g == 0
                for c in range(16 if main else 4):
                    if main:
                        if c % 2 == 0:
                            wait(pe, e_act, g * 16 + (c - 2))
                            pe.matmul((pG, pM)[(c // 2) % 2][:, :], sel[:, c // 2, :], cwt[:, bass.ds(g * GRP, GRP)],
                                      start=True, stop=True).then_inc(e_cw, 1)
                        if c == 0:
                            pe.wait_ge(c_tgl, g + 1)
                        if first and c % 4 == 0:
                            pe.wait_ge(c_f1l, c // 4 + 1)
                        i1, i2 = pieces(c)
                        wait(pe, e_sil, g * 16 + (c - 1))
                        split_product((pSA, pSB)[c % 2][:, :], f1h[:, i1 * 128:(i1 + 1) * 128],
                                      f1l[:, i1 * 128:(i1 + 1) * 128], tgh[:, par, :], tgl[:, par, :])\
                            .then_inc(e_h1, 1)
                        wait(pe, e_gat, g * 16 + (c - 1))
                        split_product((pTA, pTB)[c % 2][:, :], f1h[:, i2 * 128:(i2 + 1) * 128],
                                      f1l[:, i2 * 128:(i2 + 1) * 128], tgh[:, par, :], tgl[:, par, :])\
                            .then_inc(e_h2, 1)
                    if (main and c >= 2) or (c < 2 and not first):
                        k = (c - 2) % 16
                        y = (pOA, pOB)[par if c >= 2 else 1 - par]
                        pe.wait_ge(e_act, g * 16 + (c - 1))
                        if k == 0:
                            wait(pe, y_add, g - 1)
                            pe.matmul(y[:, :], f2bst[:, :], cwt[:, bass.ds(g * GRP, GRP)], start=True, stop=False)
                        pe.matmul(y[:, :], f2s[:, k, :], act[:, k % 4, :], start=False, stop=(k == 15))\
                            .then_inc(e_y, 1)
                    if c == 3 and not first:
                        pe.wait_ge(y_ev, g)
                        for s in range(GRP // 128):
                            mm = pe.transpose((pOA, pOB)[1 - par][:, s * 128:(s + 1) * 128],
                                              yt[:, s * 128:(s + 1) * 128], ident[:, :])
                        mm.then_inc(y_T, 1)

            ffn(pe, group)


def kernel(x, L0_conv_w_qkv, L0_conv_pos_embedding, L0_conv_w_out, L0_conv_b_out, L1_attn_w_qkv, L1_attn_b_qkv,
           L1_attn_w_out, L1_attn_b_out, L1_ffn_router_w, L1_ffn_router_b, L1_ffn_fc1_w, L1_ffn_fc1_b,
           L1_ffn_fc2_w, L1_ffn_fc2_b):
    import concourse.bacc as bacc
    from concourse.bass_utils import run_bass_kernel_spmd

    def host(a):
        return np.asarray(a)

    xr = np.roll(host(x), (-4, -4), axis=(1, 2))
    xw = xr.reshape(B, 2, 8, 2, 8, C).transpose(0, 1, 3, 2, 4, 5).reshape(NTOK, C)

    q = np.arange(WIN)
    ul = (q[:, None] >= 32) != (q[None, :] >= 32)
    lr = (q[:, None] % 8 >= 4) != (q[None, :] % 8 >= 4)
    mask = np.zeros((128, 2, WIN), np.float32)
    mask[WIN:, 0][lr] = -1e30
    mask[:WIN, 1][ul] = -1e30
    mask[WIN:, 1][ul | lr] = -1e30

    eye = np.eye(128, dtype=np.float32)
    gmat = np.kron(np.eye(32), np.full((4, 4), 0.25)).astype(np.float32)
    sel = np.zeros((128, E, 128), np.float32)
    for e in range(E):
        sel[[e, 32 + e], e, :] = 1.0
    iota = np.tile(np.arange(E, dtype=np.float32), (128, 1))

    def padded(a):
        a = a.reshape((H1, D1) + a.shape[1:])
        return np.concatenate([a, np.zeros_like(a)], axis=1).reshape((H1 * PAD1,) + a.shape[2:])

    w1 = host(L1_attn_w_qkv)
    bq = host(L1_attn_b_qkv)
    arrays = {
        "x_tok": xw,
        "x_ch": xw.T,
        "w0": host(L0_conv_w_qkv).T,
        "wo0": host(L0_conv_w_out).T,
        "bo0": np.stack([host(L0_conv_b_out)] * 2),
        "pos": host(L0_conv_pos_embedding)[:, ::-1],
        "mask": mask.reshape(128, 2 * WIN),
        "ident": eye,
        "gmat": gmat,
        "sel": sel.reshape(128, E * 128),
        "iota": iota,
        "w1": np.concatenate([w1[:, :2 * C], padded(w1[:, 2 * C:].T).T], axis=1),
        "bq1": bq[0:C].reshape(C, 1),
        "bk1": bq[C:2 * C].reshape(C, 1),
        "bv1": padded(bq[2 * C:]).reshape(2, 128).T,
        "wo1": padded(host(L1_attn_w_out)),
        "bo1": np.stack([host(L1_attn_b_out)] * 2),
        "rw": host(L1_ffn_router_w).T,
        "rb": np.stack([host(L1_ffn_router_b)] * 2),
        "f1": host(L1_ffn_fc1_w).reshape(2 * NFC * 128, C).T,
        "f1b": host(L1_ffn_fc1_b).reshape(2 * NFC, 128).T,
        "f2": host(L1_ffn_fc2_w).reshape(E, C, 2, 128).transpose(3, 0, 2, 1).reshape(128, NFC * C),
        "f2b": host(L1_ffn_fc2_b),
    }
    arrays = {n + "_dram": np.ascontiguousarray(a) for n, a in arrays.items()}

    nc = bacc.Bacc("TRN2", target_bir_lowering=False, num_devices=1)
    args = [nc.dram_tensor(n, a.shape, mybir.dt.from_np(a.dtype), kind="ExternalInput").ap()
            for n, a in arrays.items()]
    out = nc.dram_tensor("out_dram", (NTOK, C), mybir.dt.float32, kind="ExternalOutput").ap()
    hybrid_kernel(nc, *args, out)
    y = run_bass_kernel_spmd(nc, [arrays], core_ids=[0]).results[0]["out_dram"]
    y = y.reshape(B, 2, 2, 8, 8, C).transpose(0, 1, 3, 2, 4, 5).reshape(B, 16, 16, C)
    return np.roll(y, (4, 4), axis=(1, 2))
```

```python
import numpy as np
import concourse.bass as bass
from concourse import mybir
from contextlib import ExitStack

B, C = 16, 128
TOK = 256
NTOK = B * TOK
H0, D0 = 16, 32
NCH = H0 * D0 // 128
WIN = 64
NWIN = TOK // WIN
H1, D1 = 8, 16
PAD1 = 32
QK1 = 2 * C
W1COLS = 2 * QK1 + H1 * PAD1
E, HID, TOPK = 8, 256, 2
NFC = E * HID // 128
GRP = 512
NGRP = NTOK // GRP
PBUFS = 4
AU, BU = 4, 8
GU = 10
SCALE0 = D0 ** -0.5
SCALE1 = C ** -0.5
EPS = 1e-5
LOOP_FROM, LOOP_TO = 4, 14
C0_DMAS, C1_DMAS, F_DMAS = 3 * 16, 8 * 16, 5 * 16
GN_FIRST = B // 4
EARLY = 12


class Image:

    def __init__(self, j, half, par):
        self.j, self.half, self.par = j, half, par

    def cols(self, width):
        return bass.ds(self.j * width, width)


def wait(eng, sem, value):
    if isinstance(value, int) and value <= 0:
        return
    eng.wait_ge(sem, value)


def chunk_use(n):
    return n + n // NCH


def value_use(pr):
    return (NCH + 1) * pr + NCH


def steps_back(J, prev, n, back):
    k = n - back
    if k >= 0:
        return [] if J is None else [(J, k)]
    return [] if prev is None else [(prev, k + BU)]


def turned(J, prev, n):
    if n % 2:
        return []
    u = n // 2 - 1
    return [(x, u % AU) for x in ((J if u >= 0 else prev),) if x is not None]


def applied(J, prev, n):
    return turned(J, prev, n - 1) if n % 2 else []


def collected(J, prev, n):
    if n % 2:
        return []
    return applied(J, prev, n - 1) if n else ([] if prev is None else [(prev, 2)])


def values_made(G, A, n):
    if n % NCH:
        return []
    return [(x, (n // NCH - 1) % 2) for x in ((G if n else A),) if x is not None]


def hybrid_kernel(nc, x_tok, x_ch, w0, wo0, bo0, pos, mask, ident_d, gmat_d, sel_d, iota_d,
                  w1, bq1, bk1, bv1, wo1, bo1, rw, rb, f1, f1b, f2, f2b, out):
    f32, f32r, u32 = mybir.dt.float32, mybir.dt.float32r, mybir.dt.uint32
    ALU, ACT, AX = mybir.AluOpType, mybir.ActivationFunctionType, mybir.AxisListType

    ctx = ExitStack()
    with ctx:
        def sb(name, shape, dt=f32):
            return ctx.enter_context(nc.sbuf_tensor(name, shape, dt))

        def sem(name):
            return ctx.enter_context(nc.semaphore(name))

        def sem2(name):
            return [sem(f"{name}{p}") for p in range(2)]

        ident = sb("ident", [128, 128])
        gmat = sb("gmat", [128, 128])
        posr = sb("posr", [128, 8, 8])
        masks = sb("masks", [128, 2, 8, 8])
        bias0 = sb("bias0", [128, 2, 8, 8])
        half = sb("half", [128, B])
        wo0s = sb("wo0s", [128, NCH, C])
        bo0s = sb("bo0s", [128, 2, C])
        wo1s = sb("wo1s", [128, 2, C])
        bo1s = sb("bo1s", [128, 2, C])
        bq1s = sb("bq1s", [C, 2])
        bq1x = sb("bq1x", [C, 2])
        bk1s = sb("bk1s", [C, 2])
        bv1s = sb("bv1s", [128, 2])
        rws = sb("rws", [C, E])
        rbs = sb("rbs", [128, 2, E])
        xch = sb("xch", [C, NTOK])
        res2 = xch
        tnx = sb("tnx", [C, NTOK])
        logit = sb("logit", [128, 2 * B, E])
        f1bs = sb("f1bs", [128, 2 * NFC])
        f2bs = sb("f2bs", [128, C])
        iota = sb("iota", [128, E])
        with ExitStack() as first:
            def sf(name, shape):
                return first.enter_context(nc.sbuf_tensor(name, shape, f32))

            kbd0 = [sf(f"kbd0_{p}", [128, NCH, 4, TOK]) for p in range(2)]
            q0 = sf("q0", [128, 2, NCH, TOK])
            v0 = sf("v0", [128, 2, NWIN, H0 // 2, 2, D0])
        f1s = sb("f1s", [C, 2 * NFC * 128])
        f1h = sb("f1h", [C, 2 * NFC * 128], f32r)
        f2s = sb("f2s", [128, NFC, C])
        f1l = sb("f1l", [C, 2 * NFC * 128], f32r)
        wvs = q0[:, 0, 0:2, :].rearrange("p a b -> p (a b)")
        w1s = q0[:, 1, 0:3, :].rearrange("p a b -> p (a b)")

        attention = ctx.enter_context(ExitStack())

        def sa_(name, shape, dt=f32):
            return attention.enter_context(nc.sbuf_tensor(name, shape, dt))

        w0h = sa_("w0h", [C, 2 * NCH * 128], f32r)
        w0l = sa_("w0l", [C, 2 * NCH * 128], f32r)
        wvh = sa_("wvh", [C, H0 * D0], f32r)
        wvl = sa_("wvl", [C, H0 * D0], f32r)
        w1h = sa_("w1h", [C, W1COLS], f32r)
        w1l = sa_("w1l", [C, W1COLS], f32r)
        gst = sa_("gst", [C, B, 6])
        gmv = sa_("gmv", [C, B, 2])
        gsum = sa_("gsum", [C, B, 2])
        gsq = sa_("gsq", [C, B])
        grs = sa_("grs", [C, B])
        xns = sa_("xns", [C, TOK])
        xnh = sa_("xnh", [C, 2, TOK], f32r)
        xnl = sa_("xnl", [C, 2, TOK], f32r)
        kst0 = sa_("kst0", [128, NCH, TOK])
        o0 = sa_("o0", [128, NCH, TOK])
        w0s = o0[:, :, :].rearrange("p a b -> p (a b)")
        xt = sa_("xt", [128, 2, 2, C])
        t1 = sa_("t1", [128, 2, C])
        t1h = sa_("t1h", [C, TOK], f32r)
        t1l = sa_("t1l", [C, TOK], f32r)
        t1b = sa_("t1b", [128, 2, 2, C])
        t2 = sa_("t2", [128, 2, C])
        st1, st2 = sa_("st1", [128, 2, 6]), sa_("st2", [128, 2, 6])
        mv1, mv2 = sa_("mv1", [128, 2, 2]), sa_("mv2", [128, 2, 2])
        tn1, tn2 = sa_("tn1", [128, 2, C]), sa_("tn2", [128, 2, C])
        rs1, rs2 = sa_("rs1", [128, 2]), sa_("rs2", [128, 2])
        t2f = sa_("t2f", [C, TOK])
        q1 = sa_("q1", [128, 2, 2, TOK], f32r)
        kst1 = sa_("kst1", [128, 2, 2, TOK], f32r)
        kbd1 = [sa_(f"kbd1_{p}", [128, 2, 2, 4, TOK], f32r) for p in range(2)]
        v1 = sa_("v1", [128, 2, 2, H1 * PAD1])
        o1 = sa_("o1", [128, 2, TOK])
        pa = sa_("pa", [128, 2, 8, WIN])
        mxa = sa_("mxa", [128, 2, 8])
        sma = sa_("sma", [128, 2, 8])
        rca = sa_("rca", [128, 2, 8])
        pta = sa_("pta", [128, 2, 512])
        pb = sa_("pb", [128, PBUFS, 2, TOK])
        mxb = sa_("mxb", [128, PBUFS, 2])
        smb = sa_("smb", [128, PBUFS, 2])
        rcb = sa_("rcb", [128, PBUFS, 2])
        ptb = sa_("ptb", [128, 2, 2, TOK])

        attention.close()
        sel = sb("sel", [128, E, 128], f32r)
        f2bst = sb("f2bst", [128, C], f32r)
        mx8 = sb("mx8", [128, 2 * B, 8])
        ix8 = sb("ix8", [128, 2 * B, 8], u32)
        ixf = sb("ixf", [128, 2 * B, 8])
        rdel = sb("rdel", [128, 2 * B, 1])
        rexp = sb("rexp", [128, 2 * B, 1])
        rden = sb("rden", [128, 2 * B, 1])
        wt1 = sb("wt1", [128, 2 * B, 1])
        wt2 = sb("wt2", [128, 2 * B, 1])
        cwa = sb("cwa", [128, 2 * B, E])
        cwb = sb("cwb", [128, 2 * B, E])
        cws = sb("cws", [128, 2 * B, E])
        cwt = sb("cwt", [128, NTOK], f32r)
        tgh, tgl = [sb("tgh0", [C, GRP], f32r)], [sb("tgl0", [C, GRP], f32r)]
        sels = sb("sels", [128, E, 128])
        tgh.append(sb("tgh1", [C, GRP], f32r))
        tgl.append(sb("tgl1", [C, GRP], f32r))
        f2h = sb("f2h", [128, NFC, C], f32r)
        f2l = sb("f2l", [128, NFC, C], f32r)
        sil = sb("sil", [128, 2, GRP])
        gat = sb("gat", [128, 4, GRP])
        act = sb("act", [128, 4, GRP])
        acth = sb("acth", [128, 4, GRP], f32r)
        actl = sb("actl", [128, 4, GRP], f32r)
        yt = sb("yt", [128, GRP])
        yo = sb("yo", [128, 2, GRP])

        def bank(name):
            return ctx.enter_context(nc.psum_tensor(name, [128, 512], f32))

        pG, pM, pSA, pSB, pTA, pTB, pOA, pOB = (bank(n) for n in ("pG", "pM", "pSA", "pSB", "pTA", "pTB", "pOA", "pOB"))

        d_x = [sem(f"d_x{n}") for n in range(4)]
        d_c0 = sem("d_c0")
        d_c1 = sem("d_c1")
        d_gm, d_w0, d_wv = sem("d_gm"), sem("d_w0"), sem("d_wv")
        d_mask = sem("d_mask")
        d_pos = sem("d_pos")
        d_f1, d_f2, d_f = sem("d_f1"), sem("d_f2"), sem("d_f")
        d_sel = sem("d_sel")
        z_half, z_kv, z_k1 = sem("z_half"), sem2("z_kv"), sem("z_k1")
        c_w0h, c_w0l, c_wvh, c_wvl, c_w1s, c_w1h, c_w1l, c_bq, c_bias = (
            sem(n) for n in ("c_w0h", "c_w0l", "c_wvh", "c_wvl", "c_w1s", "c_w1h", "c_w1l", "c_bq", "c_bias"))
        gn_st, gn_ag, gn_sq, gn_e2, gn_mm, gn_cp, gn_q, gn_v, gn_eps, gn_pow = (
            sem(n) for n in ("gn_st", "gn_ag", "gn_sq", "gn_e2", "gn_mm", "gn_cp", "gn_q", "gn_v", "gn_eps", "gn_pow"))
        x_c, x_s, x_h, x_l = sem("x_c"), sem("x_s"), sem("x_h"), sem("x_l")
        g_mm, g_ev = sem("g_mm"), sem("g_ev")
        k0_dma = [sem("k0_dma0"), sem("k0_dma1")]
        sa_mm, sa_add, sa_max, sa_sub, sa_exp, sa_sum, sa_rcp, sa_nrm = (
            sem(n) for n in ("sa_mm", "sa_add", "sa_max", "sa_sub", "sa_exp", "sa_sum", "sa_rcp", "sa_nrm"))
        ta_mm, ta_ev, oa_mm, oa_ev = (sem(n) for n in ("ta_mm", "ta_ev", "oa_mm", "oa_ev"))
        sb_mm, sb_max, sb_exp, sb_rcp, sb_nrm = (sem(n) for n in ("sb_mm", "sb_max", "sb_exp", "sb_rcp", "sb_nrm"))
        tb_mm, tb_ev, ob_mm, ob_ev = (sem(n) for n in ("tb_mm", "tb_ev", "ob_mm", "ob_ev"))
        xt_dma = [sem("xt_dma0"), sem("xt_dma1")]
        k1_dma = [sem("k1_dma0"), sem("k1_dma1")]
        m_xb, m_o, m_t, m_st, m_ag, m_eps, m_pow, m_tn, m_T, m_hi, m_lo, m_k, m_khi, m_klo, m_q, m_qhi, m_qlo = (
            sem(n) for n in ("m_xb", "m_o", "m_t", "m_st", "m_ag", "m_eps", "m_pow", "m_tn", "m_T", "m_hi", "m_lo",
                             "m_k", "m_khi", "m_klo", "m_q", "m_qhi", "m_qlo"))
        m_v, m_vev, m_tb, m_ctr, r_ctr = (sem(n) for n in ("m_v", "m_vev", "m_tb", "m_ctr", "r_ctr"))
        r_o, r_t, r_st, r_ag, r_eps, r_pow, r_tn, r_T, r_f, r_x, r_lg, r_lgev = (
            sem(n) for n in ("r_o", "r_t", "r_st", "r_ag", "r_eps", "r_pow", "r_tn", "r_T", "r_f", "r_x",
                             "r_lg", "r_lgev"))
        c_f1h, c_f1l, c_tgh, c_tgl, c_sel, c_b2z, c_b2h, c_b2l, c_cwz, c_f2h, c_f2l = (
            sem(n) for n in ("c_f1h", "c_f1l", "c_tgh", "c_tgl", "c_sel", "c_b2z", "c_b2h", "c_b2l", "c_cwz", "c_f2h", "c_f2l"))
        q_max, q_ix, q_ixf, q_d, q_exp, q_den, q_w1, q_w2, q_a, q_b, q_am, q_bm, q_cw = (
            sem(n) for n in ("q_max", "q_ix", "q_ixf", "q_d", "q_exp", "q_den", "q_w1", "q_w2", "q_a", "q_b",
                             "q_am", "q_bm", "q_cw"))
        ct_mm, ct_hi, ct_lo = sem("ct_mm"), sem("ct_hi"), sem("ct_lo")
        e_cw, e_h1, e_h2, e_sil, e_gat, e_act, e_ahi, e_alo, e_y = (
            sem(n) for n in ("e_cw", "e_h1", "e_h2", "e_sil", "e_gat", "e_act", "e_ahi", "e_alo", "e_y"))
        y_ev, y_T, y_add = sem("y_ev"), sem("y_T"), sem("y_add")
        y_dma = [sem("y_dma0"), sem("y_dma1")]

        out_v = out.rearrange("(g s p) c -> g p s c", s=GRP // 128, p=128)
        xt_v = x_tok.rearrange("(b s p) c -> p b s c", s=2, p=128)
        pos_t = pos.tensor
        w0v = w0[:, 2 * H0 * D0:3 * H0 * D0]

        LAGS = (2, 1, 0, -1, -2, -3, -4)

        def peeled(i):
            return [Image(i + lag, (i + lag) // 2, (i + lag) % 2) if 0 <= i + lag < B else None for lag in LAGS]

        def looped(it, p):
            first = LOOP_FROM + p
            return [Image(it * 2 + (first + lag), it + (first + lag) // 2, (first + lag) % 2) for lag in LAGS]

        def pipeline(eng, iteration, after=None):
            for i in range(-2, LOOP_FROM):
                iteration(*peeled(i))
                if after is not None:
                    after(i)
            with eng.Fori(0, (LOOP_TO - LOOP_FROM) // 2) as it:
                for p in range(2):
                    iteration(*looped(it, p))
            for i in range(LOOP_TO, B + 4):
                iteration(*peeled(i))
                if after is not None:
                    after(i)

        def ffn(eng, group):
            for g in range(3):
                group(g, g // 2, g % 2, True)
            with eng.Fori(0, (NGRP - 4) // 2) as it:
                for p in range(2):
                    group(it * 2 + (3 + p), it + (3 + p) // 2, (3 + p) % 2, True)
            group(NGRP - 1, (NGRP - 1) // 2, (NGRP - 1) % 2, True)
            group(NGRP, NGRP // 2, NGRP % 2, False)

        def pieces(c):
            e, hc = c // 2, c % 2
            return (e * 4 + hc, e * 4 + 2 + hc)

        def tiles(part):
            return slice(0, 2 * EARLY) if part == 0 else slice(2 * EARLY, 2 * B)

        def projection(J, use):
            return pM if isinstance(J.j, int) and J.j < 2 and use % 2 else pG

        def projection_read(J, use):
            return J.j * GU + use - (1 if isinstance(J.j, int) and J.j < 2 else 0)

        GN_PARTS = (range(0, GN_FIRST), range(GN_FIRST, B))

        block = ctx.enter_context(nc.Block())

        @block.sync
        def _(sp):
            sp.dma_start(xch[:, 0:NTOK // 4], x_ch[:, 0:NTOK // 4]).then_inc(d_x[0], 16)
            sp.dma_start(xch[:, NTOK // 4:NTOK // 2], x_ch[:, NTOK // 4:NTOK // 2]).then_inc(d_x[1], 16)
            sp.dma_start(masks[:, :, :, :], mask.rearrange("p (r x y) -> p r x y", r=2, x=8)).then_inc(d_mask, 16)
            for qx in range(8):
                for r in range(2):
                    p = r * WIN + qx * 8
                    sp.dma_start(posr[p:p + 8, :, :],
                                bass.AP(tensor=pos_t, offset=(7 - qx) * 15, ap=[[1, 8], [15, 8], [1, 8]]))\
                     .then_inc(d_pos, 16)
            sp.dma_start(xch[:, NTOK // 2:3 * NTOK // 4], x_ch[:, NTOK // 2:3 * NTOK // 4]).then_inc(d_x[2], 16)
            sp.dma_start(xch[:, 3 * NTOK // 4:NTOK], x_ch[:, 3 * NTOK // 4:NTOK]).then_inc(d_x[3], 16)
            sp.dma_start(ident[:, :], ident_d).then_inc(d_c0, 16)
            sp.dma_start(wo0s[:, :, :], wo0.rearrange("(j p) c -> p j c", p=128)).then_inc(d_c0, 16)
            sp.dma_start(bo0s[:, :, :], bo0.partition_broadcast(128)).then_inc(d_c0, 16)
            sp.dma_start(wo1s[:, :, :], wo1.rearrange("(g p) c -> p g c", p=128)).then_inc(d_c1, 16)
            sp.dma_start(bo1s[:, :, :], bo1.partition_broadcast(128)).then_inc(d_c1, 16)
            sp.dma_start(w1s, w1).then_inc(d_c1, 16)
            sp.dma_start(bq1s[:, :], bq1).then_inc(d_c1, 16)
            sp.dma_start(bk1s[:, :], bk1).then_inc(d_c1, 16)
            sp.dma_start(bv1s[:, :], bv1).then_inc(d_c1, 16)
            sp.dma_start(rws[:, :], rw).then_inc(d_c1, 16)
            sp.dma_start(rbs[:, :, :], rb.partition_broadcast(128)).then_inc(d_c1, 16)
            sp.dma_start(f1bs[:, :], f1b).then_inc(d_f, 16)
            sp.dma_start(f2bs[0:E, :], f2b).then_inc(d_f, 16)
            sp.dma_start(f2bs[32:32 + E, :], f2b).then_inc(d_f, 16)
            sp.dma_start(f2bs[64:64 + E, :], f2b).then_inc(d_f, 16)
            sp.dma_start(iota[:, :], iota_d).then_inc(d_f, 16)

            def iteration(X, G, A, M, Bm, R, L):
                if A is not None:
                    wait(sp, m_t, A.j - 1)
                if G is not None:
                    wait(sp, g_ev, G.j * GU + (chunk_use(NCH - 1) + 1))
                    if isinstance(G.j, int) and G.j < 2:
                        sp.wait_ge(z_kv[G.j], 1)
                    for h in range(4):
                        sp.dma_start(kbd0[G.par][32 * h:32 * h + 32, :, h, :],
                                     kst0[32 * h:32 * h + 32, :, :]).then_inc(k0_dma[G.par], 16)
                if A is not None:
                    sp.dma_start(xt[:, A.par, :, :],
                                 xt_v[:, bass.ds(A.j, 1), :, :].rearrange("p b s c -> p (b s) c"))\
                      .then_inc(xt_dma[A.par], 16)
                if M is not None:
                    wait(sp, m_klo, M.j + 1)
                    if isinstance(M.j, int) and M.j < 2:
                        sp.wait_ge(z_k1, M.j + 1)
                    for h in range(8):
                        rows = slice(D1 * h, D1 * h + D1)
                        sp.dma_start(kbd1[M.par][rows, :, :, h % 4, :].bitcast(f32), kst1[rows, :, :, :].bitcast(f32))\
                          .then_inc(k1_dma[M.par], 16)

            def after(i):
                if i == B - 1:
                    sp.wait_ge(sa_mm, (B - 1) * AU)
                    sp.dma_start(f1s[:, :], f1).then_inc(d_f1, 16)
                if i == B:
                    sp.wait_ge(sa_mm, B * AU)
                    sp.dma_start(f2s[:, :, :], f2.rearrange("p (j d) -> p j d", d=C)).then_inc(d_f2, 16)
                    sp.wait_ge(m_v, B)
                    sp.dma_start(sels[:, :, :], sel_d.rearrange("p (e c) -> p e c", e=E)).then_inc(d_sel, 16)

            pipeline(sp, iteration, after)

            for g in range(NGRP):
                sp.wait_ge(y_add, g + 1)
                sp.dma_start(out_v[g, :, :, :], yo[:, g % 2, :].rearrange("p (s c) -> p s c", c=C))\
                  .then_inc(y_dma[g % 2], 16)
            for p in range(2):
                sp.wait_ge(y_dma[p], 16 * NGRP // 2)

        @block.gpsimd
        def _(pool):
            pool.memset(half[:, :], -0.5).then_inc(z_half, 1)
            pool.wait_ge(z_half, 1)

            def group_roots(part):
                t = slice(GN_PARTS[part].start, GN_PARTS[part].stop)
                pool.wait_ge(gn_eps, part + 1)
                pool.tensor_tensor(grs[:, t], gsq[:, t], half[:, t], ALU.pow).then_inc(gn_pow, 1)
                pool.wait_ge(gn_pow, part + 1)

            group_roots(0)

            def iteration(X, G, A, M, Bm, R, L):
                if X is not None and isinstance(X.j, int) and X.j == GN_FIRST:
                    group_roots(1)
                if X is not None and isinstance(X.j, int) and X.j == 1:
                    pool.memset(kbd0[0][:, :, :, :], 0.0)
                    pool.memset(v0[:, 0, :, :, :, :], 0.0).then_inc(z_kv[0], 1)
                if X is not None and isinstance(X.j, int) and X.j in (2, 3):
                    pool.memset(kbd1[X.par][:, :, :, :, :].bitcast(f32), 0.0).then_inc(z_k1, 1)
                for n in range(8):
                    if n == 0 and M is not None:
                        if isinstance(M.j, int) and M.j == 0:
                            pool.wait_ge(d_c0, C0_DMAS)
                        pool.wait_ge(xt_dma[M.par], M.half * 16 + 16)
                        pool.tensor_tensor(xt[:, M.par, :, :], xt[:, M.par, :, :], bo0s[:, :, :],
                                           ALU.add).then_inc(m_xb, 1)
                    if n == 4 and M is not None:
                        pool.wait_ge(m_eps, M.j + 1)
                        pool.tensor_tensor(rs1[:, :], rs1[:, :], half[:, 0:2], ALU.pow).then_inc(m_pow, 1)
                        pool.wait_ge(m_pow, M.j + 1)
                        wait(pool, m_T, M.j)
                        pool.tensor_tensor(tn1[:, :, :], t1[:, :, :],
                                           mv1[:, :, 0:1].to_broadcast([128, 2, C]), ALU.subtract).then_inc(m_ctr, 1)
                        pool.wait_ge(m_ctr, M.j + 1)
                        pool.tensor_tensor(tn1[:, :, :], tn1[:, :, :],
                                           rs1[:, :].unsqueeze(2).to_broadcast([128, 2, C]),
                                           ALU.mult).then_inc(m_tn, 1)
                    if n == 5 and M is not None:
                        pool.wait_ge(m_t, M.j + 1)
                        wait(pool, r_t, M.j - 1)
                        pool.tensor_tensor(t1b[:, M.par, :, :], t1[:, :, :], bo1s[:, :, :], ALU.add).then_inc(m_tb, 1)
                    if n == 6 and R is not None:
                        pool.wait_ge(r_eps, R.j + 1)
                        pool.tensor_tensor(rs2[:, :], rs2[:, :], half[:, 0:2], ALU.pow).then_inc(r_pow, 1)
                        pool.wait_ge(r_pow, R.j + 1)
                        wait(pool, r_T, R.j)
                        pool.tensor_tensor(tn2[:, :, :], t2[:, :, :],
                                           mv2[:, :, 0:1].to_broadcast([128, 2, C]), ALU.subtract).then_inc(r_ctr, 1)
                        pool.wait_ge(r_ctr, R.j + 1)
                        pool.tensor_tensor(tn2[:, :, :], tn2[:, :, :],
                                           rs2[:, :].unsqueeze(2).to_broadcast([128, 2, C]),
                                           ALU.mult).then_inc(r_tn, 1)
                    if Bm is not None:
                        b = n % PBUFS
                        pool.wait_ge(sb_rcp, Bm.j * BU + (n + 1))
                        pool.tensor_tensor(pb[:, b, :, :], pb[:, b, :, :],
                                           rcb[:, b, :].unsqueeze(2).to_broadcast([128, 2, TOK]),
                                           ALU.mult).then_inc(sb_nrm, 1)
                    if A is not None and n % 2 == 1:
                        u = n // 2
                        b = u % 2
                        pool.wait_ge(sa_rcp, A.j * AU + (u + 1))
                        pool.tensor_tensor(pa[:, b, :, :], pa[:, b, :, :],
                                           rca[:, b, :].unsqueeze(2).to_broadcast([128, 8, WIN]),
                                           ALU.mult).then_inc(sa_nrm, 1)
                    if X is not None and n == 0:
                        wait(pool, x_l, X.j)
                        pool.tensor_tensor(xns[:, :], xch[:, X.cols(TOK)],
                                           gsum[:, X.cols(1), 0].to_broadcast([C, TOK]),
                                           ALU.subtract).then_inc(x_c, 1)
                        pool.wait_ge(x_c, X.j + 1)
                        pool.tensor_tensor(xns[:, :], xns[:, :], grs[:, X.cols(1)].to_broadcast([C, TOK]),
                                           ALU.mult).then_inc(x_s, 1)
                    if X is not None and n == 4:
                        pool.wait_ge(x_h, X.j + 1)
                        pool.tensor_tensor(xnl[:, X.par, :], xns[:, :], xnh[:, X.par, :].bitcast(f32),
                                           ALU.subtract).then_inc(x_l, 1)

            def after(i):
                if i == B:
                    pool.wait_ge(m_v, B)
                    pool.memset(cwt[:, :].bitcast(f32), 0.0).then_inc(c_cwz, 1)

            pipeline(pool, iteration, after)

            pool.wait_ge(r_lgev, B)

            def group(g, gh, par, main):
                first = isinstance(g, int) and g == 0
                for c in range(16 if main else 2):
                    if c >= 2 or not first:
                        k = (c - 2) % 16
                        pool.wait_ge(e_ahi, g * 16 + (c - 1))
                        wait(pool, e_y, g * 16 + (c - 5))
                        pool.tensor_tensor(actl[:, k % 4, :], act[:, k % 4, :], acth[:, k % 4, :].bitcast(f32),
                                           ALU.subtract).then_inc(e_alo, 1)

            ffn(pool, group)

        @block.scalar
        def _(a):
            a.dma_start(gmat[:, :], gmat_d).then_inc(d_gm, 16)
            a.dma_start(w0s, w0[:, 0:2 * H0 * D0]).then_inc(d_w0, 16)
            a.dma_start(wvs, w0v).then_inc(d_wv, 16)
            a.wait_ge(d_w0, 16)
            a.activation(w0h[:, :], w0s, ACT.Copy).then_inc(c_w0h, 1)
            a.wait_ge(d_wv, 16)
            a.activation(wvh[:, :], wvs, ACT.Copy).then_inc(c_wvh, 1)

            def iteration(X, G, A, M, Bm, R, L):
                def keys_or_queries(n):
                    a.wait_ge(g_mm, G.j * GU + (chunk_use(n) + 1))
                    if n < NCH:
                        if n == 0:
                            wait(a, k0_dma[(G.par + 1) % 2],
                                 (G.half + G.par) * 64 if not isinstance(G.j, int) or G.j > 0 else 0)
                        a.activation(kst0[:, n, :], projection(G, chunk_use(n))[:, 0:TOK], ACT.Copy).then_inc(g_ev, 1)
                    else:
                        wait(a, sa_mm, (G.j - 1) * AU)
                        if isinstance(G.j, int) and G.j < 2:
                            a.wait_ge((c_wvl, c_w1l)[G.j], 1)
                        a.activation(q0[:, G.par, n - NCH, :], projection(G, chunk_use(n))[:, 0:TOK], ACT.Copy,
                                     scale=SCALE0).then_inc(g_ev, 1)

                for n in range(8):
                    if Bm is not None and n == 0:
                        a.wait_ge(m_v, Bm.j + 1)
                        wait(a, ob_mm, (Bm.j - 1) * BU)
                        a.activation(v1[:, Bm.par, :, :], pM[:, :].rearrange("p (a b) -> p a b", a=2),
                                     ACT.Copy).then_inc(m_vev, 1)
                    if R is not None and n == 3:
                        a.wait_ge(ob_mm, R.j * BU + BU)
                        wait(a, r_o, R.j)
                        for g in range(2):
                            last = a.activation(o1[:, g, :], pOB[:, g * TOK:(g + 1) * TOK], ACT.Identity,
                                                bias=bv1s[:, g:g + 1])
                        last.then_inc(ob_ev, 1)
                    for J, u in collected(A, M, n):
                        wait(a, oa_mm, J.j * AU + (u + 1))
                        if u == 0:
                            wait(a, m_o, J.j)
                        pr, hf = u // 2, u % 2
                        for w in range(2):
                            o = pOA[:, w * TOK:(w + 1) * TOK].rearrange("p (c q) -> p c q", c=2)
                            last = a.activation(o0[:, 2 * hf:2 * hf + 2, 128 * pr + WIN * w:128 * pr + WIN * w + WIN],
                                                o[:, :, WIN * w:WIN * w + WIN], ACT.Copy)
                        last.then_inc(oa_ev, 1)
                    for J, pr in values_made(G, A, n):
                        a.wait_ge(g_mm, J.j * GU + (value_use(pr) + 1))
                        if isinstance(J.j, int) and J.j < 2:
                            a.wait_ge(z_kv[J.j], 1)
                        wait(a, oa_mm, (J.j - 2) * AU + 2 * pr + 2)
                        for w in range(2):
                            for half_ in range(2):
                                last = a.activation(
                                    v0[WIN * half_:WIN * half_ + WIN, J.par, 2 * pr + w, :, half_, :],
                                    projection(J, value_use(pr))[WIN * w:WIN * w + WIN, :].rearrange("p (a b d) -> p a b d", b=2, d=D0)
                                    [:, :, half_, :], ACT.Copy)
                        last.then_inc(g_ev, 1)
                    if M is not None and n == 5:
                        a.wait_ge(m_T, M.j + 1)
                        wait(a, m_v, M.j)
                        a.activation(t1h[:, :], pM[:, 0:TOK], ACT.Copy).then_inc(m_hi, 1)
                    if M is not None and n == 6:
                        a.wait_ge(m_k, M.j + 1)
                        wait(a, k1_dma[(M.par + 1) % 2],
                             (M.half + M.par) * 128 if not isinstance(M.j, int) or M.j > 0 else 0)
                        for g in range(2):
                            last = a.activation(kst1[:, 0, g, :], pM[:, g * TOK:(g + 1) * TOK], ACT.Identity,
                                                bias=bk1s[:, g:g + 1])
                        last.then_inc(m_khi, 1)
                    if X is not None and n == 3:
                        wait(a, g_mm, (X.j - 1) * GU)
                        a.wait_ge(x_s, X.j + 1)
                        a.activation(xnh[:, X.par, :], xns[:, :], ACT.Copy).then_inc(x_h, 1)
                    if M is not None and n == 7:
                        a.wait_ge(m_q, M.j + 1)
                        if isinstance(M.j, int) and M.j == 0:
                            a.wait_ge(c_bq, 1)
                        wait(a, sb_mm, (M.j - 1) * BU)
                        for g in range(2):
                            last = a.activation(q1[:, M.par, g, :], pM[:, g * TOK:(g + 1) * TOK], ACT.Identity,
                                                bias=bq1x[:, g:g + 1])
                        last.then_inc(m_qhi, 1)
                    if A is not None and n % 2 == 1:
                        u = n // 2
                        a.wait_ge(sa_sub, A.j * AU + (u + 1))
                        a.activation(pa[:, u % 2, :, :], pa[:, u % 2, :, :], ACT.Exp).then_inc(sa_exp, 1)
                    if R is not None and n == 7:
                        a.wait_ge(r_T, R.j + 1)
                        wait(a, r_lg, R.j)
                        a.activation(t2f[:, :], pOA[:, 0:TOK], ACT.Copy).then_inc(r_f, 1)
                        a.activation(tnx[:, R.cols(TOK)], pOA[:, 0:TOK], ACT.Copy).then_inc(r_x, 1)
                    if G is not None and n % 2 == 1:
                        keys_or_queries(n)
                    if Bm is not None:
                        b = n % PBUFS
                        wait(a, sb_max, Bm.j * BU + (n + 1))
                        wait(a, sb_rcp, Bm.j * BU + (n + 1 - PBUFS))
                        wait(a, tb_mm, Bm.j * BU + (n + 1 - PBUFS))
                        for qc in range(2):
                            last = a.activation(pb[:, b, qc, :], (pSB, pSA)[n % 2][:, qc * TOK:(qc + 1) * TOK], ACT.Exp,
                                                bias=mxb[:, b, qc:qc + 1], accum_out=smb[:, b, qc:qc + 1])
                        last.then_inc(sb_exp, 1)
                    for J, k in steps_back(Bm, R, n, 2):
                        wait(a, tb_mm, J.j * BU + (k + 1))
                        wait(a, ob_mm, J.j * BU + (k - 1))
                        a.activation(ptb[:, k % 2, :, :], pTB[:, :].rearrange("p (a b) -> p a b", a=2),
                                     ACT.Copy).then_inc(tb_ev, 1)
                    if G is not None and n % 2 == 0:
                        keys_or_queries(n)
                    for J, u in turned(A, M, n):
                        wait(a, ta_mm, J.j * AU + (u + 1))
                        wait(a, oa_mm, J.j * AU + (u - 1))
                        a.activation(pta[:, u % 2, :], pTA[:, :], ACT.Copy).then_inc(ta_ev, 1)

            def choice_exponentials(part):
                a.wait_ge(q_d, part + 1)
                t = tiles(part)
                a.activation(rexp[:, t, :], rdel[:, t, :], ACT.Exp).then_inc(q_exp, 1)

            def weights_high(g, bank):
                a.wait_ge(ct_mm, g + 1)
                a.activation(cwt[0:E, g * GRP:(g + 1) * GRP], bank[0:E, :], ACT.Copy)
                a.activation(cwt[64:64 + E, g * GRP:(g + 1) * GRP], bank[0:E, :], ACT.Copy).then_inc(ct_hi, 1)

            def after(i):
                if i == -1:
                    a.wait_ge(d_c1, C1_DMAS)
                    a.activation(w1s[:, 0:QK1], w1s[:, 0:QK1], ACT.Copy, scale=SCALE1).then_inc(c_w1s, 1)
                    a.wait_ge(c_w1s, 1)
                    a.activation(w1h[:, :], w1s, ACT.Copy).then_inc(c_w1h, 1)
                    a.activation(bq1x[:, :], bq1s[:, :], ACT.Copy, scale=SCALE1).then_inc(c_bq, 1)
                if i == B:
                    a.wait_ge(m_v, B)
                    a.wait_ge(d_f1, 16)
                    for q in range(4):
                        w = 2 * NFC * 128 // 4
                        a.activation(f1h[:, q * w:(q + 1) * w], f1s[:, q * w:(q + 1) * w], ACT.Copy).then_inc(c_f1h, 1)
                    a.wait_ge(r_x, 2)
                    a.activation(tgh[0][:, :], tnx[:, 0:GRP], ACT.Copy).then_inc(c_tgh, 1)
                    a.wait_ge(c_b2z, 1)
                    a.wait_ge(d_f, F_DMAS)
                    for r in range(3):
                        last = a.activation(f2bst[32 * r:32 * r + E, :], f2bs[32 * r:32 * r + E, :], ACT.Copy)
                    last.then_inc(c_b2h, 1)
                if i == B + 1:
                    choice_exponentials(0)
                    a.wait_ge(d_sel, 16)
                    a.activation(sel[:, :, :], sels[:, :, :], ACT.Copy).then_inc(c_sel, 1)
                if i == B + 2:
                    a.wait_ge(c_cwz, 1)
                    for g in range(EARLY // 2):
                        weights_high(g, (pG, pTA)[g % 2])

            pipeline(a, iteration, after)

            a.wait_ge(r_lgev, B)
            choice_exponentials(1)
            a.wait_ge(d_f2, 16)

            def group(g, gh, par, main):
                first = isinstance(g, int) and g == 0
                for c in range(16 if main else 5):
                    if main:
                        a.wait_ge(e_h1, g * 16 + (c + 1))
                        wait(a, e_gat, g * 16 + (c - 1))
                        i1, _ = pieces(c)
                        a.activation(sil[:, c % 2, :], (pSA, pSB)[c % 2][:, :], ACT.Silu,
                                     bias=f1bs[:, i1:i1 + 1]).then_inc(e_sil, 1)
                    if (main and c >= 2) or (c < 2 and not first):
                        k = (c - 2) % 16
                        a.wait_ge(e_act, g * 16 + (c - 1))
                        wait(a, e_y, g * 16 + (c - 5))
                        a.activation(acth[:, k % 4, :], act[:, k % 4, :], ACT.Copy).then_inc(e_ahi, 1)
                    if first and c < 2:
                        h = slice(c * NFC // 2, (c + 1) * NFC // 2)
                        a.activation(f2h[:, h, :], f2s[:, h, :], ACT.Copy).then_inc(c_f2h, 1)
                    if first and c in (9, 13):
                        weights_high(EARLY // 2 + (c - 9) // 4, pOB)
                    if c == 4 and not first:
                        a.wait_ge(e_y, g * 16)
                        wait(a, y_T, g - 1)
                        a.activation(yt[:, :], (pOA, pOB)[1 - par][:, :], ACT.Copy).then_inc(y_ev, 1)
                    if c == 8 and main and not (isinstance(g, int) and g == NGRP - 1):
                        wait(a, e_h2, g * 16)
                        a.activation(tgh[1 - par][:, :], tnx[:, bass.ds(g * GRP + GRP, GRP)],
                                     ACT.Copy).then_inc(c_tgh, 1)

            ffn(a, group)

        @block.vector
        def _(v):
            def statistics(images, part):
                for j in images:
                    if j % 4 == 0:
                        v.wait_ge(d_x[j // 4], 16)
                    last = v.bn_stats(gst[:, j, :], xch[:, j * TOK:(j + 1) * TOK])
                last.then_inc(gn_st, 1)
                v.wait_ge(gn_st, part)
                for j in images:
                    last = v.bn_aggr(gmv[:, j, :], gst[:, j, :])
                last.then_inc(gn_ag, 1)
                v.wait_ge(gn_ag, part)
                t = slice(images.start, images.stop)
                v.tensor_tensor(gsq[:, t], gmv[:, t, 0], gmv[:, t, 0], ALU.mult).then_inc(gn_sq, 1)
                v.wait_ge(gn_sq, part)
                v.tensor_tensor(gmv[:, t, 1], gmv[:, t, 1], gsq[:, t], ALU.add).then_inc(gn_e2, 1)

            def group_variance(images, part):
                t = slice(images.start, images.stop)
                v.wait_ge(gn_mm, part)
                v.tensor_copy(gsum[:, t, :], pOB[:, 2 * t.start:2 * t.stop].rearrange("p (b t) -> p b t", t=2))\
                 .then_inc(gn_cp, 1)
                v.wait_ge(gn_cp, part)
                v.tensor_tensor(gsq[:, t], gsum[:, t, 0], gsum[:, t, 0], ALU.mult).then_inc(gn_q, 1)
                v.wait_ge(gn_q, part)
                v.tensor_tensor(gsq[:, t], gsum[:, t, 1], gsq[:, t], ALU.subtract).then_inc(gn_v, 1)
                v.wait_ge(gn_v, part)
                v.tensor_scalar(gsq[:, t], gsq[:, t], EPS, None, ALU.add).then_inc(gn_eps, 1)

            statistics(GN_PARTS[0], 1)
            group_variance(GN_PARTS[0], 1)
            v.wait_ge(c_w0h, 1)
            v.tensor_tensor(w0l[:, :], w0s, w0h[:, :].bitcast(f32), ALU.subtract).then_inc(c_w0l, 1)
            v.wait_ge(c_wvh, 1)
            v.tensor_tensor(wvl[:, :], wvs, wvh[:, :].bitcast(f32), ALU.subtract).then_inc(c_wvl, 1)
            v.wait_ge(d_mask, 16)
            v.wait_ge(d_pos, 16 * 16)
            for pr in range(2):
                for ky in range(8):
                    last = v.tensor_tensor(bias0[:, pr, :, ky], posr[:, :, 7 - ky], masks[:, pr, :, ky], ALU.add)
            last.then_inc(c_bias, 1)
            statistics(GN_PARTS[1], 2)
            v.memset(kbd0[1][:, :, :, :], 0.0)
            v.memset(v0[:, 1, :, :, :, :], 0.0).then_inc(z_kv[1], 1)

            def iteration(X, G, A, M, Bm, R, L):
                def reciprocal_b(n):
                    b = n % PBUFS
                    v.wait_ge(sb_exp, Bm.j * BU + (n + 1))
                    wait(v, sb_nrm, Bm.j * BU + (n + 1 - PBUFS))
                    v.reciprocal(rcb[:, b, :], smb[:, b, :]).then_inc(sb_rcp, 1)

                for n in range(8):
                    if L is not None and n == 2:
                        v.wait_ge(r_lg, L.j + 1)
                        v.tensor_tensor(logit[:, bass.ds(L.j * 2, 2), :],
                                        pM[:, 0:2 * E].rearrange("p (s e) -> p s e", s=2), rbs[:, :, :],
                                        ALU.add).then_inc(r_lgev, 1)
                    if M is not None and n == 6:
                        v.wait_ge(m_khi, M.j + 1)
                        for g in range(2):
                            last = v.scalar_tensor_tensor(kst1[:, 1, g, :], pM[:, g * TOK:(g + 1) * TOK],
                                                          bk1s[:, g:g + 1], kst1[:, 0, g, :].bitcast(f32),
                                                          ALU.add, ALU.subtract)
                        last.then_inc(m_klo, 1)
                    if M is not None and n == 7:
                        v.wait_ge(m_qhi, M.j + 1)
                        for g in range(2):
                            last = v.scalar_tensor_tensor(q1[64:, M.par, g, :], pM[64:, g * TOK:(g + 1) * TOK],
                                                          bq1x[64:, g:g + 1], q1[64:, M.par, g, :].bitcast(f32),
                                                          ALU.add, ALU.subtract)
                        last.then_inc(m_qlo, 1)
                    if M is not None and n == 3:
                        v.wait_ge(m_o, M.j + 1)
                        v.wait_ge(m_xb, M.j + 1)
                        wait(v, m_tb, M.j)
                        v.tensor_tensor(t1[:, :, :], pM[:, 0:TOK].rearrange("p (s c) -> p s c", s=2),
                                        xt[:, M.par, :, :], ALU.add).then_inc(m_t, 1)
                        v.wait_ge(m_t, M.j + 1)
                        for s in range(2):
                            last = v.bn_stats(st1[:, s, :], t1[:, s, :])
                        last.then_inc(m_st, 1)
                    if M is not None and n == 3:
                        v.wait_ge(m_st, M.j + 1)
                    if R is not None and n == 5:
                        v.wait_ge(r_o, R.j + 1)
                        v.wait_ge(m_tb, R.j + 1)
                        v.tensor_tensor(t2[:, :, :], pOA[:, 0:TOK].rearrange("p (s c) -> p s c", s=2),
                                        t1b[:, R.par, :, :], ALU.add).then_inc(r_t, 1)
                    if Bm is not None:
                        bank, b1 = (pSB, pSA)[n % 2], n % PBUFS
                        v.wait_ge(sb_mm, Bm.j * BU + (n + 1))
                        v.tensor_reduce(mxb[:, b1, :], bank[:, :].rearrange("p (a k) -> p a k", a=2), AX.X, ALU.max,
                                        negate=True).then_inc(sb_max, 1)
                    if M is not None and n == 3:
                        for s in range(2):
                            last = v.bn_aggr(mv1[:, s, :], st1[:, s, :])
                        last.then_inc(m_ag, 1)
                        v.wait_ge(m_ag, M.j + 1)
                        v.tensor_scalar(rs1[:, :], mv1[:, :, 1], EPS, None, ALU.add).then_inc(m_eps, 1)
                    if A is not None and n % 2 == 0:
                        u = n // 2
                        b = u % 2
                        if isinstance(A.j, int) and A.j == 0 and u == 0:
                            v.wait_ge(c_bias, 1)
                        v.wait_ge(sa_mm, A.j * AU + (u + 1))
                        wait(v, ta_mm, A.j * AU + (u - 1))
                        v.tensor_tensor(pa[:, b, :, :], pSA[:, :].rearrange("p (h k) -> p h k", h=8),
                                        bias0[:, u // 2, :, :].rearrange("p x y -> p (x y)").unsqueeze(1)
                                        .to_broadcast([128, 8, WIN]), ALU.add).then_inc(sa_add, 1)
                    if A is not None and n % 2 == 0:
                        v.wait_ge(sa_add, A.j * AU + (u + 1))
                        v.tensor_reduce(mxa[:, b, :], pa[:, b, :, :], AX.X, ALU.max).then_inc(sa_max, 1)
                    if Bm is not None and n % 2 == 0:
                        reciprocal_b(n)
                    if A is not None and n % 2 == 0:
                        v.wait_ge(sa_max, A.j * AU + (u + 1))
                        v.tensor_tensor(pa[:, b, :, :], pa[:, b, :, :],
                                        mxa[:, b, :].unsqueeze(2).to_broadcast([128, 8, WIN]),
                                        ALU.subtract).then_inc(sa_sub, 1)
                    if M is not None and n == 5:
                        v.wait_ge(m_hi, M.j + 1)
                        v.tensor_tensor(t1l[:, :], pM[:, 0:TOK], t1h[:, :].bitcast(f32),
                                        ALU.subtract).then_inc(m_lo, 1)
                    if A is not None and n % 2 == 1:
                        u = n // 2
                        b = u % 2
                        v.wait_ge(sa_exp, A.j * AU + (u + 1))
                        v.tensor_reduce(sma[:, b, :], pa[:, b, :, :], AX.X, ALU.add).then_inc(sa_sum, 1)
                    if Bm is not None and n % 2 == 1:
                        reciprocal_b(n)
                    if R is not None and n == 5:
                        v.wait_ge(r_t, R.j + 1)
                        for s in range(2):
                            last = v.bn_stats(st2[:, s, :], t2[:, s, :])
                        last.then_inc(r_st, 1)
                        v.wait_ge(r_st, R.j + 1)
                        v.tensor_scalar(res2[:, R.cols(TOK)], t2[:, :, :].rearrange("p s c -> p (s c)"),
                                        1.0, None, ALU.mult)
                        for s in range(2):
                            last = v.bn_aggr(mv2[:, s, :], st2[:, s, :])
                        last.then_inc(r_ag, 1)
                        v.wait_ge(r_ag, R.j + 1)
                        v.tensor_scalar(rs2[:, :], mv2[:, :, 1], EPS, None, ALU.add).then_inc(r_eps, 1)
                    if A is not None and n % 2 == 1:
                        v.wait_ge(sa_sum, A.j * AU + (u + 1))
                        wait(v, sa_nrm, A.j * AU + (u - 1))
                        v.reciprocal(rca[:, b, :], sma[:, b, :]).then_inc(sa_rcp, 1)

            def choose(part):
                t, n = tiles(part), part + 1
                full = [128, t.stop - t.start, E]
                for k in range(t.start, t.stop):
                    last = v.max(mx8[:, k, :], logit[:, k, :])
                last.then_inc(q_max, 1)
                v.wait_ge(q_max, n)
                v.tensor_tensor(rdel[:, t, :], mx8[:, t, 1:2], mx8[:, t, 0:1], ALU.subtract).then_inc(q_d, 1)
                for k in range(t.start, t.stop):
                    last = v.max_index(ix8[:, k, :], mx8[:, k, :], logit[:, k, :])
                last.then_inc(q_ix, 1)
                v.wait_ge(q_ix, n)
                v.tensor_copy(ixf[:, t, :], ix8[:, t, :]).then_inc(q_ixf, 1)
                v.wait_ge(q_exp, n)
                v.tensor_scalar(rden[:, t, :], rexp[:, t, :], 1.0, None, ALU.add).then_inc(q_den, 1)
                v.wait_ge(q_ixf, n)
                v.tensor_tensor(cwa[:, t, :], iota[:, :].unsqueeze(1).to_broadcast(full),
                                ixf[:, t, 0:1].to_broadcast(full), ALU.is_equal).then_inc(q_a, 1)
                v.wait_ge(q_den, n)
                v.reciprocal(wt1[:, t, :], rden[:, t, :]).then_inc(q_w1, 1)
                v.tensor_tensor(cwb[:, t, :], iota[:, :].unsqueeze(1).to_broadcast(full),
                                ixf[:, t, 1:2].to_broadcast(full), ALU.is_equal).then_inc(q_b, 1)
                v.wait_ge(q_w1, n)
                v.tensor_tensor(wt2[:, t, :], rexp[:, t, :], wt1[:, t, :], ALU.mult).then_inc(q_w2, 1)
                v.wait_ge(q_a, n)
                v.tensor_tensor(cwa[:, t, :], cwa[:, t, :], wt1[:, t, :].to_broadcast(full), ALU.mult).then_inc(q_am, 1)
                v.wait_ge(q_b, n)
                v.wait_ge(q_w2, n)
                v.tensor_tensor(cwb[:, t, :], cwb[:, t, :], wt2[:, t, :].to_broadcast(full), ALU.mult).then_inc(q_bm, 1)
                v.wait_ge(q_am, n)
                v.wait_ge(q_bm, n)
                v.tensor_tensor(cws[:, t, :], cwa[:, t, :], cwb[:, t, :], ALU.add).then_inc(q_cw, 1)

            def weights_low(g, bank):
                v.wait_ge(ct_hi, g + 1)
                v.tensor_tensor(cwt[32:32 + E, g * GRP:(g + 1) * GRP], bank[0:E, :],
                                cwt[0:E, g * GRP:(g + 1) * GRP].bitcast(f32), ALU.subtract).then_inc(ct_lo, 1)

            def after(i):
                if i == -1:
                    v.wait_ge(c_w1h, 1)
                    v.tensor_tensor(w1l[:, :], w1s, w1h[:, :].bitcast(f32), ALU.subtract).then_inc(c_w1l, 1)
                    group_variance(GN_PARTS[1], 2)
                if i == B:
                    v.wait_ge(m_v, B)
                    v.memset(f2bst[:, :].bitcast(f32), 0.0).then_inc(c_b2z, 1)
                    w = 2 * NFC * 128 // 4
                    for q in range(4):
                        v.wait_ge(c_f1h, q + 1)
                        v.tensor_tensor(f1l[:, q * w:(q + 1) * w], f1s[:, q * w:(q + 1) * w],
                                        f1h[:, q * w:(q + 1) * w].bitcast(f32), ALU.subtract).then_inc(c_f1l, 1)
                    v.wait_ge(c_tgh, 1)
                    v.tensor_tensor(tgl[0][:, :], tnx[:, 0:GRP], tgh[0][:, :].bitcast(f32),
                                    ALU.subtract).then_inc(c_tgl, 1)
                    v.wait_ge(c_b2h, 1)
                    v.tensor_tensor(f2bst[64:64 + E, :], f2bs[64:64 + E, :], f2bst[64:64 + E, :].bitcast(f32),
                                    ALU.subtract).then_inc(c_b2l, 1)
                if i == B + 1:
                    v.wait_ge(r_lgev, EARLY)
                    choose(0)
                if i == B + 2:
                    for g in range(EARLY // 2):
                        weights_low(g, (pG, pTA)[g % 2])

            pipeline(v, iteration, after)

            v.wait_ge(r_lgev, B)
            choose(1)

            def group(g, gh, par, main):
                first = isinstance(g, int) and g == 0
                for c in range(16 if main else 7):
                    if main:
                        i1, i2 = pieces(c)
                        v.wait_ge(e_h2, g * 16 + (c + 1))
                        v.wait_ge(e_sil, g * 16 + (c + 1))
                        v.scalar_tensor_tensor(gat[:, c % 4, :], (pTA, pTB)[c % 2][:, :], f1bs[:, i2:i2 + 1],
                                               sil[:, c % 2, :], ALU.add, ALU.mult).then_inc(e_gat, 1)
                    if (main and c > 0) or (c == 0 and not first):
                        k = (c - 1) % 16
                        v.wait_ge(e_gat, g * 16 + c)
                        v.wait_ge(e_cw, g * 8 + (c + 1) // 2)
                        wait(v, e_alo, g * 16 + (c - 4))
                        v.tensor_tensor(act[:, k % 4, :], gat[:, k % 4, :], (pG, pM)[(k // 2) % 2][:, :],
                                        ALU.mult).then_inc(e_act, 1)
                    if first and c in (1, 3):
                        h = slice((c // 2) * NFC // 2, (c // 2 + 1) * NFC // 2)
                        v.wait_ge(c_f2h, c // 2 + 1)
                        v.tensor_tensor(f2l[:, h, :], f2s[:, h, :], f2h[:, h, :].bitcast(f32),
                                        ALU.subtract).then_inc(c_f2l, 1)
                    if first and c in (10, 14):
                        weights_low(EARLY // 2 + (c - 10) // 4, pOB)
                    if c == 6 and not first:
                        v.wait_ge(y_T, g)
                        if not (isinstance(g, int) and g < 3):
                            v.wait_ge(y_dma[1 - par], (gh - 1 + par) * 16)
                        v.tensor_tensor(yo[:, 1 - par, :], (pOA, pOB)[1 - par][:, :],
                                        res2[:, bass.ds(g * GRP - GRP, GRP)], ALU.add).then_inc(y_add, 1)
                    if c == 9 and main and not (isinstance(g, int) and g == NGRP - 1):
                        v.wait_ge(c_tgh, g + 2)
                        v.tensor_tensor(tgl[1 - par][:, :], tnx[:, bass.ds(g * GRP + GRP, GRP)],
                                        tgh[1 - par][:, :].bitcast(f32), ALU.subtract).then_inc(c_tgl, 1)

            ffn(v, group)

        @block.tensor
        def _(pe):
            def split_product(out_, wh, wl, xh, xl):
                pe.matmul(out_, wh, xh, start=True, stop=False)
                pe.matmul(out_, wl, xh, start=False, stop=False)
                return pe.matmul(out_, wh, xl, start=False, stop=True)

            def group_means(part):
                images = GN_PARTS[part]
                pe.wait_ge(gn_e2, part + 1)
                pe.matmul(pOB[:, 2 * images.start:2 * images.stop], gmat[:, :],
                          gmv[:, images.start:images.stop, :].rearrange("p b t -> p (b t)"),
                          start=True, stop=True).then_inc(gn_mm, 1)

            pe.wait_ge(d_gm, 16)
            group_means(0)

            def iteration(X, G, A, M, Bm, R, L):
                def keys_or_queries(n):
                    if n == 0:
                        pe.wait_ge(x_l, G.j + 1)
                        if isinstance(G.j, int) and G.j == 0:
                            pe.wait_ge(c_w0l, 1)
                        if isinstance(G.j, int) and G.j == 1:
                            pe.wait_ge(gn_cp, 1)
                            group_means(1)
                    wait(pe, g_ev, projection_read(G, chunk_use(n)))
                    c = NCH + n if n < NCH else n - NCH
                    split_product(projection(G, chunk_use(n))[:, 0:TOK], w0h[:, c * 128:(c + 1) * 128], w0l[:, c * 128:(c + 1) * 128],
                                  xnh[:, G.par, :], xnl[:, G.par, :]).then_inc(g_mm, 1)

                for n in range(8):
                    if Bm is not None:
                        if n == 0:
                            pe.wait_ge(m_qlo, Bm.j + 1)
                            pe.wait_ge(k1_dma[Bm.par], Bm.half * 128 + 128)
                        wait(pe, sb_exp, Bm.j * BU + (n - 1))
                        if A is not None and n % 2 == 1:
                            pe.wait_ge(sa_add, A.j * AU + (n // 2 + 1))
                        for qc in range(2):
                            for part in range(2):
                                mm = pe.matmul((pSB, pSA)[n % 2][:, qc * TOK:(qc + 1) * TOK],
                                               q1[:, Bm.par, n // 4, qc * 128:(qc + 1) * 128],
                                               kbd1[Bm.par][:, part, n // 4, n % 4, :],
                                               start=(part == 0), stop=(part == 1))
                        mm.then_inc(sb_mm, 1)
                    if A is not None and n % 2 == 0:
                        u = n // 2
                        pr, hf = u // 2, u % 2
                        if u == 0:
                            pe.wait_ge(g_ev, A.j * GU + (chunk_use(2 * NCH - 1) + 1))
                            pe.wait_ge(k0_dma[A.par], A.half * 64 + 64)
                        wait(pe, sa_add, A.j * AU + u)
                        if Bm is not None:
                            wait(pe, sb_exp, Bm.j * BU + n)
                        for cc in range(2):
                            for w in range(2):
                                t = 128 * pr + WIN * w
                                mm = pe.matmul(pSA[WIN * w:WIN * w + WIN, cc * TOK:(cc + 1) * TOK],
                                               q0[:, A.par, 2 * hf + cc, t:t + WIN],
                                               kbd0[A.par][:, 2 * hf + cc, :, t:t + WIN], start=True, stop=True)
                        mm.then_inc(sa_mm, 1)
                    if G is not None and n % 2 == 1:
                        keys_or_queries(n)
                    for J, k in steps_back(Bm, R, n, 2):
                        wait(pe, sb_nrm, J.j * BU + (k + 1))
                        wait(pe, tb_ev, J.j * BU + k)
                        for kc in range(2):
                            for qc in range(2):
                                mm = pe.transpose(pTB[:, kc * TOK + qc * 128:kc * TOK + (qc + 1) * 128],
                                                  pb[:, k % PBUFS, qc, kc * 128:(kc + 1) * 128], ident[:, :])
                        mm.then_inc(tb_mm, 1)
                    if R is not None and n == 4:
                        pe.wait_ge(ob_ev, R.j + 1)
                        if A is not None:
                            pe.wait_ge(oa_ev, A.j * AU + 1)
                        else:
                            pe.wait_ge(oa_ev, B * AU)
                            pe.wait_ge(r_x, R.j)
                        for s in range(2):
                            for g in range(2):
                                mm = pe.matmul(pOA[:, s * C:(s + 1) * C], o1[:, g, s * 128:(s + 1) * 128],
                                               wo1s[:, g, :], start=(g == 0), stop=(g == 1))
                        mm.then_inc(r_o, 1)
                    if G is not None and n % 2 == 0:
                        keys_or_queries(n)
                    for J, k in steps_back(Bm, R, n, 3):
                        wait(pe, tb_ev, J.j * BU + (k + 1))
                        if k == 0:
                            if isinstance(J.j, int) and J.j == 0:
                                pe.wait_ge(gn_cp, 2)
                                pe.wait_ge(d_c0, C0_DMAS)
                            wait(pe, ob_ev, J.j)
                            wait(pe, m_vev, J.j + 1)
                        r, g = D1 * 2 * (k % 4), k // 4
                        for kc in range(2):
                            mm = pe.matmul(pOB[r:r + PAD1, g * TOK:(g + 1) * TOK],
                                           v1[:, J.par, kc, k * PAD1:(k + 1) * PAD1], ptb[:, k % 2, kc, :],
                                           start=(kc == 0), stop=(kc == 1))
                        mm.then_inc(ob_mm, 1)
                    for J, u in applied(A, M, n):
                        if u == 0:
                            pe.wait_ge(g_ev, J.j * GU + GU)
                        wait(pe, ta_ev, J.j * AU + (u + 1))
                        wait(pe, oa_ev, J.j * AU + u)
                        if R is not None and n == 5:
                            pe.wait_ge(r_t, R.j + 1)
                        if R is not None and n == 7:
                            pe.wait_ge(r_x, R.j + 1)
                        pr, hf = u // 2, u % 2
                        for w in range(2):
                            for jj in range(4):
                                mm = pe.matmul(pOA[WIN * (jj % 2):WIN * (jj % 2) + WIN,
                                                   (2 * w + jj // 2) * 128:(2 * w + jj // 2 + 1) * 128],
                                               v0[:, J.par, 2 * pr + w, 4 * hf + jj, :, :].rearrange("p a d -> p (a d)"),
                                               pta[:, u % 2, jj * 128:(jj + 1) * 128], start=True, stop=True)
                        mm.then_inc(oa_mm, 1)
                    for J, u in turned(A, M, n):
                        wait(pe, sa_nrm, J.j * AU + (u + 1))
                        wait(pe, ta_ev, J.j * AU + u)
                        for jj in range(4):
                            mm = pe.transpose(pTA[:, jj * 128:(jj + 1) * 128],
                                              pa[:, u % 2, 2 * jj:2 * jj + 2, :].rearrange("p h k -> p (h k)"),
                                              ident[:, :])
                        mm.then_inc(ta_mm, 1)
                    if M is not None and n == 2:
                        pe.wait_ge(oa_ev, M.j * AU + AU)
                        if L is not None:
                            pe.wait_ge(r_lgev, L.j + 1)
                        else:
                            wait(pe, m_vev, M.j)
                        for s in range(2):
                            for c in range(NCH):
                                mm = pe.matmul(pM[:, s * C:(s + 1) * C], o0[:, c, s * 128:(s + 1) * 128],
                                               wo0s[:, c, :], start=(c == 0), stop=(c == NCH - 1))
                        mm.then_inc(m_o, 1)
                    if M is not None and n == 4:
                        pe.wait_ge(m_tn, M.j + 1)
                        for s in range(2):
                            mm = pe.transpose(pM[:, s * 128:(s + 1) * 128], tn1[:, s, :], ident[:, :])
                        mm.then_inc(m_T, 1)
                    if M is not None and n in (5, 6):
                        if n == 5:
                            pe.wait_ge(m_lo, M.j + 1)
                            if isinstance(M.j, int) and M.j == 0:
                                pe.wait_ge(c_w1l, 1)
                        else:
                            pe.wait_ge(m_klo, M.j + 1)
                        for g in range(2):
                            c = (QK1 if n == 5 else 0) + g * 128
                            mm = split_product(pM[:, g * TOK:(g + 1) * TOK], w1h[:, c:c + 128], w1l[:, c:c + 128],
                                               t1h[:, :], t1l[:, :])
                        mm.then_inc(m_k if n == 5 else m_q, 1)
                    if M is not None and n == 7:
                        pe.wait_ge(m_qlo, M.j + 1)
                        for s in range(2):
                            mm = split_product(pM[:, s * TOK:(s + 1) * TOK], t1h[:, s * 128:(s + 1) * 128],
                                               t1l[:, s * 128:(s + 1) * 128], w1h[:, 2 * QK1:], w1l[:, 2 * QK1:])
                        mm.then_inc(m_v, 1)
                    if R is not None and n == 6:
                        pe.wait_ge(r_tn, R.j + 1)
                        if A is not None:
                            pe.wait_ge(oa_ev, A.j * AU + 2)
                        for s in range(2):
                            mm = pe.transpose(pOA[:, s * 128:(s + 1) * 128], tn2[:, s, :], ident[:, :])
                        mm.then_inc(r_T, 1)
                    if G is not None and n % NCH == NCH - 1:
                        pr = n // NCH
                        if isinstance(G.j, int) and G.j == 0:
                            pe.wait_ge(c_wvl, 1)
                        pe.wait_ge(g_ev, projection_read(G, value_use(pr)))
                        split_product(projection(G, value_use(pr))[:, :], xnh[:, G.par, pr * 128:(pr + 1) * 128],
                                      xnl[:, G.par, pr * 128:(pr + 1) * 128], wvh[:, :], wvl[:, :]).then_inc(g_mm, 1)
                    if L is not None and n == 1:
                        pe.wait_ge(r_f, L.j + 1)
                        if Bm is not None:
                            pe.wait_ge(m_vev, Bm.j + 1)
                        else:
                            wait(pe, r_lgev, L.j)
                        for s in range(2):
                            mm = pe.matmul(pM[:, s * E:(s + 1) * E], t2f[:, s * 128:(s + 1) * 128], rws[:, :],
                                           start=True, stop=True)
                        mm.then_inc(r_lg, 1)

            def turn_weights(g, bank):
                for s in range(GRP // 128):
                    mm = pe.transpose(bank[0:E, s * 128:(s + 1) * 128], cws[:, g * 4 + s, :], ident[:, :])
                mm.then_inc(ct_mm, 1)

            def after(i):
                if i == B + 2:
                    pe.wait_ge(q_cw, 1)
                    pe.wait_ge(g_ev, B * GU)
                    pe.wait_ge(ta_ev, B * AU)
                    for g in range(EARLY // 2):
                        if g >= 2:
                            pe.wait_ge(ct_lo, g - 1)
                        turn_weights(g, (pG, pTA)[g % 2])

            pipeline(pe, iteration, after)

            pe.wait_ge(r_lgev, B)
            pe.wait_ge(c_tgl, 1)
            pe.wait_ge(c_b2l, 1)
            pe.wait_ge(c_sel, 1)
            pe.wait_ge(ct_lo, EARLY // 2)

            def group(g, gh, par, main):
                first = isinstance(g, int) and g == 0
                for c in range(16 if main else 6):
                    if main:
                        if c % 2 == 0:
                            wait(pe, e_act, g * 16 + (c - 2))
                            pe.matmul((pG, pM)[(c // 2) % 2][:, :], sel[:, c // 2, :], cwt[:, bass.ds(g * GRP, GRP)],
                                      start=True, stop=True).then_inc(e_cw, 1)
                        if c == 0:
                            pe.wait_ge(c_tgl, g + 1)
                        if first and c % 4 == 0:
                            pe.wait_ge(c_f1l, c // 4 + 1)
                        i1, i2 = pieces(c)
                        wait(pe, e_sil, g * 16 + (c - 1))
                        split_product((pSA, pSB)[c % 2][:, :], f1h[:, i1 * 128:(i1 + 1) * 128],
                                      f1l[:, i1 * 128:(i1 + 1) * 128], tgh[par][:, :], tgl[par][:, :])\
                            .then_inc(e_h1, 1)
                        wait(pe, e_gat, g * 16 + (c - 1))
                        split_product((pTA, pTB)[c % 2][:, :], f1h[:, i2 * 128:(i2 + 1) * 128],
                                      f1l[:, i2 * 128:(i2 + 1) * 128], tgh[par][:, :], tgl[par][:, :])\
                            .then_inc(e_h2, 1)
                    if (main and c >= 4) or (c < 4 and not first):
                        k = (c - 4) % 16
                        y = (pOA, pOB)[par if c >= 4 else 1 - par]
                        pe.wait_ge(e_alo, g * 16 + (c - 3))
                        if first and k in (0, 8):
                            pe.wait_ge(c_f2l, k // 8 + 1)
                        if k == 0:
                            wait(pe, y_add, g - 1)
                            if isinstance(g, int) and g == 1:
                                pe.wait_ge(ct_lo, NGRP)
                            pe.matmul(y[:, :], f2bst[:, :], cwt[:, bass.ds(g * GRP, GRP)], start=True, stop=False)
                        pe.matmul(y[:, :], f2h[:, k, :], acth[:, k % 4, :], start=False, stop=False)
                        pe.matmul(y[:, :], f2l[:, k, :], acth[:, k % 4, :], start=False, stop=False)
                        pe.matmul(y[:, :], f2h[:, k, :], actl[:, k % 4, :], start=False, stop=(k == 15))\
                            .then_inc(e_y, 1)
                    if first and c in (8, 12):
                        if c == 8:
                            pe.wait_ge(q_cw, 2)
                        else:
                            pe.wait_ge(ct_lo, EARLY // 2 + 1)
                        turn_weights(EARLY // 2 + (c - 8) // 4, pOB)
                    if c == 5 and not first:
                        pe.wait_ge(y_ev, g)
                        for s in range(GRP // 128):
                            mm = pe.transpose((pOA, pOB)[1 - par][:, s * 128:(s + 1) * 128],
                                              yt[:, s * 128:(s + 1) * 128], ident[:, :])
                        mm.then_inc(y_T, 1)

            ffn(pe, group)


def kernel(x, L0_conv_w_qkv, L0_conv_pos_embedding, L0_conv_w_out, L0_conv_b_out, L1_attn_w_qkv, L1_attn_b_qkv,
           L1_attn_w_out, L1_attn_b_out, L1_ffn_router_w, L1_ffn_router_b, L1_ffn_fc1_w, L1_ffn_fc1_b,
           L1_ffn_fc2_w, L1_ffn_fc2_b):
    import concourse.bacc as bacc
    from concourse.bass_utils import run_bass_kernel_spmd

    def host(a):
        return np.asarray(a)

    xr = np.roll(host(x), (-4, -4), axis=(1, 2))
    xw = xr.reshape(B, 2, 8, 2, 8, C).transpose(0, 1, 3, 2, 4, 5).reshape(NTOK, C)

    q = np.arange(WIN)
    ul = (q[:, None] >= 32) != (q[None, :] >= 32)
    lr = (q[:, None] % 8 >= 4) != (q[None, :] % 8 >= 4)
    mask = np.zeros((128, 2, WIN), np.float32)
    mask[WIN:, 0][lr] = -1e30
    mask[:WIN, 1][ul] = -1e30
    mask[WIN:, 1][ul | lr] = -1e30

    eye = np.eye(128, dtype=np.float32)
    gmat = np.kron(np.eye(32), np.full((4, 4), 0.25)).astype(np.float32)
    sel = np.zeros((128, E, 128), np.float32)
    for e in range(E):
        sel[[e, 32 + e], e, :] = 1.0
    iota = np.tile(np.arange(E, dtype=np.float32), (128, 1))

    def padded(a):
        a = a.reshape((H1, D1) + a.shape[1:])
        return np.concatenate([a, np.zeros_like(a)], axis=1).reshape((H1 * PAD1,) + a.shape[2:])

    w1 = host(L1_attn_w_qkv)
    bq = host(L1_attn_b_qkv)
    def twice(a):
        a = a.reshape(a.shape[:-1] + (2, 1, 64))
        return np.concatenate([a, a], axis=-2).reshape(a.shape[:-3] + (QK1,))

    arrays = {
        "x_tok": xw,
        "x_ch": xw.T,
        "w0": host(L0_conv_w_qkv).T,
        "wo0": host(L0_conv_w_out).T,
        "bo0": np.stack([host(L0_conv_b_out)] * 2),
        "pos": host(L0_conv_pos_embedding)[:, ::-1],
        "mask": mask.reshape(128, 2 * WIN),
        "ident": eye,
        "gmat": gmat,
        "sel": sel.reshape(128, E * 128),
        "iota": iota,
        "w1": np.concatenate([twice(w1[:, :C]), twice(w1[:, C:2 * C]), padded(w1[:, 2 * C:].T).T], axis=1),
        "bq1": twice(bq[0:C]).reshape(2, C).T,
        "bk1": twice(bq[C:2 * C]).reshape(2, C).T,
        "bv1": padded(bq[2 * C:]).reshape(2, 128).T,
        "wo1": padded(host(L1_attn_w_out)),
        "bo1": np.stack([host(L1_attn_b_out)] * 2),
        "rw": host(L1_ffn_router_w).T,
        "rb": np.stack([host(L1_ffn_router_b)] * 2),
        "f1": host(L1_ffn_fc1_w).reshape(2 * NFC * 128, C).T,
        "f1b": host(L1_ffn_fc1_b).reshape(2 * NFC, 128).T,
        "f2": host(L1_ffn_fc2_w).reshape(E, C, 2, 128).transpose(3, 0, 2, 1).reshape(128, NFC * C),
        "f2b": host(L1_ffn_fc2_b),
    }
    arrays = {n + "_dram": np.ascontiguousarray(a) for n, a in arrays.items()}

    nc = bacc.Bacc("TRN2", target_bir_lowering=False, num_devices=1)
    args = [nc.dram_tensor(n, a.shape, mybir.dt.from_np(a.dtype), kind="ExternalInput").ap()
            for n, a in arrays.items()]
    out = nc.dram_tensor("out_dram", (NTOK, C), mybir.dt.float32, kind="ExternalOutput").ap()
    hybrid_kernel(nc, *args, out)
    y = run_bass_kernel_spmd(nc, [arrays], core_ids=[0]).results[0]["out_dram"]
    y = y.reshape(B, 2, 2, 8, 8, C).transpose(0, 1, 3, 2, 4, 5).reshape(B, 16, 16, C)
    return np.roll(y, (4, 4), axis=(1, 2))
```

```python
import numpy as np
import concourse.bass as bass
from concourse import mybir
from contextlib import ExitStack

B, C = 16, 128
TOK = 256
NTOK = B * TOK
H0, D0 = 16, 32
NCH = H0 * D0 // 128
WIN = 64
NWIN = TOK // WIN
H1, D1 = 8, 16
PAD1 = 32
QK1 = 2 * C
W1COLS = 2 * QK1 + H1 * PAD1
E, HID, TOPK = 8, 256, 2
NFC = E * HID // 128
GRP = 512
NGRP = NTOK // GRP
PBUFS = 4
AU, BU = 4, 8
GU = 10
SCALE0 = D0 ** -0.5
SCALE1 = C ** -0.5
EPS = 1e-5
LOOP_FROM, LOOP_TO = 4, 14
C0_DMAS, C1_DMAS, F_DMAS = 3 * 16, 8 * 16, 5 * 16
GN_FIRST = B // 4
EARLY = 8
LAST_STEPS = 3


class Image:

    def __init__(self, j, half, par):
        self.j, self.half, self.par = j, half, par

    def cols(self, width):
        return bass.ds(self.j * width, width)


def wait(eng, sem, value):
    if isinstance(value, int) and value <= 0:
        return
    eng.wait_ge(sem, value)


def chunk_use(n):
    return n + n // NCH


def value_use(pr):
    return (NCH + 1) * pr + NCH


def steps_back(J, prev, n, back):
    k = n - back
    if k >= 0:
        return [] if J is None else [(J, k)]
    return [] if prev is None else [(prev, k + BU)]


def turned(J, prev, n):
    if n % 2:
        return []
    u = n // 2 - 1
    return [(x, u % AU) for x in ((J if u >= 0 else prev),) if x is not None]


def applied(J, prev, n):
    return turned(J, prev, n - 1) if n % 2 else []


def collected(J, prev, n):
    if n % 2:
        return []
    return applied(J, prev, n - 1) if n else ([] if prev is None else [(prev, 2)])


def values_made(G, A, n):
    if n % NCH:
        return []
    return [(x, (n // NCH - 1) % 2) for x in ((G if n else A),) if x is not None]


def hybrid_kernel(nc, x_tok, x_ch, w0, wo0, bo0, pos, mask, ident_d, gmat_d, sel_d, iota_d,
                  w1, bq1, bk1, bv1, wo1, bo1, rw, rb, f1, f1b, f2, f2b, out):
    f32, f32r, u32 = mybir.dt.float32, mybir.dt.float32r, mybir.dt.uint32
    ALU, ACT, AX = mybir.AluOpType, mybir.ActivationFunctionType, mybir.AxisListType

    ctx = ExitStack()
    with ctx:
        def sb(name, shape, dt=f32):
            return ctx.enter_context(nc.sbuf_tensor(name, shape, dt))

        def sem(name):
            return ctx.enter_context(nc.semaphore(name))

        def sem2(name):
            return [sem(f"{name}{p}") for p in range(2)]

        ident = sb("ident", [128, 128])
        gmat = sb("gmat", [128, 128])
        posr = sb("posr", [128, 8, 8])
        masks = sb("masks", [128, 2, 8, 8])
        bias0 = sb("bias0", [128, 2, 8, 8])
        half = sb("half", [128, B])
        wo0s = sb("wo0s", [128, NCH, C])
        bo0s = sb("bo0s", [128, 2, C])
        wo1s = sb("wo1s", [128, 2, C])
        bo1s = sb("bo1s", [128, 2, C])
        bq1s = sb("bq1s", [C, 2])
        bq1x = sb("bq1x", [C, 2])
        bk1s = sb("bk1s", [C, 2])
        bv1s = sb("bv1s", [128, 2])
        rws = sb("rws", [C, E])
        rbs = sb("rbs", [128, 2, E])
        xch = sb("xch", [C, NTOK])
        res2 = xch
        tnx = sb("tnx", [C, NTOK])
        logit = sb("logit", [128, 2 * B, E])
        f1bs = sb("f1bs", [128, 2 * NFC])
        f2bs = sb("f2bs", [128, C])
        iota = sb("iota", [128, E])
        o1 = sb("o1", [128, 2, TOK])
        t1b = sb("t1b", [128, 2, 2, C])
        t2 = sb("t2", [128, 2, C])
        st2, mv2, rs2, tn2 = sb("st2", [128, 2, 6]), sb("mv2", [128, 2, 2]), sb("rs2", [128, 2]), sb("tn2", [128, 2, C])
        t2f = sb("t2f", [C, TOK])

        with ExitStack() as first:
            def sf(name, shape):
                return first.enter_context(nc.sbuf_tensor(name, shape, f32))

            kbd0 = [sf(f"kbd0_{p}", [128, NCH, 4, TOK]) for p in range(2)]
            q0 = sf("q0", [128, 2, NCH, TOK])
            v0 = sf("v0", [128, 2, NWIN, H0 // 2, 2, D0])
        f1s = sb("f1s", [C, 2 * NFC * 128])
        f1h = sb("f1h", [C, 2 * NFC * 128], f32r)
        f2s = sb("f2s", [128, NFC, C])
        f1l = sb("f1l", [C, 2 * NFC * 128], f32r)
        wvs = q0[:, 0, 0:2, :].rearrange("p a b -> p (a b)")
        w1s = q0[:, 1, 0:3, :].rearrange("p a b -> p (a b)")

        attention = ctx.enter_context(ExitStack())

        def sa_(name, shape, dt=f32):
            return attention.enter_context(nc.sbuf_tensor(name, shape, dt))

        w0h = sa_("w0h", [C, 2 * NCH * 128], f32r)
        w0l = sa_("w0l", [C, 2 * NCH * 128], f32r)
        wvh = sa_("wvh", [C, H0 * D0], f32r)
        wvl = sa_("wvl", [C, H0 * D0], f32r)
        w1h = sa_("w1h", [C, W1COLS], f32r)
        w1l = sa_("w1l", [C, W1COLS], f32r)
        gst = sa_("gst", [C, B, 6])
        gmv = sa_("gmv", [C, B, 2])
        gsum = sa_("gsum", [C, B, 2])
        gsq = sa_("gsq", [C, B])
        grs = sa_("grs", [C, B])
        st1, mv1, rs1 = sa_("st1", [128, 2, 6]), sa_("mv1", [128, 2, 2]), sa_("rs1", [128, 2])
        tn1 = sa_("tn1", [128, 2, C])
        xns = sa_("xns", [C, TOK])
        xnh = sa_("xnh", [C, 2, TOK], f32r)
        xnl = sa_("xnl", [C, 2, TOK], f32r)
        kst0 = sa_("kst0", [128, NCH, TOK])
        o0 = sa_("o0", [128, NCH, TOK])
        w0s = o0[:, :, :].rearrange("p a b -> p (a b)")
        xt = sa_("xt", [128, 2, 2, C])
        t1 = sa_("t1", [128, 2, C])
        t1h = sa_("t1h", [C, TOK], f32r)
        t1l = sa_("t1l", [C, TOK], f32r)
        q1 = sa_("q1", [128, 2, 2, TOK], f32r)
        kst1 = sa_("kst1", [128, 2, 2, TOK], f32r)
        kbd1 = [sa_(f"kbd1_{p}", [128, 2, 2, 4, TOK], f32r) for p in range(2)]
        v1 = sa_("v1", [128, 2, 2, H1 * PAD1])
        pa = sa_("pa", [128, 2, 8, WIN])
        mxa = sa_("mxa", [128, 2, 8])
        sma = sa_("sma", [128, 2, 8])
        rca = sa_("rca", [128, 2, 8])
        pta = sa_("pta", [128, 2, 512])
        pb = sa_("pb", [128, PBUFS, 2, TOK])
        mxb = sa_("mxb", [128, PBUFS, 2])
        smb = sa_("smb", [128, PBUFS, 2])
        rcb = sa_("rcb", [128, PBUFS, 2])
        ptb = sa_("ptb", [128, 2, 2, TOK])

        attention.close()
        sel = sb("sel", [128, E, 128], f32r)
        f2bst = sb("f2bst", [128, C], f32r)
        mx8 = sb("mx8", [128, 2 * B, 8])
        ix8 = sb("ix8", [128, 2 * B, 8], u32)
        ixf = sb("ixf", [128, 2 * B, 8])
        rdel = sb("rdel", [128, 2 * B, 1])
        rexp = sb("rexp", [128, 2 * B, 1])
        rden = sb("rden", [128, 2 * B, 1])
        wt1 = sb("wt1", [128, 2 * B, 1])
        wt2 = sb("wt2", [128, 2 * B, 1])
        cwa = sb("cwa", [128, 2 * B, E])
        cwb = sb("cwb", [128, 2 * B, E])
        cws = sb("cws", [128, 2 * B, E])
        cwt = sb("cwt", [128, NTOK], f32r)
        tgh, tgl = [sb("tgh0", [C, GRP], f32r)], [sb("tgl0", [C, GRP], f32r)]
        sels = sb("sels", [128, E, 128])
        tgh.append(sb("tgh1", [C, GRP], f32r))
        tgl.append(sb("tgl1", [C, GRP], f32r))
        f2h = sb("f2h", [128, NFC, C], f32r)
        f2l = sb("f2l", [128, NFC, C], f32r)
        sil = sb("sil", [128, 2, GRP])
        gat = sb("gat", [128, 4, GRP])
        act = sb("act", [128, 4, GRP])
        acth = sb("acth", [128, 4, GRP], f32r)
        actl = sb("actl", [128, 4, GRP], f32r)
        yt = sb("yt", [128, GRP])
        yo = sb("yo", [128, 2, GRP])

        def bank(name):
            return ctx.enter_context(nc.psum_tensor(name, [128, 512], f32))

        pG, pM, pSA, pSB, pTA, pTB, pOA, pOB = (bank(n) for n in ("pG", "pM", "pSA", "pSB", "pTA", "pTB", "pOA", "pOB"))

        d_x = [sem(f"d_x{n}") for n in range(4)]
        d_c0 = sem("d_c0")
        d_c1 = sem("d_c1")
        d_gm, d_w0, d_wv = sem("d_gm"), sem("d_w0"), sem("d_wv")
        d_mask = sem("d_mask")
        d_pos = sem("d_pos")
        d_f1, d_f2, d_f = sem("d_f1"), sem("d_f2"), sem("d_f")
        d_sel = sem("d_sel")
        z_half, z_kv, z_k1 = sem("z_half"), sem2("z_kv"), sem("z_k1")
        c_w0h, c_w0l, c_wvh, c_wvl, c_w1s, c_w1h, c_w1l, c_bq, c_bias = (
            sem(n) for n in ("c_w0h", "c_w0l", "c_wvh", "c_wvl", "c_w1s", "c_w1h", "c_w1l", "c_bq", "c_bias"))
        gn_st, gn_ag, gn_sq, gn_e2, gn_mm, gn_cp, gn_q, gn_v, gn_eps, gn_pow = (
            sem(n) for n in ("gn_st", "gn_ag", "gn_sq", "gn_e2", "gn_mm", "gn_cp", "gn_q", "gn_v", "gn_eps", "gn_pow"))
        x_c, x_s, x_h, x_l = sem("x_c"), sem("x_s"), sem("x_h"), sem("x_l")
        g_mm, g_ev = sem("g_mm"), sem("g_ev")
        k0_dma = [sem("k0_dma0"), sem("k0_dma1")]
        sa_mm, sa_add, sa_max, sa_sub, sa_exp, sa_sum, sa_rcp, sa_nrm = (
            sem(n) for n in ("sa_mm", "sa_add", "sa_max", "sa_sub", "sa_exp", "sa_sum", "sa_rcp", "sa_nrm"))
        ta_mm, ta_ev, oa_mm, oa_ev = (sem(n) for n in ("ta_mm", "ta_ev", "oa_mm", "oa_ev"))
        sb_mm, sb_max, sb_exp, sb_rcp, sb_nrm = (sem(n) for n in ("sb_mm", "sb_max", "sb_exp", "sb_rcp", "sb_nrm"))
        tb_mm, tb_ev, ob_mm, ob_ev = (sem(n) for n in ("tb_mm", "tb_ev", "ob_mm", "ob_ev"))
        xt_dma = [sem("xt_dma0"), sem("xt_dma1")]
        k1_dma = [sem("k1_dma0"), sem("k1_dma1")]
        m_xb, m_o, m_t, m_st, m_ag, m_eps, m_pow, m_tn, m_T, m_hi, m_lo, m_k, m_khi, m_klo, m_q, m_qhi, m_qlo = (
            sem(n) for n in ("m_xb", "m_o", "m_t", "m_st", "m_ag", "m_eps", "m_pow", "m_tn", "m_T", "m_hi", "m_lo",
                             "m_k", "m_khi", "m_klo", "m_q", "m_qhi", "m_qlo"))
        m_v, m_vev, m_tb = sem("m_v"), sem("m_vev"), sem("m_tb")
        r_o, r_t, r_st, r_ag, r_eps, r_pow, r_tn, r_T, r_f, r_x, r_lg, r_lgev = (
            sem(n) for n in ("r_o", "r_t", "r_st", "r_ag", "r_eps", "r_pow", "r_tn", "r_T", "r_f", "r_x",
                             "r_lg", "r_lgev"))
        c_f1h, c_f1l, c_tgh, c_tgl, c_sel, c_b2z, c_b2h, c_b2l, c_cwz, c_f2h, c_f2l = (
            sem(n) for n in ("c_f1h", "c_f1l", "c_tgh", "c_tgl", "c_sel", "c_b2z", "c_b2h", "c_b2l", "c_cwz",
                             "c_f2h", "c_f2l"))
        q_max, q_ix, q_ixf, q_d, q_exp, q_den, q_w1, q_w2, q_a, q_b, q_am, q_bm, q_cw = (
            sem(n) for n in ("q_max", "q_ix", "q_ixf", "q_d", "q_exp", "q_den", "q_w1", "q_w2", "q_a", "q_b",
                             "q_am", "q_bm", "q_cw"))
        ct_mm, ct_hi, ct_lo = sem("ct_mm"), sem("ct_hi"), sem("ct_lo")
        e_cw, e_h1, e_h2, e_sil, e_gat, e_act, e_ahi, e_alo, e_y = (
            sem(n) for n in ("e_cw", "e_h1", "e_h2", "e_sil", "e_gat", "e_act", "e_ahi", "e_alo", "e_y"))
        y_ev, y_T, y_add = sem("y_ev"), sem("y_T"), sem("y_add")
        y_dma = [sem("y_dma0"), sem("y_dma1")]

        out_v = out.rearrange("(g s p) c -> g p s c", s=GRP // 128, p=128)
        xt_v = x_tok.rearrange("(b s p) c -> p b s c", s=2, p=128)
        pos_t = pos.tensor
        w0v = w0[:, 2 * H0 * D0:3 * H0 * D0]

        LAGS = (2, 1, 0, -1, -2, -3, -4)

        def peeled(i):
            return [Image(i + lag, (i + lag) // 2, (i + lag) % 2) if 0 <= i + lag < B else None for lag in LAGS]

        def looped(it, p):
            first = LOOP_FROM + p
            return [Image(it * 2 + (first + lag), it + (first + lag) // 2, (first + lag) % 2) for lag in LAGS]

        def pipeline(eng, iteration, after=None):
            for i in range(-2, LOOP_FROM):
                iteration(*peeled(i))
                if after is not None:
                    after(i)
            with eng.Fori(0, (LOOP_TO - LOOP_FROM) // 2) as it:
                for p in range(2):
                    iteration(*looped(it, p))
            for i in range(LOOP_TO, B + 2):
                iteration(*peeled(i))
                if after is not None:
                    after(i)
            iteration(*peeled(B + 2), steps=range(LAST_STEPS))

        LATE_STEPS = [(B + 2, n) for n in range(LAST_STEPS, 8)] + [(B + 3, n) for n in range(3)]
        PE_AT, ACT_AT, DVE_AT, POOL_AT = ((0, 1, 2, 5, 5, 7, 7, 7), (0, 1, 2, 3, 6, 6, 6, 6), (0, 1, 2, 4, 8, 8, 8, 8),
                                          (0, 1, 2, 3, 4, 5, 6, 7))

        def beside(iteration, c, at):
            for (i, n), chunk in zip(LATE_STEPS, at):
                if chunk == c:
                    iteration(*peeled(i), steps=range(n, n + 1))

        def draining(A, M, Bm):
            if A is None and M is not None and M.j == B - 1:
                return 0
            return 1 if M is None and Bm is not None else None

        def ffn(eng, group):
            for g in range(3):
                group(g, g // 2, g % 2, True)
            with eng.Fori(0, (NGRP - 4) // 2) as it:
                for p in range(2):
                    group(it * 2 + (3 + p), it + (3 + p) // 2, (3 + p) % 2, True)
            group(NGRP - 1, (NGRP - 1) // 2, (NGRP - 1) % 2, True)
            group(NGRP, NGRP // 2, NGRP % 2, False)

        def pieces(c):
            e, hc = c // 2, c % 2
            return (e * 4 + hc, e * 4 + 2 + hc)

        def tiles(part):
            return slice(0, 2 * EARLY) if part == 0 else slice(2 * EARLY, 2 * B)

        def last_alone(M, Bm, R):
            return M is None and Bm is None and R is not None

        def last_bank(M, Bm):
            return pOB if M is None and Bm is None else pOA

        def logit_bank(R):
            return pOB if R is None else pM

        def projection(J, use):
            return pM if isinstance(J.j, int) and J.j < 2 and use % 2 else pG

        def projection_read(J, use):
            return J.j * GU + use - (1 if isinstance(J.j, int) and J.j < 2 else 0)

        GN_PARTS = (range(0, GN_FIRST), range(GN_FIRST, B))

        block = ctx.enter_context(nc.Block())

        @block.sync
        def _(sp):
            sp.dma_start(xch[:, 0:NTOK // 4], x_ch[:, 0:NTOK // 4]).then_inc(d_x[0], 16)
            sp.dma_start(xch[:, NTOK // 4:NTOK // 2], x_ch[:, NTOK // 4:NTOK // 2]).then_inc(d_x[1], 16)
            sp.dma_start(masks[:, :, :, :], mask.rearrange("p (r x y) -> p r x y", r=2, x=8)).then_inc(d_mask, 16)
            for qx in range(8):
                for r in range(2):
                    p = r * WIN + qx * 8
                    sp.dma_start(posr[p:p + 8, :, :],
                                bass.AP(tensor=pos_t, offset=(7 - qx) * 15, ap=[[1, 8], [15, 8], [1, 8]]))\
                     .then_inc(d_pos, 16)
            sp.dma_start(xch[:, NTOK // 2:3 * NTOK // 4], x_ch[:, NTOK // 2:3 * NTOK // 4]).then_inc(d_x[2], 16)
            sp.dma_start(xch[:, 3 * NTOK // 4:NTOK], x_ch[:, 3 * NTOK // 4:NTOK]).then_inc(d_x[3], 16)
            sp.dma_start(ident[:, :], ident_d).then_inc(d_c0, 16)
            sp.dma_start(wo0s[:, :, :], wo0.rearrange("(j p) c -> p j c", p=128)).then_inc(d_c0, 16)
            sp.dma_start(bo0s[:, :, :], bo0.partition_broadcast(128)).then_inc(d_c0, 16)
            sp.dma_start(wo1s[:, :, :], wo1.rearrange("(g p) c -> p g c", p=128)).then_inc(d_c1, 16)
            sp.dma_start(bo1s[:, :, :], bo1.partition_broadcast(128)).then_inc(d_c1, 16)
            sp.dma_start(w1s, w1).then_inc(d_c1, 16)
            sp.dma_start(bq1s[:, :], bq1).then_inc(d_c1, 16)
            sp.dma_start(bk1s[:, :], bk1).then_inc(d_c1, 16)
            sp.dma_start(bv1s[:, :], bv1).then_inc(d_c1, 16)
            sp.dma_start(rws[:, :], rw).then_inc(d_c1, 16)
            sp.dma_start(rbs[:, :, :], rb.partition_broadcast(128)).then_inc(d_c1, 16)
            sp.dma_start(f1bs[:, :], f1b).then_inc(d_f, 16)
            sp.dma_start(f2bs[0:E, :], f2b).then_inc(d_f, 16)
            sp.dma_start(f2bs[32:32 + E, :], f2b).then_inc(d_f, 16)
            sp.dma_start(f2bs[64:64 + E, :], f2b).then_inc(d_f, 16)
            sp.dma_start(iota[:, :], iota_d).then_inc(d_f, 16)

            def iteration(X, G, A, M, Bm, R, L, steps=range(8)):
                if A is not None:
                    wait(sp, m_t, A.j - 1)
                if G is not None:
                    wait(sp, g_ev, G.j * GU + (chunk_use(NCH - 1) + 1))
                    if isinstance(G.j, int) and G.j < 2:
                        sp.wait_ge(z_kv[G.j], 1)
                    for h in range(4):
                        sp.dma_start(kbd0[G.par][32 * h:32 * h + 32, :, h, :],
                                     kst0[32 * h:32 * h + 32, :, :]).then_inc(k0_dma[G.par], 16)
                if A is not None:
                    sp.dma_start(xt[:, A.par, :, :],
                                 xt_v[:, bass.ds(A.j, 1), :, :].rearrange("p b s c -> p (b s) c"))\
                      .then_inc(xt_dma[A.par], 16)
                if M is not None:
                    wait(sp, m_klo, M.j + 1)
                    if isinstance(M.j, int) and M.j < 2:
                        sp.wait_ge(z_k1, M.j + 1)
                    for h in range(8):
                        rows = slice(D1 * h, D1 * h + D1)
                        sp.dma_start(kbd1[M.par][rows, :, :, h % 4, :].bitcast(f32), kst1[rows, :, :, :].bitcast(f32))\
                          .then_inc(k1_dma[M.par], 16)

            def after(i):
                if i == B - 1:
                    sp.wait_ge(sa_mm, (B - 1) * AU)
                    sp.dma_start(f1s[:, :], f1).then_inc(d_f1, 16)
                if i == B:
                    sp.wait_ge(sa_mm, B * AU)
                    sp.dma_start(f2s[:, :, :], f2.rearrange("p (j d) -> p j d", d=C)).then_inc(d_f2, 16)
                    sp.wait_ge(m_v, B)
                    sp.dma_start(sels[:, :, :], sel_d.rearrange("p (e c) -> p e c", e=E)).then_inc(d_sel, 16)

            pipeline(sp, iteration, after)

            for g in range(NGRP):
                sp.wait_ge(y_add, g + 1)
                sp.dma_start(out_v[g, :, :, :], yo[:, g % 2, :].rearrange("p (s c) -> p s c", c=C))\
                  .then_inc(y_dma[g % 2], 16)
            for p in range(2):
                sp.wait_ge(y_dma[p], 16 * NGRP // 2)

        @block.gpsimd
        def _(pool):
            pool.memset(half[:, :], -0.5).then_inc(z_half, 1)
            pool.wait_ge(z_half, 1)

            def group_roots(part):
                t = slice(GN_PARTS[part].start, GN_PARTS[part].stop)
                pool.wait_ge(gn_eps, part + 1)
                pool.tensor_tensor(grs[:, t], gsq[:, t], half[:, t], ALU.pow).then_inc(gn_pow, 1)
                pool.wait_ge(gn_pow, part + 1)

            group_roots(0)

            def iteration(X, G, A, M, Bm, R, L, steps=range(8)):
                if X is not None and isinstance(X.j, int) and X.j == GN_FIRST:
                    group_roots(1)
                if X is not None and isinstance(X.j, int) and X.j == 1:
                    pool.memset(kbd0[0][:, :, :, :], 0.0)
                    pool.memset(v0[:, 0, :, :, :, :], 0.0).then_inc(z_kv[0], 1)
                if X is not None and isinstance(X.j, int) and X.j in (2, 3):
                    pool.memset(kbd1[X.par][:, :, :, :, :].bitcast(f32), 0.0).then_inc(z_k1, 1)
                for n in steps:
                    if n == 0 and M is not None:
                        if isinstance(M.j, int) and M.j == 0:
                            pool.wait_ge(d_c0, C0_DMAS)
                        pool.wait_ge(xt_dma[M.par], M.half * 16 + 16)
                        pool.tensor_tensor(xt[:, M.par, :, :], xt[:, M.par, :, :], bo0s[:, :, :],
                                           ALU.add).then_inc(m_xb, 1)
                    if n == 4 and M is not None:
                        pool.wait_ge(m_eps, M.j + 1)
                        pool.tensor_tensor(rs1[:, :], rs1[:, :], half[:, 0:2], ALU.pow).then_inc(m_pow, 1)
                    if n == 5 and M is not None:
                        pool.wait_ge(m_t, M.j + 1)
                        wait(pool, r_t, M.j - 1)
                        pool.tensor_tensor(t1b[:, M.par, :, :], t1[:, :, :], bo1s[:, :, :], ALU.add).then_inc(m_tb, 1)
                    if n == 6 and R is not None:
                        pool.wait_ge(r_eps, R.j + 1)
                        pool.tensor_tensor(rs2[:, :], rs2[:, :], half[:, 0:2], ALU.pow).then_inc(r_pow, 1)
                    if Bm is not None:
                        b = n % PBUFS
                        pool.wait_ge(sb_rcp, Bm.j * BU + (n + 1))
                        pool.tensor_tensor(pb[:, b, :, :], pb[:, b, :, :],
                                           rcb[:, b, :].unsqueeze(2).to_broadcast([128, 2, TOK]),
                                           ALU.mult).then_inc(sb_nrm, 1)
                    if A is not None and n % 2 == 1:
                        u = n // 2
                        b = u % 2
                        pool.wait_ge(sa_rcp, A.j * AU + (u + 1))
                        pool.tensor_tensor(pa[:, b, :, :], pa[:, b, :, :],
                                           rca[:, b, :].unsqueeze(2).to_broadcast([128, 8, WIN]),
                                           ALU.mult).then_inc(sa_nrm, 1)
                    if X is not None and n == 0:
                        wait(pool, x_l, X.j)
                        pool.tensor_tensor(xns[:, :], xch[:, X.cols(TOK)],
                                           gsum[:, X.cols(1), 0].to_broadcast([C, TOK]),
                                           ALU.subtract).then_inc(x_c, 1)
                        pool.wait_ge(x_c, X.j + 1)
                        pool.tensor_tensor(xns[:, :], xns[:, :], grs[:, X.cols(1)].to_broadcast([C, TOK]),
                                           ALU.mult).then_inc(x_s, 1)
                    if X is not None and n == 4:
                        pool.wait_ge(x_h, X.j + 1)
                        pool.tensor_tensor(xnl[:, X.par, :], xns[:, :], xnh[:, X.par, :].bitcast(f32),
                                           ALU.subtract).then_inc(x_l, 1)
                    if draining(A, M, Bm) == 1 and n < 4:
                        pool.wait_ge(m_v, B)
                        w = slice(n * NTOK // 4, (n + 1) * NTOK // 4)
                        pool.memset(cwt[:, w].bitcast(f32), 0.0).then_inc(c_cwz, 1)

            pipeline(pool, iteration)

            pool.wait_ge(ob_mm, B * BU)

            def group(g, gh, par, main):
                first = isinstance(g, int) and g == 0
                for c in range(16 if main else 2):
                    if first:
                        beside(iteration, c, POOL_AT)
                    if c >= 2 or not first:
                        k = (c - 2) % 16
                        pool.wait_ge(e_ahi, g * 16 + (c - 1))
                        wait(pool, e_y, g * 16 + (c - 5))
                        pool.tensor_tensor(actl[:, k % 4, :], act[:, k % 4, :], acth[:, k % 4, :].bitcast(f32),
                                           ALU.subtract).then_inc(e_alo, 1)

            ffn(pool, group)

        @block.scalar
        def _(a):
            a.dma_start(gmat[:, :], gmat_d).then_inc(d_gm, 16)
            a.dma_start(w0s, w0[:, 0:2 * H0 * D0]).then_inc(d_w0, 16)
            a.dma_start(wvs, w0v).then_inc(d_wv, 16)
            a.wait_ge(d_w0, 16)
            a.activation(w0h[:, :], w0s, ACT.Copy).then_inc(c_w0h, 1)
            a.wait_ge(d_wv, 16)
            a.activation(wvh[:, :], wvs, ACT.Copy).then_inc(c_wvh, 1)

            def choice_exponentials(part):
                a.wait_ge(q_d, part + 1)
                t = tiles(part)
                a.activation(rexp[:, t, :], rdel[:, t, :], ACT.Exp).then_inc(q_exp, 1)

            def weights_high(g, bank):
                a.wait_ge(ct_mm, g + 1)
                a.activation(cwt[0:E, g * GRP:(g + 1) * GRP], bank[0:E, :], ACT.Copy)
                a.activation(cwt[64:64 + E, g * GRP:(g + 1) * GRP], bank[0:E, :], ACT.Copy).then_inc(ct_hi, 1)

            def iteration(X, G, A, M, Bm, R, L, steps=range(8)):
                def keys_or_queries(n):
                    a.wait_ge(g_mm, G.j * GU + (chunk_use(n) + 1))
                    if n < NCH:
                        if n == 0:
                            wait(a, k0_dma[(G.par + 1) % 2],
                                 (G.half + G.par) * 64 if not isinstance(G.j, int) or G.j > 0 else 0)
                        a.activation(kst0[:, n, :], projection(G, chunk_use(n))[:, 0:TOK], ACT.Copy).then_inc(g_ev, 1)
                    else:
                        wait(a, sa_mm, (G.j - 1) * AU)
                        if isinstance(G.j, int) and G.j < 2:
                            a.wait_ge((c_wvl, c_w1l)[G.j], 1)
                        a.activation(q0[:, G.par, n - NCH, :], projection(G, chunk_use(n))[:, 0:TOK], ACT.Copy,
                                     scale=SCALE0).then_inc(g_ev, 1)

                for n in steps:
                    if Bm is not None and n == 0:
                        a.wait_ge(m_v, Bm.j + 1)
                        wait(a, ob_mm, (Bm.j - 1) * BU)
                        a.activation(v1[:, Bm.par, :, :], pM[:, :].rearrange("p (a b) -> p a b", a=2),
                                     ACT.Copy).then_inc(m_vev, 1)
                    if R is not None and n == 3:
                        a.wait_ge(ob_mm, R.j * BU + BU)
                        wait(a, r_o, R.j)
                        for g in range(2):
                            last = a.activation(o1[:, g, :], pOB[:, g * TOK:(g + 1) * TOK], ACT.Identity,
                                                bias=bv1s[:, g:g + 1])
                        last.then_inc(ob_ev, 1)
                    if M is not None and n == 6:
                        a.wait_ge(m_k, M.j + 1)
                        wait(a, k1_dma[(M.par + 1) % 2],
                             (M.half + M.par) * 128 if not isinstance(M.j, int) or M.j > 0 else 0)
                        for g in range(2):
                            last = a.activation(kst1[:, 0, g, :], pM[:, g * TOK:(g + 1) * TOK], ACT.Identity,
                                                bias=bk1s[:, g:g + 1])
                        last.then_inc(m_khi, 1)
                    for J, u in collected(A, M, n):
                        wait(a, oa_mm, J.j * AU + (u + 1))
                        if u == 0:
                            wait(a, m_o, J.j)
                        pr, hf = u // 2, u % 2
                        tokens = slice(128 * pr, 128 * pr + 128)
                        a.activation(o0[:, 2 * hf:2 * hf + 2, tokens].rearrange("p c (w q) -> p c w q", w=2),
                                     pOA[:, 0:TOK].rearrange("p (w c q) -> p c w q", w=2, c=2), ACT.Copy)\
                         .then_inc(oa_ev, 1)
                    for J, pr in values_made(G, A, n):
                        a.wait_ge(g_mm, J.j * GU + (value_use(pr) + 1))
                        if isinstance(J.j, int) and J.j < 2:
                            a.wait_ge(z_kv[J.j], 1)
                        wait(a, oa_mm, (J.j - 2) * AU + 2 * pr + 2)
                        for w in range(2):
                            for half_ in range(2):
                                last = a.activation(
                                    v0[WIN * half_:WIN * half_ + WIN, J.par, 2 * pr + w, :, half_, :],
                                    projection(J, value_use(pr))[WIN * w:WIN * w + WIN, :]
                                    .rearrange("p (a b d) -> p a b d", b=2, d=D0)[:, :, half_, :], ACT.Copy)
                        last.then_inc(g_ev, 1)
                    if M is not None and n == 7:
                        a.wait_ge(m_q, M.j + 1)
                        if isinstance(M.j, int) and M.j == 0:
                            a.wait_ge(c_bq, 1)
                        wait(a, sb_mm, (M.j - 1) * BU)
                        for g in range(2):
                            last = a.activation(q1[:, M.par, g, :], pM[:, g * TOK:(g + 1) * TOK], ACT.Identity,
                                                bias=bq1x[:, g:g + 1])
                        last.then_inc(m_qhi, 1)
                    if M is not None and n == 5:
                        a.wait_ge(m_T, M.j + 1)
                        wait(a, m_v, M.j)
                        a.activation(t1h[:, :], pM[:, 0:TOK], ACT.Copy).then_inc(m_hi, 1)
                    if R is not None and n == 7:
                        a.wait_ge(r_T, R.j + 1)
                        wait(a, r_lg, R.j)
                        wait(a, r_x, R.j)
                        a.activation(t2f[:, :], last_bank(M, Bm)[:, 0:TOK], ACT.Copy).then_inc(r_f, 1)
                    if A is not None and n % 2 == 1:
                        u = n // 2
                        a.wait_ge(sa_sub, A.j * AU + (u + 1))
                        a.activation(pa[:, u % 2, :, :], pa[:, u % 2, :, :], ACT.Exp).then_inc(sa_exp, 1)
                    if G is not None and n % 2 == 1:
                        keys_or_queries(n)
                    if Bm is not None:
                        b = n % PBUFS
                        wait(a, sb_max, Bm.j * BU + (n + 1))
                        wait(a, sb_rcp, Bm.j * BU + (n + 1 - PBUFS))
                        wait(a, tb_mm, Bm.j * BU + (n + 1 - PBUFS))
                        for qc in range(2):
                            last = a.activation(pb[:, b, qc, :], (pSB, pSA)[n % 2][:, qc * TOK:(qc + 1) * TOK], ACT.Exp,
                                                bias=mxb[:, b, qc:qc + 1], accum_out=smb[:, b, qc:qc + 1])
                        last.then_inc(sb_exp, 1)
                    if X is not None and n == 3:
                        wait(a, g_mm, (X.j - 1) * GU)
                        a.wait_ge(x_s, X.j + 1)
                        a.activation(xnh[:, X.par, :], xns[:, :], ACT.Copy).then_inc(x_h, 1)
                    if G is not None and n % 2 == 0:
                        keys_or_queries(n)
                    for J, k in steps_back(Bm, R, n, 2):
                        wait(a, tb_mm, J.j * BU + (k + 1))
                        wait(a, ob_mm, J.j * BU + (k - 1))
                        a.activation(ptb[:, k % 2, :, :], pTB[:, :].rearrange("p (a b) -> p a b", a=2),
                                     ACT.Copy).then_inc(tb_ev, 1)
                    for J, u in turned(A, M, n):
                        wait(a, ta_mm, J.j * AU + (u + 1))
                        wait(a, oa_mm, J.j * AU + (u - 1))
                        a.activation(pta[:, u % 2, :], pTA[:, :], ACT.Copy).then_inc(ta_ev, 1)
                    if draining(A, M, Bm) == 1 and n == 1:
                        a.wait_ge(m_v, B)
                        a.wait_ge(r_x, 2)
                        a.activation(tgh[0][:, :], tnx[:, 0:GRP], ACT.Copy).then_inc(c_tgh, 1)
                    if draining(A, M, Bm) == 1 and n == 3:
                        a.wait_ge(c_b2z, 1)
                        a.wait_ge(d_f, F_DMAS)
                        for r in range(3):
                            last = a.activation(f2bst[32 * r:32 * r + E, :], f2bs[32 * r:32 * r + E, :], ACT.Copy)
                        last.then_inc(c_b2h, 1)
                    if draining(A, M, Bm) == 1 and n == 5:
                        choice_exponentials(0)
                    if last_alone(M, Bm, R) and n == 0:
                        a.wait_ge(c_cwz, 4)
                        for g in range(2):
                            weights_high(g, (pG, pTA)[g])
                    if last_alone(M, Bm, R) and n == 1:
                        a.wait_ge(d_sel, 16)
                        a.activation(sel[:, :, :], sels[:, :, :], ACT.Copy).then_inc(c_sel, 1)

            def after(i):
                if i == -1:
                    a.wait_ge(d_c1, C1_DMAS)
                    a.activation(w1s[:, 0:QK1], w1s[:, 0:QK1], ACT.Copy, scale=SCALE1).then_inc(c_w1s, 1)
                    a.wait_ge(c_w1s, 1)
                    a.activation(w1h[:, :], w1s, ACT.Copy).then_inc(c_w1h, 1)
                    a.activation(bq1x[:, :], bq1s[:, :], ACT.Copy, scale=SCALE1).then_inc(c_bq, 1)

            pipeline(a, iteration, after)

            a.wait_ge(ob_mm, B * BU)
            a.wait_ge(d_f2, 16)

            def group(g, gh, par, main):
                first = isinstance(g, int) and g == 0
                for c in range(16 if main else 5):
                    if first:
                        beside(iteration, c, ACT_AT)
                    if main:
                        a.wait_ge(e_h1, g * 16 + (c + 1))
                        wait(a, e_gat, g * 16 + (c - 1))
                        i1, _ = pieces(c)
                        a.activation(sil[:, c % 2, :], (pSA, pSB)[c % 2][:, :], ACT.Silu,
                                     bias=f1bs[:, i1:i1 + 1]).then_inc(e_sil, 1)
                    if (main and c >= 2) or (c < 2 and not first):
                        k = (c - 2) % 16
                        a.wait_ge(e_act, g * 16 + (c - 1))
                        wait(a, e_y, g * 16 + (c - 5))
                        a.activation(acth[:, k % 4, :], act[:, k % 4, :], ACT.Copy).then_inc(e_ahi, 1)
                    if first and c < 2:
                        h = slice(c * NFC // 2, (c + 1) * NFC // 2)
                        a.activation(f2h[:, h, :], f2s[:, h, :], ACT.Copy).then_inc(c_f2h, 1)
                    if first and c == 10:
                        choice_exponentials(1)
                    if isinstance(g, int) and g < 3 and c in (11, 14):
                        weights_high(2 + 2 * g + (c - 11) // 3, (pOA, pOB)[1 - par])
                    if c == 4 and not first:
                        a.wait_ge(e_y, g * 16)
                        wait(a, y_T, g - 1)
                        a.activation(yt[:, :], (pOA, pOB)[1 - par][:, :], ACT.Copy).then_inc(y_ev, 1)
                    if c == 8 and main and not (isinstance(g, int) and g == NGRP - 1):
                        wait(a, e_h2, g * 16)
                        a.activation(tgh[1 - par][:, :], tnx[:, bass.ds(g * GRP + GRP, GRP)],
                                     ACT.Copy).then_inc(c_tgh, 1)

            ffn(a, group)

        @block.vector
        def _(v):
            def statistics(images, part):
                for j in images:
                    if j % 4 == 0:
                        v.wait_ge(d_x[j // 4], 16)
                    last = v.bn_stats(gst[:, j, :], xch[:, j * TOK:(j + 1) * TOK])
                last.then_inc(gn_st, 1)
                v.wait_ge(gn_st, part)
                for j in images:
                    last = v.bn_aggr(gmv[:, j, :], gst[:, j, :])
                last.then_inc(gn_ag, 1)
                v.wait_ge(gn_ag, part)
                t = slice(images.start, images.stop)
                v.tensor_tensor(gsq[:, t], gmv[:, t, 0], gmv[:, t, 0], ALU.mult).then_inc(gn_sq, 1)
                v.wait_ge(gn_sq, part)
                v.tensor_tensor(gmv[:, t, 1], gmv[:, t, 1], gsq[:, t], ALU.add).then_inc(gn_e2, 1)

            def group_variance(images, part):
                t = slice(images.start, images.stop)
                v.wait_ge(gn_mm, part)
                v.tensor_copy(gsum[:, t, :], pOB[:, 2 * t.start:2 * t.stop].rearrange("p (b t) -> p b t", t=2))\
                 .then_inc(gn_cp, 1)
                v.wait_ge(gn_cp, part)
                v.tensor_tensor(gsq[:, t], gsum[:, t, 0], gsum[:, t, 0], ALU.mult).then_inc(gn_q, 1)
                v.wait_ge(gn_q, part)
                v.tensor_tensor(gsq[:, t], gsum[:, t, 1], gsq[:, t], ALU.subtract).then_inc(gn_v, 1)
                v.wait_ge(gn_v, part)
                v.tensor_scalar(gsq[:, t], gsq[:, t], EPS, None, ALU.add).then_inc(gn_eps, 1)

            statistics(GN_PARTS[0], 1)
            group_variance(GN_PARTS[0], 1)
            v.wait_ge(c_w0h, 1)
            v.tensor_tensor(w0l[:, :], w0s, w0h[:, :].bitcast(f32), ALU.subtract).then_inc(c_w0l, 1)
            v.wait_ge(c_wvh, 1)
            v.tensor_tensor(wvl[:, :], wvs, wvh[:, :].bitcast(f32), ALU.subtract).then_inc(c_wvl, 1)
            v.wait_ge(d_mask, 16)
            v.wait_ge(d_pos, 16 * 16)
            for pr in range(2):
                for ky in range(8):
                    last = v.tensor_tensor(bias0[:, pr, :, ky], posr[:, :, 7 - ky], masks[:, pr, :, ky], ALU.add)
            last.then_inc(c_bias, 1)
            statistics(GN_PARTS[1], 2)
            v.memset(kbd0[1][:, :, :, :], 0.0)
            v.memset(v0[:, 1, :, :, :, :], 0.0).then_inc(z_kv[1], 1)

            def split_first(e):
                if e == 0:
                    v.wait_ge(oa_mm, B * AU)
                    v.wait_ge(d_f1, 16)
                w = slice(e * 4 * 128, (e + 1) * 4 * 128)
                v.tensor_copy(f1h[:, w], f1s[:, w]).then_inc(c_f1h, 1)
                v.wait_ge(c_f1h, e + 1)
                v.tensor_tensor(f1l[:, w], f1s[:, w], f1h[:, w].bitcast(f32), ALU.subtract).then_inc(c_f1l, 1)

            def best_two(part):
                t, n = tiles(part), part + 1
                for k in range(t.start, t.stop):
                    last = v.max(mx8[:, k, :], logit[:, k, :])
                last.then_inc(q_max, 1)
                v.wait_ge(q_max, n)
                v.tensor_tensor(rdel[:, t, :], mx8[:, t, 1:2], mx8[:, t, 0:1], ALU.subtract).then_inc(q_d, 1)

            def best_experts(part):
                t, n = tiles(part), part + 1
                for k in range(t.start, t.stop):
                    last = v.max_index(ix8[:, k, :], mx8[:, k, :], logit[:, k, :])
                last.then_inc(q_ix, 1)
                v.wait_ge(q_ix, n)
                v.tensor_copy(ixf[:, t, :], ix8[:, t, :]).then_inc(q_ixf, 1)

            def expert_weights(part):
                t, n = tiles(part), part + 1
                full = [128, t.stop - t.start, E]
                v.wait_ge(q_exp, n)
                v.tensor_scalar(rden[:, t, :], rexp[:, t, :], 1.0, None, ALU.add).then_inc(q_den, 1)
                v.wait_ge(q_ixf, n)
                v.tensor_tensor(cwa[:, t, :], iota[:, :].unsqueeze(1).to_broadcast(full),
                                ixf[:, t, 0:1].to_broadcast(full), ALU.is_equal).then_inc(q_a, 1)
                v.wait_ge(q_den, n)
                v.reciprocal(wt1[:, t, :], rden[:, t, :]).then_inc(q_w1, 1)
                v.tensor_tensor(cwb[:, t, :], iota[:, :].unsqueeze(1).to_broadcast(full),
                                ixf[:, t, 1:2].to_broadcast(full), ALU.is_equal).then_inc(q_b, 1)
                v.wait_ge(q_w1, n)
                v.tensor_tensor(wt2[:, t, :], rexp[:, t, :], wt1[:, t, :], ALU.mult).then_inc(q_w2, 1)
                v.wait_ge(q_a, n)
                v.tensor_tensor(cwa[:, t, :], cwa[:, t, :], wt1[:, t, :].to_broadcast(full), ALU.mult).then_inc(q_am, 1)
                v.wait_ge(q_b, n)
                v.wait_ge(q_w2, n)
                v.tensor_tensor(cwb[:, t, :], cwb[:, t, :], wt2[:, t, :].to_broadcast(full), ALU.mult).then_inc(q_bm, 1)
                v.wait_ge(q_am, n)
                v.wait_ge(q_bm, n)
                v.tensor_tensor(cws[:, t, :], cwa[:, t, :], cwb[:, t, :], ALU.add).then_inc(q_cw, 1)

            def weights_low(g, bank):
                v.wait_ge(ct_hi, g + 1)
                v.tensor_tensor(cwt[32:32 + E, g * GRP:(g + 1) * GRP], bank[0:E, :],
                                cwt[0:E, g * GRP:(g + 1) * GRP].bitcast(f32), ALU.subtract).then_inc(ct_lo, 1)

            def iteration(X, G, A, M, Bm, R, L, steps=range(8)):
                def reciprocal_b(n):
                    b = n % PBUFS
                    v.wait_ge(sb_exp, Bm.j * BU + (n + 1))
                    wait(v, sb_nrm, Bm.j * BU + (n + 1 - PBUFS))
                    v.reciprocal(rcb[:, b, :], smb[:, b, :]).then_inc(sb_rcp, 1)

                for n in steps:
                    if L is not None and n == 2:
                        v.wait_ge(r_lg, L.j + 1)
                        v.tensor_tensor(logit[:, bass.ds(L.j * 2, 2), :],
                                        logit_bank(R)[:, 0:2 * E].rearrange("p (s e) -> p s e", s=2), rbs[:, :, :],
                                        ALU.add).then_inc(r_lgev, 1)
                    if M is not None and n == 7:
                        v.wait_ge(m_qhi, M.j + 1)
                        for g in range(2):
                            last = v.scalar_tensor_tensor(q1[64:, M.par, g, :], pM[64:, g * TOK:(g + 1) * TOK],
                                                          bq1x[64:, g:g + 1], q1[64:, M.par, g, :].bitcast(f32),
                                                          ALU.add, ALU.subtract)
                        last.then_inc(m_qlo, 1)
                    if M is not None and n == 3:
                        v.wait_ge(m_o, M.j + 1)
                        v.wait_ge(m_xb, M.j + 1)
                        wait(v, m_tb, M.j)
                        v.tensor_tensor(t1[:, :, :], pM[:, 0:TOK].rearrange("p (s c) -> p s c", s=2),
                                        xt[:, M.par, :, :], ALU.add).then_inc(m_t, 1)
                        v.wait_ge(m_t, M.j + 1)
                        for s in range(2):
                            last = v.bn_stats(st1[:, s, :], t1[:, s, :])
                        last.then_inc(m_st, 1)
                    if R is not None and n == 5:
                        v.wait_ge(r_o, R.j + 1)
                        v.wait_ge(m_tb, R.j + 1)
                        v.tensor_tensor(t2[:, :, :], last_bank(M, Bm)[:, 0:TOK].rearrange("p (s c) -> p s c", s=2),
                                        t1b[:, R.par, :, :], ALU.add).then_inc(r_t, 1)
                    if M is not None and n == 6:
                        v.wait_ge(m_khi, M.j + 1)
                        for g in range(2):
                            last = v.scalar_tensor_tensor(kst1[:, 1, g, :], pM[:, g * TOK:(g + 1) * TOK],
                                                          bk1s[:, g:g + 1], kst1[:, 0, g, :].bitcast(f32),
                                                          ALU.add, ALU.subtract)
                        last.then_inc(m_klo, 1)
                    if M is not None and n == 3:
                        v.wait_ge(m_st, M.j + 1)
                    if Bm is not None:
                        bank, b1 = (pSB, pSA)[n % 2], n % PBUFS
                        v.wait_ge(sb_mm, Bm.j * BU + (n + 1))
                        v.tensor_reduce(mxb[:, b1, :], bank[:, :].rearrange("p (a k) -> p a k", a=2), AX.X, ALU.max,
                                        negate=True).then_inc(sb_max, 1)
                    if M is not None and n == 3:
                        for s in range(2):
                            last = v.bn_aggr(mv1[:, s, :], st1[:, s, :])
                        last.then_inc(m_ag, 1)
                        v.wait_ge(m_ag, M.j + 1)
                        v.tensor_scalar(rs1[:, :], mv1[:, :, 1], EPS, None, ALU.add).then_inc(m_eps, 1)
                    if A is not None and n % 2 == 0:
                        u = n // 2
                        b = u % 2
                        if isinstance(A.j, int) and A.j == 0 and u == 0:
                            v.wait_ge(c_bias, 1)
                        v.wait_ge(sa_mm, A.j * AU + (u + 1))
                        wait(v, ta_mm, A.j * AU + (u - 1))
                        v.tensor_tensor(pa[:, b, :, :], pSA[:, :].rearrange("p (h k) -> p h k", h=8),
                                        bias0[:, u // 2, :, :].rearrange("p x y -> p (x y)").unsqueeze(1)
                                        .to_broadcast([128, 8, WIN]), ALU.add).then_inc(sa_add, 1)
                    if M is not None and n == 4:
                        wait(v, m_T, M.j)
                        v.wait_ge(m_pow, M.j + 1)
                        for s in range(2):
                            last = v.tensor_scalar(tn1[:, s, :], t1[:, s, :],
                                                   mv1[:, s, 0:1], rs1[:, s:s + 1], ALU.subtract, ALU.mult)
                        last.then_inc(m_tn, 1)
                    if R is not None and n == 6:
                        wait(v, r_T, R.j)
                        v.wait_ge(r_pow, R.j + 1)
                        for s in range(2):
                            last = v.tensor_scalar(tn2[:, s, :], t2[:, s, :],
                                                   mv2[:, s, 0:1], rs2[:, s:s + 1], ALU.subtract, ALU.mult)
                        last.then_inc(r_tn, 1)
                    if A is not None and n % 2 == 0:
                        v.wait_ge(sa_add, A.j * AU + (u + 1))
                        v.tensor_reduce(mxa[:, b, :], pa[:, b, :, :], AX.X, ALU.max).then_inc(sa_max, 1)
                    if Bm is not None and n % 2 == 0:
                        reciprocal_b(n)
                    if A is not None and n % 2 == 0:
                        v.wait_ge(sa_max, A.j * AU + (u + 1))
                        v.tensor_tensor(pa[:, b, :, :], pa[:, b, :, :],
                                        mxa[:, b, :].unsqueeze(2).to_broadcast([128, 8, WIN]),
                                        ALU.subtract).then_inc(sa_sub, 1)
                    if M is not None and n == 5:
                        v.wait_ge(m_hi, M.j + 1)
                        v.tensor_tensor(t1l[:, :], pM[:, 0:TOK], t1h[:, :].bitcast(f32),
                                        ALU.subtract).then_inc(m_lo, 1)
                    if A is not None and n % 2 == 1:
                        u = n // 2
                        b = u % 2
                        v.wait_ge(sa_exp, A.j * AU + (u + 1))
                        v.tensor_reduce(sma[:, b, :], pa[:, b, :, :], AX.X, ALU.add).then_inc(sa_sum, 1)
                    if R is not None and n == 5:
                        v.wait_ge(r_t, R.j + 1)
                        for s in range(2):
                            last = v.bn_stats(st2[:, s, :], t2[:, s, :])
                        last.then_inc(r_st, 1)
                        v.wait_ge(r_st, R.j + 1)
                        v.tensor_scalar(res2[:, R.cols(TOK)], t2[:, :, :].rearrange("p s c -> p (s c)"),
                                        1.0, None, ALU.mult)
                        for s in range(2):
                            last = v.bn_aggr(mv2[:, s, :], st2[:, s, :])
                        last.then_inc(r_ag, 1)
                        v.wait_ge(r_ag, R.j + 1)
                        v.tensor_scalar(rs2[:, :], mv2[:, :, 1], EPS, None, ALU.add).then_inc(r_eps, 1)
                    if A is not None and n % 2 == 1:
                        v.wait_ge(sa_sum, A.j * AU + (u + 1))
                        wait(v, sa_nrm, A.j * AU + (u - 1))
                        v.reciprocal(rca[:, b, :], sma[:, b, :]).then_inc(sa_rcp, 1)
                    if R is not None and n == 7:
                        v.wait_ge(r_f, R.j + 1)
                        v.tensor_scalar(tnx[:, R.cols(TOK)], t2f[:, :], 1.0, None, ALU.mult).then_inc(r_x, 1)
                    if Bm is not None and n % 2 == 1:
                        reciprocal_b(n)
                    if draining(A, M, Bm) == 1 and n < 4:
                        split_first(n)
                    if draining(A, M, Bm) == 1 and n == 0:
                        v.wait_ge(m_v, B)
                        v.memset(f2bst[:, :].bitcast(f32), 0.0).then_inc(c_b2z, 1)
                    if draining(A, M, Bm) == 1 and n == 3:
                        v.wait_ge(c_tgh, 1)
                        v.tensor_tensor(tgl[0][:, :], tnx[:, 0:GRP], tgh[0][:, :].bitcast(f32),
                                        ALU.subtract).then_inc(c_tgl, 1)
                    if draining(A, M, Bm) == 1 and n == 4:
                        v.wait_ge(r_lgev, EARLY)
                        best_two(0)
                    if draining(A, M, Bm) == 1 and n == 5:
                        best_experts(0)
                    if draining(A, M, Bm) == 1 and n == 6:
                        v.wait_ge(d_f, F_DMAS)
                        expert_weights(0)
                    if draining(A, M, Bm) == 1 and n == 7:
                        v.wait_ge(c_b2h, 1)
                        v.tensor_tensor(f2bst[64:64 + E, :], f2bs[64:64 + E, :], f2bst[64:64 + E, :].bitcast(f32),
                                        ALU.subtract).then_inc(c_b2l, 1)
                    if last_alone(M, Bm, R) and n == 1:
                        for g in range(2):
                            weights_low(g, (pG, pTA)[g])

            def after(i):
                if i == -1:
                    v.wait_ge(c_w1h, 1)
                    v.tensor_tensor(w1l[:, :], w1s, w1h[:, :].bitcast(f32), ALU.subtract).then_inc(c_w1l, 1)
                    group_variance(GN_PARTS[1], 2)

            pipeline(v, iteration, after)

            v.wait_ge(ob_mm, B * BU)

            def group(g, gh, par, main):
                first = isinstance(g, int) and g == 0
                for c in range(16 if main else 7):
                    if first:
                        beside(iteration, c, DVE_AT)
                    if main:
                        i1, i2 = pieces(c)
                        v.wait_ge(e_h2, g * 16 + (c + 1))
                        v.wait_ge(e_sil, g * 16 + (c + 1))
                        v.scalar_tensor_tensor(gat[:, c % 4, :], (pTA, pTB)[c % 2][:, :], f1bs[:, i2:i2 + 1],
                                               sil[:, c % 2, :], ALU.add, ALU.mult).then_inc(e_gat, 1)
                    if (main and c > 0) or (c == 0 and not first):
                        k = (c - 1) % 16
                        v.wait_ge(e_gat, g * 16 + c)
                        v.wait_ge(e_cw, g * 8 + (c + 1) // 2)
                        wait(v, e_alo, g * 16 + (c - 4))
                        v.tensor_tensor(act[:, k % 4, :], gat[:, k % 4, :], (pG, pM)[(k // 2) % 2][:, :],
                                        ALU.mult).then_inc(e_act, 1)
                    if first and c in (1, 3):
                        h = slice((c // 2) * NFC // 2, (c // 2 + 1) * NFC // 2)
                        v.wait_ge(c_f2h, c // 2 + 1)
                        v.tensor_tensor(f2l[:, h, :], f2s[:, h, :], f2h[:, h, :].bitcast(f32),
                                        ALU.subtract).then_inc(c_f2l, 1)
                    if first and c in (0, 2, 4, 6):
                        split_first(4 + c // 2)
                    if first and c in (9, 11, 13):
                        v.wait_ge(r_lgev, B)
                        (best_two, best_experts, expert_weights)[(c - 9) // 2](1)
                    if isinstance(g, int) and g < 3 and c in (12, 15):
                        weights_low(2 + 2 * g + (c - 12) // 3, (pOA, pOB)[1 - par])
                    if c == 6 and not first:
                        v.wait_ge(y_T, g)
                        if not (isinstance(g, int) and g < 3):
                            v.wait_ge(y_dma[1 - par], (gh - 1 + par) * 16)
                        v.tensor_tensor(yo[:, 1 - par, :], (pOA, pOB)[1 - par][:, :],
                                        res2[:, bass.ds(g * GRP - GRP, GRP)], ALU.add).then_inc(y_add, 1)
                    if c == 9 and main and not (isinstance(g, int) and g == NGRP - 1):
                        v.wait_ge(c_tgh, g + 2)
                        v.tensor_tensor(tgl[1 - par][:, :], tnx[:, bass.ds(g * GRP + GRP, GRP)],
                                        tgh[1 - par][:, :].bitcast(f32), ALU.subtract).then_inc(c_tgl, 1)

            ffn(v, group)

        @block.tensor
        def _(pe):
            def split_product(out_, wh, wl, xh, xl):
                pe.matmul(out_, wh, xh, start=True, stop=False)
                pe.matmul(out_, wl, xh, start=False, stop=False)
                return pe.matmul(out_, wh, xl, start=False, stop=True)

            def group_means(part):
                images = GN_PARTS[part]
                pe.wait_ge(gn_e2, part + 1)
                pe.matmul(pOB[:, 2 * images.start:2 * images.stop], gmat[:, :],
                          gmv[:, images.start:images.stop, :].rearrange("p b t -> p (b t)"),
                          start=True, stop=True).then_inc(gn_mm, 1)

            pe.wait_ge(d_gm, 16)
            group_means(0)

            def turn_weights(g, bank):
                for s in range(GRP // 128):
                    mm = pe.transpose(bank[0:E, s * 128:(s + 1) * 128], cws[:, g * 4 + s, :], ident[:, :])
                mm.then_inc(ct_mm, 1)

            def iteration(X, G, A, M, Bm, R, L, steps=range(8)):
                def keys_or_queries(n):
                    if n == 0:
                        pe.wait_ge(x_l, G.j + 1)
                        if isinstance(G.j, int) and G.j == 0:
                            pe.wait_ge(c_w0l, 1)
                        if isinstance(G.j, int) and G.j == 1:
                            pe.wait_ge(gn_cp, 1)
                            group_means(1)
                    wait(pe, g_ev, projection_read(G, chunk_use(n)))
                    c = NCH + n if n < NCH else n - NCH
                    split_product(projection(G, chunk_use(n))[:, 0:TOK],
                                  w0h[:, c * 128:(c + 1) * 128], w0l[:, c * 128:(c + 1) * 128],
                                  xnh[:, G.par, :], xnl[:, G.par, :]).then_inc(g_mm, 1)

                for n in steps:
                    if Bm is not None:
                        if n == 0:
                            pe.wait_ge(m_qlo, Bm.j + 1)
                            pe.wait_ge(k1_dma[Bm.par], Bm.half * 128 + 128)
                        wait(pe, sb_exp, Bm.j * BU + (n - 1))
                        if A is not None and n % 2 == 1:
                            pe.wait_ge(sa_add, A.j * AU + (n // 2 + 1))
                        for qc in range(2):
                            for part in range(2):
                                mm = pe.matmul((pSB, pSA)[n % 2][:, qc * TOK:(qc + 1) * TOK],
                                               q1[:, Bm.par, n // 4, qc * 128:(qc + 1) * 128],
                                               kbd1[Bm.par][:, part, n // 4, n % 4, :],
                                               start=(part == 0), stop=(part == 1))
                        mm.then_inc(sb_mm, 1)
                    if A is not None and n % 2 == 0:
                        u = n // 2
                        pr, hf = u // 2, u % 2
                        if u == 0:
                            pe.wait_ge(g_ev, A.j * GU + (chunk_use(2 * NCH - 1) + 1))
                            pe.wait_ge(k0_dma[A.par], A.half * 64 + 64)
                        wait(pe, sa_add, A.j * AU + u)
                        if Bm is not None:
                            wait(pe, sb_exp, Bm.j * BU + n)
                        for cc in range(2):
                            for w in range(2):
                                t = 128 * pr + WIN * w
                                mm = pe.matmul(pSA[WIN * w:WIN * w + WIN, cc * TOK:(cc + 1) * TOK],
                                               q0[:, A.par, 2 * hf + cc, t:t + WIN],
                                               kbd0[A.par][:, 2 * hf + cc, :, t:t + WIN], start=True, stop=True)
                        mm.then_inc(sa_mm, 1)
                    if G is not None and n % 2 == 1:
                        keys_or_queries(n)
                    for J, k in steps_back(Bm, R, n, 2):
                        wait(pe, sb_nrm, J.j * BU + (k + 1))
                        wait(pe, tb_ev, J.j * BU + k)
                        for kc in range(2):
                            for qc in range(2):
                                mm = pe.transpose(pTB[:, kc * TOK + qc * 128:kc * TOK + (qc + 1) * 128],
                                                  pb[:, k % PBUFS, qc, kc * 128:(kc + 1) * 128], ident[:, :])
                        mm.then_inc(tb_mm, 1)
                    if G is not None and n % 2 == 0:
                        keys_or_queries(n)
                    for J, k in steps_back(Bm, R, n, 3):
                        wait(pe, tb_ev, J.j * BU + (k + 1))
                        if k == 0:
                            if isinstance(J.j, int) and J.j == 0:
                                pe.wait_ge(gn_cp, 2)
                                pe.wait_ge(d_c0, C0_DMAS)
                            wait(pe, ob_ev, J.j)
                            wait(pe, m_vev, J.j + 1)
                        r, g = D1 * 2 * (k % 4), k // 4
                        for kc in range(2):
                            mm = pe.matmul(pOB[r:r + PAD1, g * TOK:(g + 1) * TOK],
                                           v1[:, J.par, kc, k * PAD1:(k + 1) * PAD1], ptb[:, k % 2, kc, :],
                                           start=(kc == 0), stop=(kc == 1))
                        mm.then_inc(ob_mm, 1)
                    if R is not None and n == 4:
                        pe.wait_ge(ob_ev, R.j + 1)
                        if A is not None:
                            pe.wait_ge(oa_ev, A.j * AU + 1)
                        else:
                            pe.wait_ge(oa_ev, B * AU)
                            pe.wait_ge(r_f, R.j)
                        for s in range(2):
                            for g in range(2):
                                mm = pe.matmul(last_bank(M, Bm)[:, s * C:(s + 1) * C], o1[:, g, s * 128:(s + 1) * 128],
                                               wo1s[:, g, :], start=(g == 0), stop=(g == 1))
                        mm.then_inc(r_o, 1)
                    if M is not None and n in (5, 6):
                        if n == 5:
                            pe.wait_ge(m_lo, M.j + 1)
                            if isinstance(M.j, int) and M.j == 0:
                                pe.wait_ge(c_w1l, 1)
                        else:
                            pe.wait_ge(m_klo, M.j + 1)
                        for g in range(2):
                            c = (QK1 if n == 5 else 0) + g * 128
                            mm = split_product(pM[:, g * TOK:(g + 1) * TOK], w1h[:, c:c + 128], w1l[:, c:c + 128],
                                               t1h[:, :], t1l[:, :])
                        mm.then_inc(m_k if n == 5 else m_q, 1)
                    for J, u in applied(A, M, n):
                        if u == 0:
                            pe.wait_ge(g_ev, J.j * GU + GU)
                        wait(pe, ta_ev, J.j * AU + (u + 1))
                        wait(pe, oa_ev, J.j * AU + u)
                        if R is not None and n == 5:
                            pe.wait_ge(r_t, R.j + 1)
                        if R is not None and n == 7:
                            pe.wait_ge(r_f, R.j + 1)
                        pr, hf = u // 2, u % 2
                        for w in range(2):
                            for jj in range(4):
                                mm = pe.matmul(pOA[WIN * (jj % 2):WIN * (jj % 2) + WIN,
                                                   (2 * w + jj // 2) * WIN:(2 * w + jj // 2 + 1) * WIN],
                                               v0[:, J.par, 2 * pr + w, 4 * hf + jj, :, :]
                                               .rearrange("p a d -> p (a d)"),
                                               pta[:, u % 2, jj * 128 + w * WIN:jj * 128 + w * WIN + WIN],
                                               start=True, stop=True)
                        mm.then_inc(oa_mm, 1)
                    if M is not None and n == 2:
                        pe.wait_ge(oa_ev, M.j * AU + AU)
                        if L is not None:
                            pe.wait_ge(r_lgev, L.j + 1)
                        else:
                            wait(pe, m_vev, M.j)
                        for s in range(2):
                            for c in range(NCH):
                                mm = pe.matmul(pM[:, s * C:(s + 1) * C], o0[:, c, s * 128:(s + 1) * 128],
                                               wo0s[:, c, :], start=(c == 0), stop=(c == NCH - 1))
                        mm.then_inc(m_o, 1)
                    for J, u in turned(A, M, n):
                        wait(pe, sa_nrm, J.j * AU + (u + 1))
                        wait(pe, ta_ev, J.j * AU + u)
                        for jj in range(4):
                            mm = pe.transpose(pTA[:, jj * 128:(jj + 1) * 128],
                                              pa[:, u % 2, 2 * jj:2 * jj + 2, :].rearrange("p h k -> p (h k)"),
                                              ident[:, :])
                        mm.then_inc(ta_mm, 1)
                    if M is not None and n == 4:
                        pe.wait_ge(m_tn, M.j + 1)
                        for s in range(2):
                            mm = pe.transpose(pM[:, s * 128:(s + 1) * 128], tn1[:, s, :], ident[:, :])
                        mm.then_inc(m_T, 1)
                    if R is not None and n == 6:
                        pe.wait_ge(r_tn, R.j + 1)
                        if A is not None:
                            pe.wait_ge(oa_ev, A.j * AU + 2)
                        for s in range(2):
                            mm = pe.transpose(last_bank(M, Bm)[:, s * 128:(s + 1) * 128], tn2[:, s, :], ident[:, :])
                        mm.then_inc(r_T, 1)
                    if M is not None and n == 7:
                        pe.wait_ge(m_qlo, M.j + 1)
                        for s in range(2):
                            mm = split_product(pM[:, s * TOK:(s + 1) * TOK], t1h[:, s * 128:(s + 1) * 128],
                                               t1l[:, s * 128:(s + 1) * 128], w1h[:, 2 * QK1:], w1l[:, 2 * QK1:])
                        mm.then_inc(m_v, 1)
                    if G is not None and n % NCH == NCH - 1:
                        pr = n // NCH
                        if isinstance(G.j, int) and G.j == 0:
                            pe.wait_ge(c_wvl, 1)
                        pe.wait_ge(g_ev, projection_read(G, value_use(pr)))
                        split_product(projection(G, value_use(pr))[:, :], xnh[:, G.par, pr * 128:(pr + 1) * 128],
                                      xnl[:, G.par, pr * 128:(pr + 1) * 128], wvh[:, :], wvl[:, :]).then_inc(g_mm, 1)
                    if L is not None and n == 1:
                        pe.wait_ge(r_f, L.j + 1)
                        if Bm is not None:
                            pe.wait_ge(m_vev, Bm.j + 1)
                        else:
                            wait(pe, r_lgev, L.j)
                            wait(pe, r_f, L.j + 1)
                        for s in range(2):
                            mm = pe.matmul(logit_bank(R)[:, s * E:(s + 1) * E],
                                           t2f[:, s * 128:(s + 1) * 128], rws[:, :],
                                           start=True, stop=True)
                        mm.then_inc(r_lg, 1)
                    if draining(A, M, Bm) == 1 and n == 7:
                        pe.wait_ge(q_cw, 1)
                        pe.wait_ge(g_ev, B * GU)
                        pe.wait_ge(ta_ev, B * AU)
                        for g in range(2):
                            turn_weights(g, (pG, pTA)[g])

            pipeline(pe, iteration)

            pe.wait_ge(r_lgev, B - 1)
            pe.wait_ge(r_f, B - 1)
            pe.wait_ge(c_tgl, 1)
            pe.wait_ge(c_b2l, 1)
            pe.wait_ge(c_sel, 1)
            pe.wait_ge(ct_lo, 2)

            def group(g, gh, par, main):
                first = isinstance(g, int) and g == 0
                for c in range(16 if main else 6):
                    if main:
                        if c % 2 == 0:
                            wait(pe, e_act, g * 16 + (c - 2))
                            pe.matmul((pG, pM)[(c // 2) % 2][:, :], sel[:, c // 2, :], cwt[:, bass.ds(g * GRP, GRP)],
                                      start=True, stop=True).then_inc(e_cw, 1)
                        if c == 0:
                            pe.wait_ge(c_tgl, g + 1)
                        if first and c % 2 == 0:
                            pe.wait_ge(c_f1l, c // 2 + 1)
                        i1, i2 = pieces(c)
                        wait(pe, e_sil, g * 16 + (c - 1))
                        split_product((pSA, pSB)[c % 2][:, :], f1h[:, i1 * 128:(i1 + 1) * 128],
                                      f1l[:, i1 * 128:(i1 + 1) * 128], tgh[par][:, :], tgl[par][:, :])\
                            .then_inc(e_h1, 1)
                        wait(pe, e_gat, g * 16 + (c - 1))
                        split_product((pTA, pTB)[c % 2][:, :], f1h[:, i2 * 128:(i2 + 1) * 128],
                                      f1l[:, i2 * 128:(i2 + 1) * 128], tgh[par][:, :], tgl[par][:, :])\
                            .then_inc(e_h2, 1)
                    if (main and c >= 4) or (c < 4 and not first):
                        k = (c - 4) % 16
                        y = (pOA, pOB)[par if c >= 4 else 1 - par]
                        pe.wait_ge(e_alo, g * 16 + (c - 3))
                        if first and k in (0, 8):
                            pe.wait_ge(c_f2l, k // 8 + 1)
                        if k == 0:
                            wait(pe, y_add, g - 1)
                            pe.wait_ge(ct_lo, 2 + 2 * g if isinstance(g, int) and g < 3 else NGRP)
                            pe.matmul(y[:, :], f2bst[:, :], cwt[:, bass.ds(g * GRP, GRP)], start=True, stop=False)
                        pe.matmul(y[:, :], f2h[:, k, :], acth[:, k % 4, :], start=False, stop=False)
                        pe.matmul(y[:, :], f2l[:, k, :], acth[:, k % 4, :], start=False, stop=False)
                        pe.matmul(y[:, :], f2h[:, k, :], actl[:, k % 4, :], start=False, stop=(k == 15))\
                            .then_inc(e_y, 1)
                    if first:
                        beside(iteration, c, PE_AT)
                    if isinstance(g, int) and g < 3 and c in (10, 13):
                        if g:
                            pe.wait_ge(y_add, g)
                        else:
                            pe.wait_ge(r_lgev, B)
                        if g == 1:
                            pe.wait_ge(q_cw, 2)
                        if c == 13:
                            pe.wait_ge(ct_lo, 3 + 2 * g)
                        turn_weights(2 + 2 * g + (c - 10) // 3, (pOA, pOB)[1 - par])
                    if c == 5 and not first:
                        pe.wait_ge(y_ev, g)
                        for s in range(GRP // 128):
                            mm = pe.transpose((pOA, pOB)[1 - par][:, s * 128:(s + 1) * 128],
                                              yt[:, s * 128:(s + 1) * 128], ident[:, :])
                        mm.then_inc(y_T, 1)

            ffn(pe, group)


def kernel(x, L0_conv_w_qkv, L0_conv_pos_embedding, L0_conv_w_out, L0_conv_b_out, L1_attn_w_qkv, L1_attn_b_qkv,
           L1_attn_w_out, L1_attn_b_out, L1_ffn_router_w, L1_ffn_router_b, L1_ffn_fc1_w, L1_ffn_fc1_b,
           L1_ffn_fc2_w, L1_ffn_fc2_b):
    import concourse.bacc as bacc
    from concourse.bass_utils import run_bass_kernel_spmd

    def host(a):
        return np.asarray(a)

    xr = np.roll(host(x), (-4, -4), axis=(1, 2))
    xw = xr.reshape(B, 2, 8, 2, 8, C).transpose(0, 1, 3, 2, 4, 5).reshape(NTOK, C)

    q = np.arange(WIN)
    ul = (q[:, None] >= 32) != (q[None, :] >= 32)
    lr = (q[:, None] % 8 >= 4) != (q[None, :] % 8 >= 4)
    mask = np.zeros((128, 2, WIN), np.float32)
    mask[WIN:, 0][lr] = -1e30
    mask[:WIN, 1][ul] = -1e30
    mask[WIN:, 1][ul | lr] = -1e30

    eye = np.eye(128, dtype=np.float32)
    gmat = np.kron(np.eye(32), np.full((4, 4), 0.25)).astype(np.float32)
    sel = np.zeros((128, E, 128), np.float32)
    for e in range(E):
        sel[[e, 32 + e], e, :] = 1.0
    iota = np.tile(np.arange(E, dtype=np.float32), (128, 1))

    def padded(a):
        a = a.reshape((H1, D1) + a.shape[1:])
        return np.concatenate([a, np.zeros_like(a)], axis=1).reshape((H1 * PAD1,) + a.shape[2:])

    w1 = host(L1_attn_w_qkv)
    bq = host(L1_attn_b_qkv)
    def twice(a):
        a = a.reshape(a.shape[:-1] + (2, 1, 64))
        return np.concatenate([a, a], axis=-2).reshape(a.shape[:-3] + (QK1,))

    arrays = {
        "x_tok": xw,
        "x_ch": xw.T,
        "w0": host(L0_conv_w_qkv).T,
        "wo0": host(L0_conv_w_out).T,
        "bo0": np.stack([host(L0_conv_b_out)] * 2),
        "pos": host(L0_conv_pos_embedding)[:, ::-1],
        "mask": mask.reshape(128, 2 * WIN),
        "ident": eye,
        "gmat": gmat,
        "sel": sel.reshape(128, E * 128),
        "iota": iota,
        "w1": np.concatenate([twice(w1[:, :C]), twice(w1[:, C:2 * C]), padded(w1[:, 2 * C:].T).T], axis=1),
        "bq1": twice(bq[0:C]).reshape(2, C).T,
        "bk1": twice(bq[C:2 * C]).reshape(2, C).T,
        "bv1": padded(bq[2 * C:]).reshape(2, 128).T,
        "wo1": padded(host(L1_attn_w_out)),
        "bo1": np.stack([host(L1_attn_b_out)] * 2),
        "rw": host(L1_ffn_router_w).T,
        "rb": np.stack([host(L1_ffn_router_b)] * 2),
        "f1": host(L1_ffn_fc1_w).reshape(2 * NFC * 128, C).T,
        "f1b": host(L1_ffn_fc1_b).reshape(2 * NFC, 128).T,
        "f2": host(L1_ffn_fc2_w).reshape(E, C, 2, 128).transpose(3, 0, 2, 1).reshape(128, NFC * C),
        "f2b": host(L1_ffn_fc2_b),
    }
    arrays = {n + "_dram": np.ascontiguousarray(a) for n, a in arrays.items()}

    nc = bacc.Bacc("TRN2", target_bir_lowering=False, num_devices=1)
    args = [nc.dram_tensor(n, a.shape, mybir.dt.from_np(a.dtype), kind="ExternalInput").ap()
            for n, a in arrays.items()]
    out = nc.dram_tensor("out_dram", (NTOK, C), mybir.dt.float32, kind="ExternalOutput").ap()
    hybrid_kernel(nc, *args, out)
    y = run_bass_kernel_spmd(nc, [arrays], core_ids=[0]).results[0]["out_dram"]
    y = y.reshape(B, 2, 2, 8, 8, C).transpose(0, 1, 3, 2, 4, 5).reshape(B, 16, 16, C)
    return np.roll(y, (4, 4), axis=(1, 2))
```
